# Optimizing a Trainium2 kernel written in Bass

```python
import numpy as np
import jax
import jax.numpy as jnp

def _softmax(x, axis=-1):
    return jax.nn.softmax(x, axis=axis)

def _gelu(x):
    return jax.nn.gelu(x, approximate=True)

def _silu(x):
    return jax.nn.silu(x)

def _sigmoid(x):
    return jax.nn.sigmoid(x)

def _layernorm(x, axis=-1, eps=1e-05):
    m = jnp.mean(x, axis=axis, keepdims=True)
    v = jnp.var(x, axis=axis, keepdims=True)
    return (x - m) / jnp.sqrt(v + eps)

def _scatter_add(tgt, idx, src, axis=0):
    return tgt.at[idx].add(src)

def _segment_sum(src, seg, n):
    return jax.ops.segment_sum(src, seg, n)
kernel_name = 'mk_gnn_ffn_d1_gnn_r8_1b92e5'

def setup_inputs(seed: int=0):
    np.random.seed(seed)
    _w = jnp.asarray

    def _rec_inputs():
        import jax
        import jax.numpy as jnp
        _gk = jax.random.key(seed)
        x = -8.776e-05 + 1 * jax.random.normal(jax.random.fold_in(_gk, 1), (6250, 256), jnp.float32)
        src = jax.random.randint(jax.random.fold_in(_gk, 2), (100000,), 0, 6250, jnp.int32)
        dst = jax.random.randint(jax.random.fold_in(_gk, 3), (100000,), 0, 6250, jnp.int32)
        _o = jnp.argsort(dst, stable=True)
        src = src[_o]
        dst = dst[_o]
        edge_attr_64 = 1.36993e-05 + 0.999972 * jax.random.normal(jax.random.fold_in(_gk, 11), (100000, 64), jnp.float32)
        edge_weight = jax.random.uniform(jax.random.fold_in(_gk, 13), (100000,), jnp.float32, 0.0, 0.999998)
        return (x, src, dst, edge_attr_64, edge_weight)
    x, src, dst, edge_attr_64, edge_weight = _rec_inputs()

    def _L0_gnn_setup():
        import jax, jax.numpy as jnp
        import numpy as np
        N = 2500
        E = 40000
        D = 256
        H = 8
        DH = D // H
        ED = 64
        FF = 4 * D
        EPS = 1e-05

        def _layernorm(x, g, b):
            m = jnp.mean(x, axis=-1, keepdims=True)
            v = jnp.var(x, axis=-1, keepdims=True)
            return (x - m) * jax.lax.rsqrt(v + EPS) * g + b

        def _edge_attention(xn, edge_index, ef, ew, Wq, bq, Wk, bk, Wv, bv, We, be, Wo, bo):
            n = xn.shape[0]
            scale = DH ** (-0.5)
            q = (xn @ Wq + bq).reshape(n, H, DH)
            k = (xn @ Wk + bk).reshape(n, H, DH)
            v = (xn @ Wv + bv).reshape(n, H, DH)
            src, dst = (edge_index[0], edge_index[1])
            ep = ef @ We + be
            scores = jnp.einsum('ehd,ehd->eh', q[dst], k[src] + ep[:, None, :]) * scale
            scores = scores * ew[:, None]
            m = jax.ops.segment_max(scores, dst, num_segments=n)
            m = jnp.where(jnp.isfinite(m), m, 0.0)
            ex = jnp.exp(scores - m[dst])
            s = jax.ops.segment_sum(ex, dst, num_segments=n)
            attn = ex / s[dst]
            out = jax.ops.segment_sum(attn[:, :, None] * v[src], dst, num_segments=n)
            out = out.reshape(n, D) @ Wo + bo
            return out
        key = jax.random.key(seed)
        ks = jax.random.split(key, 32)

        def lin_w(k, i, o):
            return (jax.random.normal(k, (i, o), jnp.float32) / np.sqrt(i)).astype(jnp.float32)
        return {'x': jax.random.normal(ks[0], (N, D), jnp.float32), 'edge_features': jax.random.normal(ks[1], (E, ED), jnp.float32), 'edge_weights': jax.random.uniform(ks[2], (E,), jnp.float32), 'edge_index': jax.random.randint(ks[3], (2, E), 0, N, dtype=jnp.int32), 'Wq': lin_w(ks[4], D, D), 'bq': jnp.zeros((D,), jnp.float32), 'Wk': lin_w(ks[5], D, D), 'bk': jnp.zeros((D,), jnp.float32), 'Wv': lin_w(ks[6], D, D), 'bv': jnp.zeros((D,), jnp.float32), 'We': lin_w(ks[7], ED, DH), 'be': jnp.zeros((DH,), jnp.float32), 'Wo': lin_w(ks[8], D, D), 'bo': jnp.zeros((D,), jnp.float32), 'ln1_g': jnp.ones((D,), jnp.float32), 'ln1_b': jnp.zeros((D,), jnp.float32), 'ln2_g': jnp.ones((D,), jnp.float32), 'ln2_b': jnp.zeros((D,), jnp.float32), 'W1': lin_w(ks[9], D, FF), 'b1': jnp.zeros((FF,), jnp.float32), 'W2': lin_w(ks[10], FF, D), 'b2': jnp.zeros((D,), jnp.float32), 'alpha': jnp.ones((1,), jnp.float32), 'beta': jnp.ones((1,), jnp.float32)}
    _L0_gnn_all = _L0_gnn_setup()
    _L0_gnn_in = {k: v for k, v in _L0_gnn_all.items() if k in ('Wq', 'bq', 'Wk', 'bk', 'Wv', 'bv', 'We', 'be', 'Wo', 'bo', 'ln1_g', 'ln1_b', 'ln2_g', 'ln2_b', 'W1', 'b1', 'W2', 'b2', 'alpha', 'beta')}
    del _L0_gnn_all

    def _L0_ffn_setup():
        import jax, jax.numpy as jnp
        import numpy as np
        E = 8
        K = 2
        D = 256
        H = 512
        DOUT = 256
        EPS = 1e-05
        key = jax.random.key(seed)
        ks = jax.random.split(key, 9)
        s = 0.02
        return {'x': jax.random.normal(ks[0], (4, 1024, D), jnp.float32), 'gamma': 1.0 + 0.05 * jax.random.normal(ks[1], (D,), jnp.float32), 'beta': 0.05 * jax.random.normal(ks[2], (D,), jnp.float32), 'Wr': 0.01 * jax.random.normal(ks[3], (D, E), jnp.float32), 'br': jnp.zeros((E,), jnp.float32), 'W1': s * jax.random.normal(ks[4], (E, D, H), jnp.float32), 'b1': s * jax.random.normal(ks[5], (E, H), jnp.float32), 'W2': s * jax.random.normal(ks[6], (E, H, DOUT), jnp.float32), 'b2': s * jax.random.normal(ks[7], (E, DOUT), jnp.float32)}
    _L0_ffn_all = _L0_ffn_setup()
    _L0_ffn_in = {k: v for k, v in _L0_ffn_all.items() if k in ('gamma', 'beta', 'Wr', 'br', 'W1', 'b1', 'W2', 'b2')}
    del _L0_ffn_all
    return {'x': x, 'src': src, 'dst': dst, 'edge_attr_64': edge_attr_64, 'edge_weight': edge_weight, 'L0_gnn_Wq': _L0_gnn_in['Wq'], 'L0_gnn_bq': _L0_gnn_in['bq'], 'L0_gnn_Wk': _L0_gnn_in['Wk'], 'L0_gnn_bk': _L0_gnn_in['bk'], 'L0_gnn_Wv': _L0_gnn_in['Wv'], 'L0_gnn_bv': _L0_gnn_in['bv'], 'L0_gnn_We': _L0_gnn_in['We'], 'L0_gnn_be': _L0_gnn_in['be'], 'L0_gnn_Wo': _L0_gnn_in['Wo'], 'L0_gnn_bo': _L0_gnn_in['bo'], 'L0_gnn_ln1_g': _L0_gnn_in['ln1_g'], 'L0_gnn_ln1_b': _L0_gnn_in['ln1_b'], 'L0_gnn_ln2_g': _L0_gnn_in['ln2_g'], 'L0_gnn_ln2_b': _L0_gnn_in['ln2_b'], 'L0_gnn_W1': _L0_gnn_in['W1'], 'L0_gnn_b1': _L0_gnn_in['b1'], 'L0_gnn_W2': _L0_gnn_in['W2'], 'L0_gnn_b2': _L0_gnn_in['b2'], 'L0_gnn_alpha': _L0_gnn_in['alpha'], 'L0_gnn_beta': _L0_gnn_in['beta'], 'L0_ffn_gamma': _L0_ffn_in['gamma'], 'L0_ffn_beta': _L0_ffn_in['beta'], 'L0_ffn_Wr': _L0_ffn_in['Wr'], 'L0_ffn_br': _L0_ffn_in['br'], 'L0_ffn_W1': _L0_ffn_in['W1'], 'L0_ffn_b1': _L0_ffn_in['b1'], 'L0_ffn_W2': _L0_ffn_in['W2'], 'L0_ffn_b2': _L0_ffn_in['b2']}

def reference(x, src, dst, edge_attr_64, edge_weight, L0_gnn_Wq, L0_gnn_bq, L0_gnn_Wk, L0_gnn_bk, L0_gnn_Wv, L0_gnn_bv, L0_gnn_We, L0_gnn_be, L0_gnn_Wo, L0_gnn_bo, L0_gnn_ln1_g, L0_gnn_ln1_b, L0_gnn_ln2_g, L0_gnn_ln2_b, L0_gnn_W1, L0_gnn_b1, L0_gnn_W2, L0_gnn_b2, L0_gnn_alpha, L0_gnn_beta, L0_ffn_gamma, L0_ffn_beta, L0_ffn_Wr, L0_ffn_br, L0_ffn_W1, L0_ffn_b1, L0_ffn_W2, L0_ffn_b2):
    import jax
    import jax.numpy as jnp

    def _L0_gnn_ref(x, edge_features, edge_weights, edge_index, Wq, bq, Wk, bk, Wv, bv, We, be, Wo, bo, ln1_g, ln1_b, ln2_g, ln2_b, W1, b1, W2, b2, alpha, beta):
        import jax, jax.numpy as jnp
        import numpy as np
        N = 2500
        E = 40000
        D = 256
        H = 8
        DH = D // H
        ED = 64
        FF = 4 * D
        EPS = 1e-05

        def _layernorm(x, g, b):
            m = jnp.mean(x, axis=-1, keepdims=True)
            v = jnp.var(x, axis=-1, keepdims=True)
            return (x - m) * jax.lax.rsqrt(v + EPS) * g + b

        def _edge_attention(xn, edge_index, ef, ew, Wq, bq, Wk, bk, Wv, bv, We, be, Wo, bo):
            n = xn.shape[0]
            scale = DH ** (-0.5)
            q = (xn @ Wq + bq).reshape(n, H, DH)
            k = (xn @ Wk + bk).reshape(n, H, DH)
            v = (xn @ Wv + bv).reshape(n, H, DH)
            src, dst = (edge_index[0], edge_index[1])
            ep = ef @ We + be
            scores = jnp.einsum('ehd,ehd->eh', q[dst], k[src] + ep[:, None, :]) * scale
            scores = scores * ew[:, None]
            m = jax.ops.segment_max(scores, dst, num_segments=n)
            m = jnp.where(jnp.isfinite(m), m, 0.0)
            ex = jnp.exp(scores - m[dst])
            s = jax.ops.segment_sum(ex, dst, num_segments=n)
            attn = ex / s[dst]
            out = jax.ops.segment_sum(attn[:, :, None] * v[src], dst, num_segments=n)
            out = out.reshape(n, D) @ Wo + bo
            return out
        xn = _layernorm(x, ln1_g, ln1_b)
        attn_out = _edge_attention(xn, edge_index, edge_features, edge_weights, Wq, bq, Wk, bk, Wv, bv, We, be, Wo, bo)
        x = x + alpha * attn_out
        xn = _layernorm(x, ln2_g, ln2_b)
        ff = jax.nn.gelu(xn @ W1 + b1, approximate=False) @ W2 + b2
        x = x + beta * ff
        return x

    def _L0_ffn_ref(x, gamma, beta, Wr, br, W1, b1, W2, b2):
        import jax, jax.numpy as jnp
        import numpy as np
        E = 8
        K = 2
        D = 256
        H = 512
        DOUT = 256
        EPS = 1e-05
        mu = jnp.mean(x, axis=-1, keepdims=True)
        var = jnp.mean(jnp.square(x - mu), axis=-1, keepdims=True)
        xn = (x - mu) * jax.lax.rsqrt(var + EPS) * gamma + beta
        logits = jnp.einsum('bsd,de->bse', xn, Wr) + br
        top_vals, top_idx = jax.lax.top_k(logits, K)
        w = jax.nn.softmax(top_vals, axis=-1)
        w_full = jnp.einsum('bsk,bske->bse', w, jax.nn.one_hot(top_idx, E, dtype=w.dtype))
        y = jnp.zeros(x.shape[:-1] + (DOUT,), x.dtype)
        for e in range(E):
            h = jax.nn.gelu(jnp.einsum('bsd,dh->bsh', xn, W1[e]) + b1[e], approximate=False)
            y_e = jnp.einsum('bsh,hd->bsd', h, W2[e]) + b2[e]
            y = y + y_e * w_full[..., e, None]
        return y
    edge_index = jnp.stack([src, dst])
    x = x + _L0_gnn_ref(_layernorm(x, axis=-1), edge_attr_64, edge_weight, edge_index, L0_gnn_Wq, L0_gnn_bq, L0_gnn_Wk, L0_gnn_bk, L0_gnn_Wv, L0_gnn_bv, L0_gnn_We, L0_gnn_be, L0_gnn_Wo, L0_gnn_bo, L0_gnn_ln1_g, L0_gnn_ln1_b, L0_gnn_ln2_g, L0_gnn_ln2_b, L0_gnn_W1, L0_gnn_b1, L0_gnn_W2, L0_gnn_b2, L0_gnn_alpha, L0_gnn_beta)
    x = x + _L0_ffn_ref(_layernorm(x, axis=-1)[None], L0_ffn_gamma, L0_ffn_beta, L0_ffn_Wr, L0_ffn_br, L0_ffn_W1, L0_ffn_b1, L0_ffn_W2, L0_ffn_b2)[0]
    return x

_drawn_inputs = setup_inputs


def setup_inputs(seed=0):
    import zlib

    import numpy as np

    out = dict(_drawn_inputs(seed))
    spreads = {'L0_gnn_bq': (0.0, 0.472),
     'L0_gnn_bk': (0.0, 0.8),
     'L0_gnn_bv': (0.0, 0.1),
     'L0_gnn_be': (0.0, 0.8),
     'L0_gnn_bo': (0.0, 0.1),
     'L0_gnn_ln1_g': (1.0, 0.2),
     'L0_gnn_ln1_b': (0.0, 0.1),
     'L0_gnn_ln2_g': (1.0, 0.2),
     'L0_gnn_ln2_b': (0.0, 0.1),
     'L0_gnn_b1': (0.0, 0.1),
     'L0_gnn_b2': (0.0, 0.1),
     'L0_ffn_br': (0.0, 0.302)}
    factors = {'L0_ffn_gamma': 8.0,
     'L0_ffn_beta': 8.0,
     'L0_ffn_Wr': 3.229,
     'L0_ffn_b1': 22.38,
     'L0_ffn_b2': 8.0}
    for name, (base, spread) in spreads.items():
        noise = np.random.default_rng([zlib.crc32(name.encode()), seed]).standard_normal(out[name].shape)
        drawn = base * np.exp(spread * noise) if base else spread * noise
        out[name] = jnp.asarray(drawn.astype(out[name].dtype))
    for name, factor in factors.items():
        out[name] = (out[name] * factor).astype(out[name].dtype)
    return out
```

```python
import concourse.bass as bass
from concourse import mybir
from contextlib import ExitStack

P = 128
N, D, H, ED, FF = 6250, 256, 8, 64, 1024
DH = D // H
E = 100000
NE, EH = 8, 512
EPS = 1e-5
TILES = -(-N // P)
LAST = N - (TILES - 1) * P
ROWS = TILES * P
RUN = 784
CH = 8
CHUNKS = RUN // CH
TAIL = E - (P - 1) * RUN
ACC = D + H
BIG = 1e38
PADNODE = 8191
GT = 4
GROUPS = TILES // GT
GC = FF // P
HC = EH // P
A_SPLIT = 112


class Chain:

    def __init__(self, engine, sem):
        self.engine, self.sem, self.base, self.n = engine, sem, 0, 0

    def step(self, instruction):
        instruction.then_inc(self.sem, 1)
        self.n += 1

    def wait(self, hold=False):
        self.engine.wait_ge(self.sem, self.base + self.n)
        if hold:
            self.engine.nop(nofuse=True)

    def link(self, instruction):
        self.step(instruction)
        self.wait()

    def enter(self, i, per_turn):
        self.start = self.base + self.n
        self.base, self.n, self.per = self.start + i * per_turn, 0, per_turn

    def leave(self, turns):
        assert self.n == self.per, (self.n, self.per)
        self.base, self.n = self.start + turns * self.per, 0


def gnn_moe_program(nc, x, src, dst, ef, ew, Wq, bq, Wk, bk, Wv, bv, We, be, Wo, bo, g1, b1n, g2, b2n,
                    W1, b1, W2, b2, alpha, beta, gm, bm, Wr, br, M1, mb1, M2, mb2, out):
    f32, i32, bf16 = mybir.dt.float32, mybir.dt.int32, mybir.dt.bfloat16
    ALU, ACT, AX = mybir.AluOpType, mybir.ActivationFunctionType, mybir.AxisListType
    TURNS1 = GROUPS - 1

    q_rows = nc.dram_tensor("q_rows", [ROWS, D], f32)
    k_rows = nc.dram_tensor("k_rows", [ROWS, D], f32)
    v_rows = nc.dram_tensor("v_rows", [ROWS, D], f32)
    h0_rows = nc.dram_tensor("h0_rows", [ROWS, D], f32)
    sum_rows = nc.dram_tensor("sum_rows", [P * RUN, ACC], f32)

    with ExitStack() as ctx:
        def sb(name, shape, dt=f32):
            return ctx.enter_context(nc.sbuf_tensor(name, shape, dt))

        def sem(name):
            return ctx.enter_context(nc.semaphore(name))

        ident = sb("ident", [P, P])
        ones = sb("ones", [P, P])
        iota = sb("iota", [P, P])
        tri = sb("tri", [P, P])
        early = sb("early", [P, 5 * 3 * D])
        wqkv = early[:, 0:6 * D].rearrange("p (k n) -> p k n", k=2)
        qkv = early[:, 6 * D:12 * D].rearrange("p (r n) -> p r n", r=2)
        bqkv = early[:, 12 * D:15 * D]
        x2, y, yo = (early[:, j * GT * D:(j + 1) * GT * D].rearrange("p (t d) -> p t d", t=GT) for j in range(3))
        corr = early[:, 12 * D:12 * D + GT * P].rearrange("p (t n) -> p t n", t=GT)
        beb = sb("beb", [P, DH])
        ln1 = sb("ln1", [P, 2, D])
        ln2 = sb("ln2", [P, 2, D])
        lnm = sb("lnm", [P, 2, D])
        weblk = sb("weblk", [P, 2 * DH])
        wo = sb("wo", [P, 2, D])
        bo_b = sb("bo_b", [P, D])
        b2_b = sb("b2_b", [P, D])
        ab = sb("ab", [P, 2])
        w1 = sb("w1", [P, 2, FF])
        w2 = sb("w2", [P, GC, D])
        wr = sb("wr", [P, 2, NE])
        br_b = sb("br_b", [P, NE])
        mb2_sb = sb("mb2_sb", [NE, D])
        bias_raw = sb("bias_raw", [GC + NE * HC, P])
        bias_T = sb("bias_T", [P, GC + NE * HC])
        half = sb("half", [P, GT])
        ebase = sb("ebase", [P, GT])
        i8 = sb("i8", [P, NE])

        st = sb("st", [P, GT, 6])
        mv = sb("mv", [P, GT, 2])
        ve = sb("ve", [P, GT])
        rs = sb("rs", [P, GT])

        src_i = sb("src_i", [P, RUN], i32)
        gat_i = sb("gat_i", [P, 2, 2 * CH], i32)
        edges = sb("edges", [P, 4 * RUN + 1])
        dst_i = edges[:, 0:RUN].bitcast(i32)
        dstf = edges[:, RUN:2 * RUN]
        ews = edges[:, 2 * RUN:3 * RUN]
        cut = edges[:, 3 * RUN:4 * RUN + 1]
        attn = edges[:, 0:GT * D].rearrange("p (t d) -> p t d", t=GT)
        wT = edges[0:NE, GT * D:GT * D + GT * P]
        keep = sb("keep", [P, RUN])
        keep_c = sb("keep_c", [P, CH])
        next_i = sb("next_i", [P, 1], i32)
        nextf = sb("nextf", [P, 1])
        cont = sb("cont", [P, 1])
        last_rel = sb("last_rel", [P, TILES])
        last_c = sb("last_c", [P, GT])
        hist = sb("hist", [TILES, P])
        tots = sb("tots", [TILES, P])
        end_i = sb("end_i", [P, TILES + GT], i32)
        end_c = sb("end_c", [P, GT], i32)
        has = sb("has", [P, TILES + GT])
        has_c = sb("has_c", [P, GT])
        small = sb("small", [P, 2 + 2 * H])
        gmax = sb("gmax", [P, 2, H])
        sums = sb("sums", [P, 2, CH, ACC])

        SC = RUN * H
        arena = sb("arena", [P, 3 * SC + 4 * CH * D])
        S = arena[:, 0:SC]
        Fm = arena[:, SC:2 * SC]
        Mm = arena[:, 2 * SC:3 * SC]
        o = 3 * SC
        q_ring = [arena[:, o + r * CH * D:o + (r + 1) * CH * D] for r in range(2)]
        k_ring = [arena[:, o + (2 + r) * CH * D:o + (3 + r) * CH * D] for r in range(2)]
        v_ring = k_ring
        m1_sb = arena[:, SC:SC + NE * 2 * EH].rearrange("p (e k n) -> p e k n", e=NE, k=2)
        m2_sb = arena[:, SC + NE * 2 * EH:SC + NE * (2 * EH + HC * D)].rearrange("p (e c n) -> p e c n", e=NE, c=HC)
        assert NE * (2 * EH + HC * D) <= 2 * SC + 2 * CH * D
        hid = [arena[:, r * HC * 512:(r + 1) * HC * 512].rearrange("p (c n) -> p c n", c=HC) for r in range(2)]
        x3T = arena[:, 2 * HC * 512:2 * HC * 512 + 2 * GT * P].rearrange("p (k n) -> p k n", k=2)
        got = arena[:, 2 * HC * 512 + 2 * GT * P:2 * HC * 512 + 2 * GT * P + GT * ACC].rearrange("p (t n) -> p t n", t=GT)
        assert 2 * HC * 512 + 2 * GT * P + GT * ACC <= SC
        hidg = arena[:, o + 2 * CH * D:o + 4 * CH * D].rearrange("p (c n) -> p c n", c=GC)

        xb = sb("xb", [P, GT, D])
        h0 = sb("h0", [P, GT, D])
        xn = sb("xn", [P, GT, D])
        xT = sb("xT", [P, 2, GT * P])
        efb = h0[:, :, :].rearrange("p t d -> p (t d)").rearrange("p (r n) -> p r n", r=2)
        efT = xT
        xn16 = xn[:, :, :].rearrange("p t d -> p (t d)").bitcast(bf16)
        hits_hi = xn16[:, 0:CH * TILES].rearrange("p (t n) -> p t n", t=CH)
        hits_lo = xn16[:, CH * TILES:CH * (TILES + P)].rearrange("p (t n) -> p t n", t=CH)
        xb16 = xb[:, :, :].rearrange("p t d -> p (t d)").bitcast(bf16)
        dhi = xb16[:, 0:RUN]
        dlo = xb16[:, RUN:2 * RUN]
        rec = sb("rec", [P, GT, H])
        lg = sb("lg", [P, 6, GT, NE])
        tv = sb("tv", [P, 6, GT])
        wmix = sb("wmix", [P, GT, NE])
        iota49 = iota[:, 0:TILES]

        ps = ctx.enter_context(nc.psum_tensor("ps", [P, 8 * 512], f32))

        def bank(b, n=1):
            return ps[:, b * 512:(b + n) * 512]

        const_ld = sem("const_ld")
        edge_ld = sem("edge_ld")
        pool_const = sem("pool_const")
        dve_steps = sem("dve_steps")
        pool_steps = sem("pool_steps")
        bias_ps = sem("bias_ps")
        bias_done = sem("bias_done")
        x_ld = sem("x_ld")
        h0_ready = sem("h0_ready")
        h0_stored = sem("h0_stored")
        var_ready = sem("var_ready")
        rstd_ready = sem("rstd_ready")
        xn_ready = sem("xn_ready")
        xT_ps = sem("xT_ps")
        xT_ready = sem("xT_ready")
        qkv_ps = sem("qkv_ps")
        qkv_ready = sem("qkv_ready")
        qkv_stored = [sem("qkv_stored0"), sem("qkv_stored1")]
        edges_ready = sem("edges_ready")
        idx_ready = sem("idx_ready")
        rows_in = [sem("rows_in0"), sem("rows_in1")]
        scores_done = sem("scores_done")
        ef_ld = [sem("ef_ld0"), sem("ef_ld1")]
        efT_ps = sem("efT_ps")
        efT_ready = sem("efT_ready")
        ep_ready = sem("ep_ready")
        hits_ready = sem("hits_ready")
        hits_used = sem("hits_used")
        diag_ready = sem("diag_ready")
        small_ps = sem("small_ps")
        end_ready = sem("end_ready")
        exp_in = sem("exp_in")
        exp_done = sem("exp_done")
        v_in = [sem("v_in0"), sem("v_in1")]
        v_used = sem("v_used")
        run_ready = sem("run_ready")
        run_stored = [sem("run_stored0"), sem("run_stored1")]
        w_ld = sem("w_ld")
        got_in = sem("got_in")
        h0_ld = sem("h0_ld")
        xr_ld = sem("xr_ld")
        corr_ready = sem("corr_ready")
        corr_ps = sem("corr_ps")
        corr_used = sem("corr_used")
        attn_ready = sem("attn_ready")
        t_ps = sem("t_ps")
        t_ready = sem("t_ready")
        o_ps = sem("o_ps")
        x1_ready = sem("x1_ready")
        h_ps = sem("h_ps")
        h_ready = sem("h_ready")
        f_ps = sem("f_ps")
        x3_ready = sem("x3_ready")
        r_ps = sem("r_ps")
        w_ready = sem("w_ready")
        wT_ps = sem("wT_ps")
        wT_ready = sem("wT_ready")
        b_ps = sem("b_ps")
        b_used = sem("b_used")
        y_ps = sem("y_ps")
        y_done = sem("y_done")
        out_stored = sem("out_stored")

        block = ctx.enter_context(nc.Block())

        def flat(v, p):
            return v.rearrange("(p n) -> p n", p=p)

        N_CONST = 25
        N_EDGE = 12

        @block.sync
        def _(sp):
            def x_tiles(dst_t, g, nt, s):
                if nt == GT:
                    sp.dma_start(dst_t[:, :, :], x[bass.ds(g * (GT * P), GT * P), :].rearrange("(t p) d -> p t d", p=P)).then_inc(s, 16)
                else:
                    sp.dma_start(dst_t[0:LAST, 0, :], x[(TILES - 1) * P:N, :]).then_inc(s, 16)

            x_tiles(xb, 0, GT, x_ld)
            sp.sem_inc(out_stored, 16)
            for j, w in enumerate((Wq, Wk, Wv)):
                sp.dma_start(wqkv[:, :, j * D:(j + 1) * D], w.rearrange("(c p) n -> p c n", p=P)).then_inc(const_ld, 16)
            for j, b in enumerate((bq, bk, bv)):
                sp.dma_start(bqkv[:, j * D:(j + 1) * D], b.partition_broadcast(P)).then_inc(const_ld, 16)
            sp.dma_start(beb[:, :], be.partition_broadcast(P)).then_inc(const_ld, 16)
            for t, (g, b) in ((ln1, (g1, b1n)), (ln2, (g2, b2n)), (lnm, (gm, bm))):
                sp.dma_start(t[:, 0, :], g.partition_broadcast(P)).then_inc(const_ld, 16)
                sp.dma_start(t[:, 1, :], b.partition_broadcast(P)).then_inc(const_ld, 16)
            sp.dma_start(wo[:, :, :], Wo.rearrange("(c p) n -> p c n", p=P)).then_inc(const_ld, 16)
            sp.dma_start(bo_b[:, :], bo.partition_broadcast(P)).then_inc(const_ld, 16)
            sp.dma_start(b2_b[:, :], b2.partition_broadcast(P)).then_inc(const_ld, 16)
            sp.dma_start(ab[:, 0:1], alpha.partition_broadcast(P)).then_inc(const_ld, 16)
            sp.dma_start(ab[:, 1:2], beta.partition_broadcast(P)).then_inc(const_ld, 16)
            sp.dma_start(wr[:, :, :], Wr.rearrange("(c p) n -> p c n", p=P)).then_inc(const_ld, 16)
            sp.dma_start(br_b[:, :], br.partition_broadcast(P)).then_inc(const_ld, 16)
            sp.dma_start(mb2_sb[:, :], mb2).then_inc(const_ld, 16)
            sp.dma_start(w1[:, :, :], W1.rearrange("(c p) n -> p c n", p=P)).then_inc(const_ld, 16)
            sp.dma_start(w2[:, :, :], W2.rearrange("(c p) n -> p c n", p=P)).then_inc(const_ld, 16)
            sp.dma_start(bias_raw[0:GC, :], b1.rearrange("(c p) -> c p", p=P)).then_inc(const_ld, 16)
            sp.dma_start(bias_raw[GC:GC + NE * HC, :], mb1.rearrange("e (c p) -> (e c) p", p=P)).then_inc(const_ld, 16)

            def h0_out(g, nt):
                sp.wait_ge(h0_ready, g + 1)
                sp.dma_start(h0_rows[bass.ds(g * (GT * P), nt * P), :].rearrange("(t p) d -> p t d", p=P), h0[:, 0:nt, :]).then_inc(h0_stored, 16)

            with sp.Fori(0, TURNS1) as g:
                h0_out(g, GT)
                x_tiles(xb, g + 1, GT, x_ld)
            h0_out(TURNS1, GT)
            x_tiles(xb, GROUPS, 1, x_ld)
            h0_out(GROUPS, 1)

            def ef_in(c, par):
                v = ef[0:(P - 1) * RUN, :].rearrange("(p r) d -> p (r d)", p=P - 1)
                w = CH * ED
                sp.dma_start(efb[0:A_SPLIT, par, :], v[0:A_SPLIT, bass.ds(c * w, w)]).then_inc(ef_ld[par], 16)
                sp.dma_start(efb[A_SPLIT:P - 1, par, :], v[A_SPLIT:P - 1, bass.ds(c * w, w)]).then_inc(ef_ld[par], 16)

            def ef_tail(c, par):
                w = CH * ED
                t = ef[(P - 1) * RUN:E, :].rearrange("(p r) d -> p (r d)", p=1)
                sp.dma_start(efb[P - 1:P, par, :], t[:, bass.ds(c * w, w)]).then_inc(ef_ld[par], 16)

            def ef_tail_again(par):
                w = CH * ED
                t = ef[(P - 1) * RUN:E, :].rearrange("(p r) d -> p (r d)", p=1)
                sp.dma_start(efb[P - 1:P, par, :], t[:, TAIL // CH * w - w:TAIL // CH * w]).then_inc(ef_ld[par], 16)

            sp.wait_ge(h0_stored, 16 * (GROUPS + 1))
            sp.wait_ge(xn_ready, GROUPS + 1)
            for par in range(2):
                ef_in(par, par)
                ef_tail(par, par)
            half_tail = TAIL // CH // 2
            with sp.Fori(0, half_tail - 1) as i:
                for par in range(2):
                    sp.wait_ge(efT_ps, 2 * i + par + 1)
                    ef_in(2 * i + par + 2, par)
                    ef_tail(2 * i + par + 2, par)
            with sp.Fori(half_tail - 1, CHUNKS // 2 - 1) as i:
                for par in range(2):
                    sp.wait_ge(efT_ps, 2 * i + par + 1)
                    ef_in(2 * i + par + 2, par)
                    ef_tail_again(par)

            sp.wait_ge(exp_in, 1)
            for e in range(NE):
                sp.dma_start(m1_sb[:, e, :, :], M1[e, :, :].rearrange("(k p) n -> p k n", p=P)).then_inc(w_ld, 16)
                sp.dma_start(m2_sb[:, e, :, :], M2[e, :, :].rearrange("(c p) n -> p c n", p=P)).then_inc(w_ld, 16)

            rows = sum_rows[:, :].rearrange("(p r) a -> p (r a)", p=P)
            with sp.Fori(0, CHUNKS // 2) as i:
                for par in range(2):
                    sp.wait_ge(run_ready, 2 * i + par + 1)
                    sp.dma_start(rows[:, bass.ds((2 * i + par) * (CH * ACC), CH * ACC)],
                                 sums[:, par, :, :].rearrange("p t a -> p (t a)")).then_inc(run_stored[par], 16)

            def node_in(g, nt):
                sp.dma_start(h0[:, 0:nt, :], h0_rows[bass.ds(g * (GT * P), nt * P), :].rearrange("(t p) d -> p t d", p=P)).then_inc(h0_ld, 16)
                x_tiles(xb, g, nt, xr_ld)

            def rows_out(g, nt):
                sp.wait_ge(y_done, (g + 1) * NE + 1)
                if nt == GT:
                    sp.dma_start(out[bass.ds(g * (GT * P), GT * P), :].rearrange("(t p) d -> p t d", p=P), yo[:, :, :]).then_inc(out_stored, 16)
                else:
                    sp.dma_start(out[(TILES - 1) * P:N, :], yo[0:LAST, 0, :]).then_inc(out_stored, 16)

            sp.wait_ge(hits_used, CHUNKS + 1)
            node_in(0, GT)
            sp.wait_ge(x1_ready, 1)
            node_in(1, GT)
            with sp.Fori(0, TURNS1 - 1) as g:
                sp.wait_ge(x1_ready, g + 2)
                node_in(g + 2, GT)
                rows_out(g, GT)
            sp.wait_ge(x1_ready, GROUPS)
            node_in(GROUPS, 1)
            rows_out(TURNS1 - 1, GT)
            rows_out(TURNS1, GT)
            rows_out(GROUPS, 1)
            sp.wait_ge(out_stored, 16 * (GROUPS + 2))

        @block.gpsimd
        def _(pool):
            pool.memset(ident[:, :], 0.0).then_inc(pool_steps, 1)
            pool.memset(ones[:, :], 1.0).then_inc(pool_steps, 1)
            pool.memset(half[:, :], -0.5).then_inc(pool_steps, 1)
            pool.memset(ebase[:, :], 2.718281828459045).then_inc(pool_steps, 1)
            pool.memset(src_i[:, :], 0).then_inc(pool_const, 1)
            pool.memset(dst_i[:, :], PADNODE).then_inc(pool_const, 1)
            pool.memset(ews[:, :], 0.0).then_inc(pool_const, 1)
            pool.memset(weblk[:, :], 0.0).then_inc(pool_const, 1)
            pool.memset(next_i[:, :], -1).then_inc(pool_const, 1)
            pool.iota(iota[:, :], pattern=[[1, P]], base=0, channel_multiplier=0, allow_small_or_imprecise_dtypes=True).then_inc(pool_steps, 1)
            pool.iota(i8[:, :], pattern=[[1, NE]], base=0, channel_multiplier=0, allow_small_or_imprecise_dtypes=True).then_inc(pool_steps, 1)
            pool.wait_ge(pool_steps, 6)
            pool.affine_select(out=ident[:, :], in_=ident[:, :], compare_op=ALU.not_equal, fill=1.0, base=0,
                               pattern=[[-1, P]], channel_multiplier=1).then_inc(pool_steps, 1)
            pool.affine_select(out=tri[:, :], in_=ones[:, :], compare_op=ALU.is_gt, fill=0.0, base=0,
                               pattern=[[1, P]], channel_multiplier=-1).then_inc(pool_steps, 1)

            def rstd(n, nt):
                pool.wait_ge(var_ready, n + 1)
                nc.gpsimd.tensor_tensor(rs[:, 0:nt], ve[:, 0:nt], half[:, 0:nt], ALU.pow).then_inc(rstd_ready, 1)

            with pool.Fori(0, GROUPS) as g:
                rstd(2 * g, GT)
                rstd(2 * g + 1, GT)
            rstd(2 * GROUPS, 1)
            rstd(2 * GROUPS + 1, 1)

            pool.wait_ge(edges_ready, 1)
            pool.wait_ge(qkv_stored[0], 3 * 16 * (TILES // 2 + 1))
            pool.wait_ge(qkv_stored[1], 3 * 16 * (TILES // 2))

            def gather(dst_t, table, par, j, s):
                pool.indirect_dma_start(dst_t, None, table[:, :], bass.IndirectOffsetOnAxis(ap=gat_i[:, par, j:j + 1], axis=0)).then_inc(s, 16)

            with pool.Fori(0, CHUNKS // 2) as i:
                for par in range(2):
                    c = 2 * i + par
                    pool.wait_ge(scores_done, c + 1)
                    pool.nop(nofuse=True)
                    pool.tensor_copy(gat_i[:, par, 0:CH], src_i[:, bass.ds(c * CH, CH)]).then_inc(idx_ready, 1)
                    pool.tensor_copy(gat_i[:, par, CH:2 * CH], dst_i[:, bass.ds(c * CH, CH)]).then_inc(idx_ready, 1)
                    pool.wait_ge(idx_ready, 2 * c + 2)
                    pool.nop(nofuse=True)
                    for j in range(CH):
                        gather(k_ring[par][:, j * D:(j + 1) * D], k_rows, par, j, rows_in[par])
                        gather(q_ring[par][:, j * D:(j + 1) * D], q_rows, par, CH + j, rows_in[par])

            pool.wait_ge(scores_done, CHUNKS + 2)
            with pool.Fori(0, CHUNKS // 2) as i:
                for par in range(2):
                    c = 2 * i + par
                    pool.wait_ge(v_used, c + 1)
                    pool.nop(nofuse=True)
                    pool.tensor_copy(gat_i[:, par, 0:CH], src_i[:, bass.ds(c * CH, CH)]).then_inc(idx_ready, 1)
                    pool.wait_ge(idx_ready, 2 * CHUNKS + c + 1)
                    pool.nop(nofuse=True)
                    for j in range(CH):
                        gather(v_ring[par][:, j * D:(j + 1) * D], v_rows, par, j, v_in[par])

            pool.wait_ge(run_stored[0], 16 * (CHUNKS // 2))
            pool.wait_ge(run_stored[1], 16 * (CHUNKS // 2))
            pool.wait_ge(end_ready, 1)

            def ends(g, nt):
                pool.tensor_copy(end_c[:, 0:nt], end_i[:, bass.ds(g * GT, nt)]).then_inc(idx_ready, 1)
                pool.wait_ge(idx_ready, 3 * CHUNKS + g + 1)
                pool.nop(nofuse=True)
                for t in range(nt):
                    pool.indirect_dma_start(got[:, t, :], None, sum_rows[:, :],
                                            bass.IndirectOffsetOnAxis(ap=end_c[:, t:t + 1], axis=0)).then_inc(got_in, 16)

            def powers(g, nt):
                n0 = 2 * (GROUPS + 1)
                for j in range(3):
                    rstd(n0 + g * 4 + j, nt)
                pool.wait_ge(var_ready, n0 + g * 4 + 4)
                nc.gpsimd.tensor_tensor(tv[:, 3, 0:nt], ebase[:, 0:nt], tv[:, 2, 0:nt], ALU.pow).then_inc(rstd_ready, 1)

            def sums_used(g):
                pool.wait_ge(attn_ready, g + 1)
                pool.nop(nofuse=True)

            ends(0, GT)
            sums_used(0)
            ends(1, GT)
            powers(0, GT)
            with pool.Fori(0, TURNS1 - 1) as g:
                sums_used(g + 1)
                ends(g + 2, GT)
                powers(g + 1, GT)
            sums_used(TURNS1)
            ends(GROUPS, 1)
            powers(TURNS1, GT)
            powers(GROUPS, 1)

        @block.scalar
        def _(act):
            act.wait_ge(pool_const, 5)
            for d_t, s_t in ((src_i, src), (dst_i, dst), (ews, ew)):
                v = flat(s_t[0:(P - 1) * RUN], P - 1)
                act.dma_start(d_t[0:A_SPLIT, :], v[0:A_SPLIT, :]).then_inc(edge_ld, 16)
                act.dma_start(d_t[A_SPLIT:P - 1, :], v[A_SPLIT:P - 1, :]).then_inc(edge_ld, 16)
                act.dma_start(d_t[P - 1:P, 0:TAIL], flat(s_t[(P - 1) * RUN:E], 1)).then_inc(edge_ld, 16)
            with nc.allow_non_contiguous_dma(reason="127 numbers, once"):
                act.dma_start(next_i[0:P - 1, :], dst[RUN:(P - 1) * RUN + 1:RUN].rearrange("(p o) -> p o", o=1)).then_inc(edge_ld, 16)
            act.dma_start(weblk[0:ED, 0:DH], We).then_inc(edge_ld, 16)
            act.dma_start(weblk[ED:2 * ED, DH:2 * DH], We).then_inc(edge_ld, 16)

            act.wait_ge(bias_ps, 1)
            nc.scalar.copy(bias_T[:, :], bank(7)[:, 0:GC + NE * HC]).then_inc(bias_done, 1)

            def qkv_group(g, nt):
                act.wait_ge(xT_ps, g + 1)
                nc.scalar.copy(xT[:, :, 0:nt * P].rearrange("p k (t n) -> p t k n", n=P),
                               bank(0, 2)[:, 0:nt * 2 * P].rearrange("p (t k n) -> p t k n", k=2, n=P)).then_inc(xT_ready, 1)
                for t in range(nt):
                    n = g * GT + t
                    act.wait_ge(qkv_ready, n + 1)
                    for j, rows_t in enumerate((q_rows, k_rows, v_rows)):
                        act.dma_start(rows_t[bass.ds(n * P, P), :], qkv[:, t % 2, j * D:(j + 1) * D]).then_inc(qkv_stored[t % 2], 16)

            with act.Fori(0, GROUPS) as g:
                qkv_group(g, GT)
            qkv_group(GROUPS, 1)

            with act.Fori(0, CHUNKS // 2) as i:
                for par in range(2):
                    c = 2 * i + par
                    act.wait_ge(efT_ps, c + 1)
                    nc.scalar.copy(efT[:, par, :], bank(par)).then_inc(efT_ready, 1)

            act.wait_ge(exp_in, 1)
            nc.scalar.activation(S, S, ACT.Exp).then_inc(exp_done, 1)

            count = Chain(act, h_ready)

            def gelus(chunks, nt, first_bias, dest):
                for j in range(chunks):
                    act.wait_ge(h_ps, count.base + count.n + 1)
                    b = count.n % 2
                    count.step(nc.scalar.activation(dest[:, j, 0:nt * P], bank(b)[:, 0:nt * P], ACT.Gelu,
                                                    bias=bias_T[:, first_bias + j:first_bias + j + 1]))

            def copy_T(k, g, nt, dest):
                act.wait_ge(t_ps, 3 * g + k + 1)
                nc.scalar.copy(dest[:, :, 0:nt * P].rearrange("p k (t n) -> p t k n", n=P),
                               bank(4, 2)[:, 0:nt * 2 * P].rearrange("p (t k n) -> p t k n", k=2, n=P)).then_inc(t_ready, 1)

            def copy_wT(g, nt):
                act.wait_ge(wT_ps, g + 1)
                nc.scalar.copy(wT[:, 0:nt * P], bank(7)[0:NE, 0:nt * P]).then_inc(wT_ready, 1)

            def prepare(g, nt):
                copy_T(0, g, nt, xT)
                copy_T(1, g, nt, xT)
                gelus(GC, nt, 0, hidg)
                copy_T(2, g, nt, x3T)

            def group(g, nt, ahead):
                def moe(e):
                    gelus(HC, nt, GC + e * HC, hid[e % 2])

                moe(0)
                copy_wT(g, nt)
                moe(1)
                moe(2)
                if ahead:
                    copy_T(0, g + 1, ahead, xT)
                moe(3)
                moe(4)
                if ahead:
                    copy_T(1, g + 1, ahead, xT)
                moe(5)
                if ahead:
                    gelus(GC, ahead, 0, hidg)
                moe(6)
                moe(7)
                if ahead:
                    copy_T(2, g + 1, ahead, x3T)

            prepare(0, GT)
            with act.Fori(0, TURNS1) as g:
                count.enter(g, NE * HC + GC)
                group(g, GT, GT)
            count.leave(TURNS1)
            group(TURNS1, GT, 1)
            group(GROUPS, 1, 0)

        @block.tensor
        def _(pe):
            def transposes(src_t, nt, first_bank):
                for t in range(nt):
                    for k in range(2):
                        last = nc.tensor.transpose(ps[:, first_bank * 512 + (2 * t + k) * P:first_bank * 512 + (2 * t + k + 1) * P],
                                                   src_t[:, t, k * P:(k + 1) * P], ident[:, :])
                return last

            pe.wait_ge(pool_steps, 8)
            pe.wait_ge(const_ld, 16 * N_CONST)
            nb = GC + NE * HC
            nc.tensor.transpose(bank(7)[:, 0:nb], bias_raw[:, :], ident[0:nb, 0:nb]).then_inc(bias_ps, 1)

            def qkv_group(g, nt):
                pe.wait_ge(xn_ready, g + 1)
                transposes(xn, nt, 0).then_inc(xT_ps, 1)
                pe.wait_ge(xT_ready, g + 1)
                for t in range(nt):
                    n = g * GT + t
                    if not (isinstance(g, int) and g == 0 and t < 2):
                        pe.wait_ge(qkv_ready, n - 1)
                    o_ = (2 + 2 * (t % 2)) * 512
                    for c0, c1 in ((0, 512), (512, 3 * D)):
                        for k in range(2):
                            last = nc.tensor.matmul(ps[:, o_ + c0:o_ + c1], xT[:, k, t * P:(t + 1) * P], wqkv[:, k, c0:c1],
                                                    start=k == 0, stop=k == 1)
                    last.then_inc(qkv_ps, 1)

            qkv_group(0, GT)
            with pe.Fori(1, GROUPS) as g:
                qkv_group(g, GT)
            qkv_group(GROUPS, 1)

            pe.wait_ge(edges_ready, 1)
            pe.wait_ge(qkv_ready, TILES)
            nc.tensor.matmul(bank(4)[0:TILES, 0:P], hits_hi[:, 0, :], hits_lo[:, 0, :], start=True, stop=False,
                             skip_group_check=True).then_inc(hits_used, 1)

            def ef_transposes(c, i, par):
                pe.wait_ge(ef_ld[par], 48 * (i + 1))
                for j in range(CH // 2):
                    last = nc.tensor.transpose(bank(par)[:, j * P:(j + 1) * P], efb[:, par, j * P:(j + 1) * P], ident[:, :])
                last.then_inc(efT_ps, 1)

            def chunk(i, par, ahead, first=False):
                c = 2 * i + par
                if ahead:
                    ef_transposes(c + 1, i + par, 1 - par)
                pe.wait_ge(efT_ready, c + 1)
                pe.wait_ge(scores_done, c + 1)
                for j in range(CH // 2):
                    last = nc.tensor.matmul(bank(2 + par)[:, 2 * j * DH:2 * (j + 1) * DH], efT[:, par, j * P:(j + 1) * P], weblk[:, :],
                                            start=True, stop=True)
                last.then_inc(ep_ready, 1)
                pe.wait_ge(hits_ready, c + 1)
                for j in range(CH):
                    last = nc.tensor.matmul(bank(4)[0:TILES, 0:P], hits_hi[:, j, :], hits_lo[:, j, :], start=False,
                                            stop=False, skip_group_check=True)
                last.then_inc(hits_used, 1)

            ef_transposes(0, 0, 0)
            with pe.Fori(0, CHUNKS // 2 - 1) as i:
                chunk(i, 0, True)
                chunk(i, 1, True)
            chunk(CHUNKS // 2 - 1, 0, True)
            chunk(CHUNKS // 2 - 1, 1, False)

            pe.wait_ge(diag_ready, 1)
            for r in range(2 + 2 * H):
                last = nc.tensor.matmul(ps[:, r * P:(r + 1) * P], ones[:, :], arena[:, 3 * SC + r * P:3 * SC + (r + 1) * P],
                                        start=True, stop=True)
            last.then_inc(small_ps, 1)
            nc.tensor.matmul(bank(5)[0:TILES, 0:1], tri[0:TILES, 0:TILES], tots[:, P - 1:P], start=True, stop=True).then_inc(small_ps, 1)
            pe.wait_ge(diag_ready, 2)
            nc.tensor.transpose(bank(6)[:, 0:TILES], tots[:, :], ident[0:TILES, 0:TILES])
            nc.tensor.transpose(bank(6)[:, P:P + TILES], hist[:, :], ident[0:TILES, 0:TILES]).then_inc(small_ps, 1)

            count = Chain(pe, h_ps)

            def hidden(chunks, nt, weights, xt):
                for j in range(chunks):
                    if not (isinstance(count.base, int) and count.base + count.n < 2):
                        pe.wait_ge(h_ready, count.base + count.n - 1)
                    b = count.n % 2
                    for k in range(2):
                        last = nc.tensor.matmul(bank(b)[:, 0:nt * P], weights(k, j), xt[:, k, 0:nt * P], start=k == 0, stop=k == 1)
                    count.step(last)

            def P1(g, nt):
                pe.wait_ge(corr_ready, g + 1)
                for t in range(nt):
                    if t >= 2:
                        pe.wait_ge(corr_used, g * GT + t - 1)
                    nc.tensor.matmul(bank(6 + t % 2)[:, 0:ACC], corr[:, t, :], sums[:, 1, CH - 1, :], start=True, stop=True).then_inc(corr_ps, 1)

            def T(k, g, nt, ready, src_t):
                pe.wait_ge(ready, g + 1)
                transposes(src_t, nt, 4).then_inc(t_ps, 1)

            def project(g, nt):
                pe.wait_ge(t_ready, 3 * g + 1)
                for t in range(nt):
                    for k in range(2):
                        last = nc.tensor.matmul(bank(4, 2)[:, t * D:(t + 1) * D], xT[:, k, t * P:(t + 1) * P], wo[:, k, :],
                                                start=k == 0, stop=k == 1)
                last.then_inc(o_ps, 1)

            def feed(g, nt):
                pe.wait_ge(t_ready, 3 * g + 2)
                hidden(GC, nt, lambda k, j: w1[:, k, j * P:(j + 1) * P], xT)

            def feed2(g, nt):
                pe.wait_ge(h_ready, count.base + feed_end[0])
                for t in range(nt):
                    for j in range(GC):
                        last = nc.tensor.matmul(bank(4, 2)[:, t * D:(t + 1) * D], hidg[:, j, t * P:(t + 1) * P], w2[:, j, :],
                                                start=j == 0, stop=j == GC - 1)
                last.then_inc(f_ps, 1)

            feed_end = [0]

            def route(g, nt):
                T(2, g, nt, x3_ready, xn)
                pe.wait_ge(t_ready, 3 * g + 3)
                for t in range(nt):
                    for k in range(2):
                        last = nc.tensor.matmul(bank(6)[:, t * NE:(t + 1) * NE], x3T[:, k, t * P:(t + 1) * P], wr[:, k, :],
                                                start=k == 0, stop=k == 1)
                last.then_inc(r_ps, 1)

            def group(g, nt, ahead):
                ends_at = {}

                def m1(e):
                    hidden(HC, nt, lambda k, j: m1_sb[:, e, k, j * P:(j + 1) * P], x3T)
                    ends_at[e] = count.n

                def m2(e):
                    pe.wait_ge(h_ready, count.base + ends_at[e])
                    pe.wait_ge(y_done, g * NE + e + 1)
                    for t in range(nt):
                        for j in range(HC):
                            last = nc.tensor.matmul(bank(2, 2)[:, t * D:(t + 1) * D], hid[e % 2][:, j, t * P:(t + 1) * P],
                                                    m2_sb[:, e, j, :], start=j == 0, stop=j == HC - 1)
                    last.then_inc(y_ps, 1)

                m1(0)
                pe.wait_ge(w_ready, g + 1)
                for t in range(nt):
                    last = nc.tensor.transpose(bank(7)[0:NE, t * P:(t + 1) * P], wmix[:, t, :], ident[:, :])
                last.then_inc(wT_ps, 1)
                m1(1)
                pe.wait_ge(wT_ready, g + 1)
                for t in range(nt):
                    last = nc.tensor.matmul(bank(4, 2)[:, t * D:(t + 1) * D], wT[:, t * P:(t + 1) * P], mb2_sb[:, :], start=True, stop=True)
                last.then_inc(b_ps, 1)
                m2(0)
                if ahead:
                    P1(g + 1, ahead)
                m1(2)
                m2(1)
                if ahead:
                    T(0, g + 1, ahead, attn_ready, attn)
                m1(3)
                m2(2)
                if ahead:
                    project(g + 1, ahead)
                m1(4)
                m2(3)
                if ahead:
                    T(1, g + 1, ahead, x1_ready, xn)
                m1(5)
                m2(4)
                if ahead:
                    feed(g + 1, ahead)
                    feed_end[0] = count.n
                m1(6)
                m2(5)
                if ahead:
                    feed2(g + 1, ahead)
                m1(7)
                m2(6)
                m2(7)
                if ahead:
                    route(g + 1, ahead)

            pe.wait_ge(run_ready, CHUNKS)
            P1(0, GT)
            T(0, 0, GT, attn_ready, attn)
            project(0, GT)
            T(1, 0, GT, x1_ready, xn)
            feed(0, GT)
            feed_end[0] = count.n
            feed2(0, GT)
            route(0, GT)
            pe.wait_ge(w_ld, 16 * 2 * NE)
            with pe.Fori(0, TURNS1) as g:
                count.enter(g, NE * HC + GC)
                group(g, GT, GT)
            count.leave(TURNS1)
            group(TURNS1, GT, 1)
            group(GROUPS, 1, 0)

        @block.vector
        def _(dve):
            steps = Chain(dve, dve_steps)
            link, step = steps.link, steps.step
            norms = Chain(dve, var_ready)

            dve.wait_ge(const_ld, 16 * N_CONST)
            dve.wait_ge(pool_steps, 8)
            link(nc.vector.tensor_tensor(bqkv[:, D:2 * D].rearrange("p (h d) -> p h d", h=H), bqkv[:, D:2 * D].rearrange("p (h d) -> p h d", h=H),
                                         beb[:, :].unsqueeze(1).to_broadcast([P, H, DH]), ALU.add))
            dve.sem_inc(scores_done, 2)
            dve.sem_inc(v_used, 2)
            dve.sem_inc(y_done, 1)

            def norm(src_t, nt):
                for t in range(nt):
                    step(nc.vector.bn_stats(st[:, t, :], src_t[:, t, :]))
                steps.wait(hold=True)
                for t in range(nt):
                    step(nc.vector.bn_aggr(mv[:, t, :], st[:, t, :]))
                steps.wait()
                norms.step(nc.vector.tensor_scalar(ve[:, 0:nt], mv[:, 0:nt, 1], EPS, None, ALU.add))
                dve.wait_ge(rstd_ready, norms.base + norms.n)

            def scale_rows(dst_t, src_t, nt, signal=None):
                for t in range(nt):
                    ins = nc.vector.tensor_scalar(dst_t[:, t, :], src_t[:, t, :], mv[:, t, 0:1], rs[:, t:t + 1], ALU.subtract, ALU.mult)
                    if signal and t == nt - 1:
                        ins.then_inc(signal, 1)
                    else:
                        step(ins)
                steps.wait()

            def affine(t_, nt, ln, signal=None):
                link(nc.vector.tensor_tensor(t_[:, 0:nt, :], t_[:, 0:nt, :], ln[:, 0:1, :].to_broadcast([P, nt, D]), ALU.mult))
                ins = nc.vector.tensor_tensor(t_[:, 0:nt, :], t_[:, 0:nt, :], ln[:, 1:2, :].to_broadcast([P, nt, D]), ALU.add)
                if signal:
                    ins.then_inc(signal, 1)
                else:
                    link(ins)

            def group_norms(g, nt):
                dve.wait_ge(x_ld, 16 * (g + 1))
                norm(xb, nt)
                if not (isinstance(g, int) and g == 0):
                    dve.wait_ge(h0_stored, 16 * g)
                scale_rows(h0, xb, nt, h0_ready)
                dve.wait_ge(h0_ready, g + 1)
                norm(h0, nt)
                if not (isinstance(g, int) and g == 0):
                    dve.wait_ge(xT_ps, g)
                scale_rows(xn, h0, nt)
                affine(xn, nt, ln1, xn_ready)

            def group_qkv(g, nt):
                for t in range(nt):
                    n = g * GT + t
                    dve.wait_ge(qkv_ps, n + 1)
                    if not (isinstance(g, int) and g == 0 and t < 2):
                        dve.wait_ge(qkv_stored[t % 2], 3 * 16 * (g * (GT // 2) + t // 2))
                    o_ = (2 + 2 * (t % 2)) * 512
                    nc.vector.tensor_tensor(qkv[:, t % 2, :], ps[:, o_:o_ + 3 * D], bqkv[:, :], ALU.add).then_inc(qkv_ready, 1)

            group_norms(0, GT)
            group_norms(1, GT)
            group_qkv(0, GT)
            with dve.Fori(1, GROUPS - 1) as g:
                steps.enter(g - 1, 24)
                norms.enter(g - 1, 2)
                group_norms(g + 1, GT)
                group_qkv(g, GT)
            steps.leave(GROUPS - 2)
            norms.leave(GROUPS - 2)
            group_norms(GROUPS, 1)
            group_qkv(GROUPS - 1, GT)
            group_qkv(GROUPS, 1)

            dve.wait_ge(edge_ld, 16 * N_EDGE)
            step(nc.vector.tensor_copy(dstf[:, :], dst_i[:, :]))
            step(nc.vector.tensor_copy(nextf[:, :], next_i[:, :]))
            step(nc.vector.tensor_scalar(Fm[:, 0:RUN].bitcast(i32), dst_i[:, :], 7, None, ALU.arith_shift_right))
            step(nc.vector.tensor_scalar(Fm[:, RUN:2 * RUN].bitcast(i32), dst_i[:, :], P - 1, None, ALU.bitwise_and))
            step(nc.vector.tensor_scalar(ews[:, :], ews[:, :], DH ** -0.5, None, ALU.mult))
            steps.wait()
            step(nc.vector.tensor_copy(dhi[:, :], Fm[:, 0:RUN].bitcast(i32)))
            step(nc.vector.tensor_copy(dlo[:, :], Fm[:, RUN:2 * RUN].bitcast(i32)))
            step(nc.vector.memset(cut[:, 0:1], 1.0))
            step(nc.vector.memset(cut[:, RUN:RUN + 1], 1.0))
            step(nc.vector.tensor_tensor(cut[:, 1:RUN], dstf[:, 1:RUN], dstf[:, 0:RUN - 1], ALU.not_equal))
            step(nc.vector.tensor_scalar(last_rel[:, :], iota49, float(-P), dstf[:, RUN - 1:RUN], ALU.mult, ALU.add))
            step(nc.vector.tensor_tensor(cont[:, :], dstf[:, RUN - 1:RUN], nextf[:, :], ALU.is_equal))
            step(nc.vector.memset(hits_hi[:, 0, :], 0.0))
            step(nc.vector.memset(hits_lo[:, 0, :], 0.0))
            steps.wait()
            step(nc.vector.tensor_scalar(keep[:, :], cut[:, 0:RUN], -1.0, 1.0, ALU.mult, ALU.add))
            steps.wait()
            step(nc.vector.tensor_scalar(cut[:, :], cut[:, :], -BIG, None, ALU.mult))
            nc.vector.tensor_scalar(dst_i[:, :], dst_i[:, :], float(N - 1), None, ALU.min).then_inc(edges_ready, 1)

            with dve.Fori(0, CHUNKS // 2) as i:
                steps.enter(i, 6)
                for par in range(2):
                    c = 2 * i + par
                    dve.wait_ge(hits_used, c + 1)
                    step(nc.vector.tensor_tensor(hits_hi[:, :, :], iota49.unsqueeze(1).to_broadcast([P, CH, TILES]),
                                                 dhi[:, bass.ds(c * CH, CH)].unsqueeze(2).to_broadcast([P, CH, TILES]), ALU.is_equal))
                    nc.vector.tensor_tensor(hits_lo[:, :, :], iota[:, :].unsqueeze(1).to_broadcast([P, CH, P]),
                                            dlo[:, bass.ds(c * CH, CH)].unsqueeze(2).to_broadcast([P, CH, P]), ALU.is_equal).then_inc(hits_ready, 1)
                    k4 = k_ring[par].rearrange("p (t h d) -> p t h d", t=CH, h=H)
                    dve.wait_ge(rows_in[par], 16 * 2 * CH * (i + 1))
                    dve.wait_ge(ep_ready, c + 1)
                    link(nc.vector.tensor_tensor(k4, k4, bank(2 + par)[:, 0:CH * DH].rearrange("p (t d) -> p t d", t=CH).unsqueeze(2)
                                                 .to_broadcast([P, CH, H, DH]), ALU.add))
                    link(nc.vector.tensor_tensor(k_ring[par], k_ring[par], q_ring[par], ALU.mult))
                    nc.vector.tensor_reduce(S[:, bass.ds(c * (CH * H), CH * H)], k_ring[par].rearrange("p (a d) -> p a d", d=DH),
                                            AX.X, ALU.add).then_inc(scores_done, 1)
            steps.leave(CHUNKS // 2)

            dve.wait_ge(hits_used, CHUNKS + 1)
            link(nc.vector.tensor_copy(hist[:, :], bank(4)[0:TILES, 0:P]))
            link(nc.vector.tensor_tensor_scan(tots[:, :], ones[0:TILES, :], hist[:, :], 0.0, ALU.mult, ALU.add))

            S3 = S.rearrange("p (t h) -> p t h", h=H)
            F3 = Fm.rearrange("p (t h) -> p t h", h=H)
            M3 = Mm.rearrange("p (t h) -> p t h", h=H)
            dve.wait_ge(scores_done, CHUNKS + 2)
            link(nc.vector.tensor_tensor(S3, S3, ews[:, :].unsqueeze(2).to_broadcast([P, RUN, H]), ALU.mult))
            for h in range(H):
                step(nc.vector.tensor_tensor_scan(F3[:, :, h], cut[:, 0:RUN], S3[:, :, h], -BIG, ALU.add, ALU.max))
            steps.wait()
            for h in range(H):
                step(nc.vector.tensor_tensor_scan(M3[:, ::-1, h], cut[:, RUN:0:-1], F3[:, ::-1, h], -BIG, ALU.add, ALU.max))
            steps.wait()
            step(nc.vector.tensor_copy(small[:, 0:1], dstf[:, 0:1]))
            step(nc.vector.tensor_copy(small[:, 1:2], dstf[:, RUN - 1:RUN]))
            step(nc.vector.tensor_copy(small[:, 2:2 + H], M3[:, 0, :]))
            step(nc.vector.tensor_copy(small[:, 2 + H:2 + 2 * H], M3[:, RUN - 1, :]))
            steps.wait()
            nr = 2 + 2 * H
            diag = arena[:, 3 * SC:3 * SC + nr * P]
            nc.vector.tensor_tensor(diag.rearrange("p (r n) -> p r n", r=nr), ident[:, :].unsqueeze(1).to_broadcast([P, nr, P]),
                                    small[:, :].unsqueeze(2).to_broadcast([P, nr, P]), ALU.mult).then_inc(diag_ready, 1)
            dve.wait_ge(small_ps, 1)
            pen = sums[:, 0, 0:2, 0:P]
            for f in range(2):
                link(nc.vector.tensor_scalar(pen, ps[:, 0:2 * P].rearrange("p (s n) -> p s n", s=2), small[:, f:f + 1], BIG, ALU.is_equal, ALU.mult))
                link(nc.vector.tensor_scalar(pen, pen, -BIG, None, ALU.add))
                cand = Fm[:, 0:2 * H * P].rearrange("p (s h n) -> p s h n", s=2, h=H)
                link(nc.vector.tensor_tensor(cand, ps[:, 2 * P:nr * P].rearrange("p (s h n) -> p s h n", s=2, h=H),
                                             pen.unsqueeze(2).to_broadcast([P, 2, H, P]), ALU.add))
                link(nc.vector.tensor_reduce(gmax[:, f, :], cand.rearrange("p s h n -> p h s n"), AX.XY, ALU.max))
            for f in range(2):
                mask = Fm[:, f * RUN:(f + 1) * RUN]
                link(nc.vector.tensor_scalar(mask, dstf[:, :], small[:, f:f + 1], BIG, ALU.is_equal, ALU.mult))
                link(nc.vector.tensor_scalar(mask, mask, -BIG, None, ALU.add))
                for h in range(H):
                    step(nc.vector.scalar_tensor_tensor(M3[:, :, h], mask, gmax[:, f, h:h + 1], M3[:, :, h], ALU.add, ALU.max))
                steps.wait()
            nc.vector.tensor_tensor(S, S, Mm, ALU.subtract).then_inc(exp_in, 1)

            dve.wait_ge(small_ps, 2)
            step(nc.vector.tensor_copy(small[0:TILES, 0:1], bank(5)[0:TILES, 0:1]))
            steps.wait()
            nc.vector.tensor_scalar(tots[:, :], tots[:, :], small[0:TILES, 0:1], -1.0, ALU.add, ALU.add).then_inc(diag_ready, 1)
            dve.wait_ge(small_ps, 3)
            nc.vector.tensor_scalar(end_i[:, 0:TILES], bank(6)[:, 0:TILES], 0.0, None, ALU.max).then_inc(end_ready, 1)
            step(nc.vector.tensor_scalar(has[:, 0:TILES], bank(6)[:, P:P + TILES], 0.0, None, ALU.is_gt))
            link(nc.vector.memset(sums[:, 1, CH - 1, :], 0.0))
            dve.wait_ge(exp_done, 1)

            def run_chunk(i, par, first):
                c = 2 * i + par
                new = sums[:, par, :, :]
                step(nc.vector.tensor_copy(keep_c[:, :], keep[:, bass.ds(c * CH, CH)]))
                if not first:
                    dve.wait_ge(run_stored[par], 16 * i)
                ex = S[:, bass.ds(c * (CH * H), CH * H)].rearrange("p (t h) -> p t h", h=H)
                step(nc.vector.tensor_copy(new[:, :, D:ACC], ex))
                dve.wait_ge(v_in[par], 16 * CH * (i + 1))
                for j0 in (0, CH // 2):
                    j1 = j0 + CH // 2
                    ins = nc.vector.tensor_tensor(new[:, j0:j1, 0:D].rearrange("p t (h d) -> p t h d", h=H),
                                                  v_ring[par].rearrange("p (t h d) -> p t h d", t=CH, h=H)[:, j0:j1, :, :],
                                                  ex[:, j0:j1, :].unsqueeze(3).to_broadcast([P, CH // 2, H, DH]), ALU.mult)
                    if j0:
                        ins.then_inc(v_used, 1)
                        dve.wait_ge(v_used, c + 3)
                    else:
                        link(ins)
                for j in range(CH):
                    before = new[:, j - 1, :] if j else sums[:, 1 - par, CH - 1, :]
                    ins = nc.vector.scalar_tensor_tensor(new[:, j, :], before, keep_c[:, j:j + 1], new[:, j, :], ALU.mult, ALU.add)
                    if j < CH - 1:
                        link(ins)
                    else:
                        ins.then_inc(run_ready, 1)
                        dve.wait_ge(run_ready, c + 1)

            run_chunk(0, 0, True)
            run_chunk(0, 1, True)
            with dve.Fori(1, CHUNKS // 2) as i:
                steps.enter(i - 1, 20)
                run_chunk(i, 0, False)
                run_chunk(i, 1, False)
            steps.leave(CHUNKS // 2 - 1)

            def bc(t_, nt):
                return t_.unsqueeze(1).to_broadcast([P, nt, D])

            def D0(g, nt):
                step(nc.vector.tensor_copy(last_c[:, 0:nt], last_rel[:, bass.ds(g * GT, nt)]))
                step(nc.vector.tensor_copy(has_c[:, 0:nt], has[:, bass.ds(g * GT, nt)]))
                steps.wait()
                if not (isinstance(g, int) and g == 0):
                    dve.wait_ge(corr_ps, g * GT)
                for t in range(nt):
                    ins = nc.vector.tensor_scalar(corr[:, t, :], iota[:, :], last_c[:, t:t + 1], cont[:, 0:1], ALU.is_equal, ALU.mult)
                    if t < nt - 1:
                        step(ins)
                    else:
                        ins.then_inc(corr_ready, 1)

            def D1(g, nt):
                dve.wait_ge(got_in, (g * GT + nt) * 16)
                for t in range(nt):
                    dve.wait_ge(corr_ps, g * GT + t + 1)
                    nc.vector.tensor_tensor(got[:, t, :], got[:, t, :], bank(6 + t % 2)[:, 0:ACC], ALU.add).then_inc(corr_used, 1)
                dve.wait_ge(corr_used, g * GT + nt)
                link(nc.vector.reciprocal(rec[:, 0:nt, :], got[:, 0:nt, D:ACC]))
                link(nc.vector.tensor_tensor(rec[:, 0:nt, :], rec[:, 0:nt, :], has_c[:, 0:nt].unsqueeze(2).to_broadcast([P, nt, H]), ALU.mult))
                for t in range(nt):
                    ins = nc.vector.tensor_tensor(attn[:, t, :].rearrange("p (h d) -> p h d", h=H), got[:, t, 0:D].rearrange("p (h d) -> p h d", h=H),
                                                  rec[:, t, :].unsqueeze(2).to_broadcast([P, H, DH]), ALU.mult)
                    if t < nt - 1:
                        step(ins)
                    else:
                        ins.then_inc(attn_ready, 1)

            def D2(g, nt):
                dve.wait_ge(o_ps, g + 1)
                dve.wait_ge(h0_ld, 16 * (g + 1))
                dve.wait_ge(xr_ld, 16 * (g + 1))
                op = bank(4, 2)[:, 0:nt * D].rearrange("p (t d) -> p t d", t=nt)
                link(nc.vector.tensor_tensor(attn[:, 0:nt, :], op, bc(bo_b[:, :], nt), ALU.add))
                link(nc.vector.scalar_tensor_tensor(h0[:, 0:nt, :], attn[:, 0:nt, :], ab[:, 0:1], h0[:, 0:nt, :], ALU.mult, ALU.add))
                link(nc.vector.tensor_tensor(attn[:, 0:nt, :], h0[:, 0:nt, :], xb[:, 0:nt, :], ALU.add))
                norm(h0, nt)
                scale_rows(xn, h0, nt)
                affine(xn, nt, ln2, x1_ready)

            def D3(g, nt):
                dve.wait_ge(f_ps, g + 1)
                fp = bank(4, 2)[:, 0:nt * D].rearrange("p (t d) -> p t d", t=nt)
                link(nc.vector.tensor_tensor(x2[:, 0:nt, :], fp, bc(b2_b[:, :], nt), ALU.add))
                link(nc.vector.scalar_tensor_tensor(x2[:, 0:nt, :], x2[:, 0:nt, :], ab[:, 1:2], attn[:, 0:nt, :], ALU.mult, ALU.add))
                norm(x2, nt)
                scale_rows(xn, x2, nt)
                norm(xn, nt)
                scale_rows(xn, xn, nt)
                affine(xn, nt, lnm, x3_ready)

            def D4(g, nt):
                dve.wait_ge(r_ps, g + 1)
                L, A, B, O1, O2, L2 = (lg[:, j, 0:nt, :] for j in range(6))
                m1_, m2_, df, z, t4, t5 = (tv[:, j, 0:nt] for j in range(6))

                def col(v):
                    return v.unsqueeze(2).to_broadcast([P, nt, NE])

                ib = i8[:, :].unsqueeze(1).to_broadcast([P, nt, NE])
                link(nc.vector.tensor_tensor(L, bank(6)[:, 0:nt * NE].rearrange("p (t e) -> p t e", t=nt), br_b[:, :].unsqueeze(1).to_broadcast([P, nt, NE]), ALU.add))

                def first_of_max(logits, m, one):
                    link(nc.vector.tensor_reduce(m, logits, AX.X, ALU.max))
                    link(nc.vector.tensor_tensor(A, logits, col(m), ALU.is_lt))
                    link(nc.vector.scalar_tensor_tensor(A, A, float(NE), ib, ALU.mult, ALU.add))
                    link(nc.vector.tensor_reduce(t4, A, AX.X, ALU.min))
                    link(nc.vector.tensor_tensor(one, ib, col(t4), ALU.is_equal))

                first_of_max(L, m1_, O1)
                link(nc.vector.scalar_tensor_tensor(L2, O1, -BIG, L, ALU.mult, ALU.add))
                first_of_max(L2, m2_, O2)
                norms.step(nc.vector.tensor_tensor(df, m2_, m1_, ALU.subtract))
                dve.wait_ge(rstd_ready, norms.base + norms.n)
                link(nc.vector.tensor_scalar(t4, z, 1.0, None, ALU.add))
                link(nc.vector.reciprocal(t5, t4))
                link(nc.vector.tensor_tensor(t4, z, t5, ALU.mult))
                link(nc.vector.tensor_tensor(A, O1, col(t5), ALU.mult))
                link(nc.vector.tensor_tensor(B, O2, col(t4), ALU.mult))
                nc.vector.tensor_tensor(wmix[:, 0:nt, :], A, B, ALU.add).then_inc(w_ready, 1)
                dve.wait_ge(w_ready, g + 1)

            def prepare_first(nt):
                D0(0, nt)
                D1(0, nt)
                D2(0, nt)
                D3(0, nt)
                D4(0, nt)

            def group(g, nt, ahead):
                def add(e):
                    dve.wait_ge(y_ps, g * NE + e + 1)
                    dest = yo if e == NE - 1 else y
                    base = x2 if e == 0 else y
                    if e == NE - 1:
                        dve.wait_ge(out_stored, 16 * g + 16)
                    for t in range(nt):
                        ins = nc.vector.scalar_tensor_tensor(dest[:, t, :], bank(2, 2)[:, t * D:(t + 1) * D], wmix[:, t, e:e + 1],
                                                             base[:, t, :], ALU.mult, ALU.add)
                        if t < nt - 1:
                            step(ins)
                        else:
                            ins.then_inc(y_done, 1)
                    steps.wait()
                    dve.wait_ge(y_done, g * NE + e + 2)

                if ahead:
                    D0(g + 1, ahead)
                dve.wait_ge(b_ps, g + 1)
                link(nc.vector.tensor_tensor(x2[:, 0:nt, :], x2[:, 0:nt, :], bank(4, 2)[:, 0:nt * D].rearrange("p (t d) -> p t d", t=nt), ALU.add))
                add(0)
                if ahead:
                    D1(g + 1, ahead)
                add(1)
                add(2)
                if ahead:
                    D2(g + 1, ahead)
                add(3)
                add(4)
                add(5)
                if ahead:
                    D3(g + 1, ahead)
                add(6)
                add(7)
                if ahead:
                    D4(g + 1, ahead)

            prepare_first(GT)
            with dve.Fori(0, TURNS1) as g:
                steps.enter(g, 95)
                norms.enter(g, 4)
                group(g, GT, GT)
            steps.leave(TURNS1)
            norms.leave(TURNS1)
            group(TURNS1, GT, 1)
            group(GROUPS, 1, 0)


_INS = ["x", "src", "dst", "edge_attr_64", "edge_weight", "L0_gnn_Wq", "L0_gnn_bq", "L0_gnn_Wk", "L0_gnn_bk", "L0_gnn_Wv",
        "L0_gnn_bv", "L0_gnn_We", "L0_gnn_be", "L0_gnn_Wo", "L0_gnn_bo", "L0_gnn_ln1_g", "L0_gnn_ln1_b", "L0_gnn_ln2_g",
        "L0_gnn_ln2_b", "L0_gnn_W1", "L0_gnn_b1", "L0_gnn_W2", "L0_gnn_b2", "L0_gnn_alpha", "L0_gnn_beta", "L0_ffn_gamma",
        "L0_ffn_beta", "L0_ffn_Wr", "L0_ffn_br", "L0_ffn_W1", "L0_ffn_b1", "L0_ffn_W2", "L0_ffn_b2"]


def kernel(**inputs):
    import numpy as _np
    import concourse.bacc as _bacc
    from concourse import mybir as _mybir
    from concourse.bass_utils import run_bass_kernel_spmd as _run

    nc = _bacc.Bacc("TRN2", target_bir_lowering=False, num_devices=1)
    arrays, args = {}, []
    for name in _INS:
        a = _np.ascontiguousarray(inputs[name])
        arrays[f"in_{name}"] = a
        args.append(nc.dram_tensor(f"in_{name}", a.shape, _mybir.dt.from_np(a.dtype), kind="ExternalInput").ap())
    args.append(nc.dram_tensor("out_0", (N, D), _mybir.dt.float32, kind="ExternalOutput").ap())
    gnn_moe_program(nc, *args)
    return _run(nc, [arrays], core_ids=[0]).results[0]["out_0"]
```

```python
import concourse.bass as bass
from concourse import mybir
from contextlib import ExitStack

P = 128
N, D, H, ED, FF = 6250, 256, 8, 64, 1024
DH = D // H
E = 100000
NE, EH = 8, 512
EPS = 1e-5
TILES = -(-N // P)
LAST = N - (TILES - 1) * P
ROWS = TILES * P
RUN = 784
CH = 8
CHUNKS = RUN // CH
TAIL = E - (P - 1) * RUN
ACC = D + H
BIG = 1e38
PADNODE = 8191
GT = 4
GROUPS = TILES // GT
GC = FF // P
HC = EH // P
A_SPLIT = 112
EC = CH * P
CE = CHUNKS * EC
LASTP = (E - (CHUNKS - 1) * EC) // CH
VC = 4
SR = 64
SE = SR * P
SLABS = -(-E // SE)
VS = SR // VC
AHEAD = 3
SLAB_TAIL = E - (SLABS - 1) * SE
assert VS % 2 == 0 and SLABS - AHEAD < GROUPS
assert LASTP * CH == E - (CHUNKS - 1) * EC and CE == P * RUN


class Chain:

    def __init__(self, engine, sem):
        self.engine, self.sem, self.base, self.n = engine, sem, 0, 0

    def step(self, instruction):
        instruction.then_inc(self.sem, 1)
        self.n += 1

    def wait(self, hold=False):
        self.engine.wait_ge(self.sem, self.base + self.n)
        if hold:
            self.engine.nop(nofuse=True)

    def link(self, instruction):
        self.step(instruction)
        self.wait()

    def enter(self, i, per_turn):
        self.start = self.base + self.n
        self.base, self.n, self.per = self.start + i * per_turn, 0, per_turn

    def leave(self, turns):
        assert self.n == self.per, (self.n, self.per)
        self.base, self.n = self.start + turns * self.per, 0


def gnn_moe_program(nc, x, src, dst, ef, ew, Wq, bq, Wk, bk, Wv, bv, We, be, Wo, bo, g1, b1n, g2, b2n,
                    W1, b1, W2, b2, alpha, beta, gm, bm, Wr, br, M1, mb1, M2, mb2, out):
    f32, i32, bf16 = mybir.dt.float32, mybir.dt.int32, mybir.dt.bfloat16
    ALU, ACT, AX = mybir.AluOpType, mybir.ActivationFunctionType, mybir.AxisListType
    TURNS1 = GROUPS - 1

    q_rows = nc.dram_tensor("q_rows", [ROWS + P, D], f32)
    score_rows = nc.dram_tensor("score_rows", [CE, H], f32)
    k_rows = nc.dram_tensor("k_rows", [ROWS, D], f32)
    v_rows = nc.dram_tensor("v_rows", [ROWS, D], f32)
    h0_rows = nc.dram_tensor("h0_rows", [ROWS, D], f32)
    exp_rows = nc.dram_tensor("exp_rows", [SLABS * SE, H], f32)
    sum_rows = nc.dram_tensor("sum_rows", [SLABS * SE, ACC], f32)
    ring_rows = nc.dram_tensor("ring_rows", [AHEAD * SE, ACC], f32)
    carry_rows = nc.dram_tensor("carry_rows", [SLABS * P + 1, ACC], f32)

    with ExitStack() as ctx:
        def sb(name, shape, dt=f32):
            return ctx.enter_context(nc.sbuf_tensor(name, shape, dt))

        def sem(name):
            return ctx.enter_context(nc.semaphore(name))

        ident = sb("ident", [P, P])
        ones = sb("ones", [P, P])
        iota = sb("iota", [P, P])
        tri = sb("tri", [P, P])
        early = sb("early", [P, 5 * 3 * D])
        wqkv = early[:, 0:6 * D].rearrange("p (k n) -> p k n", k=2)
        qkv = early[:, 6 * D:12 * D].rearrange("p (r n) -> p r n", r=2)
        bqkv = early[:, 12 * D:15 * D]
        x2, y, yo = (early[:, j * GT * D:(j + 1) * GT * D].rearrange("p (t d) -> p t d", t=GT) for j in range(3))
        row_diag = early[:, 12 * D:12 * D + P]
        mask_in = early[:, 12 * D + P:12 * D + 2 * P]
        mask_over = early[:, 12 * D + 2 * P:12 * D + 3 * P]
        carry = early[:, 12 * D + 3 * P:12 * D + 3 * P + ACC]
        assert 3 * P + ACC <= 3 * D
        beb = sb("beb", [P, DH])
        ln1 = sb("ln1", [P, 2, D])
        ln2 = sb("ln2", [P, 2, D])
        lnm = sb("lnm", [P, 2, D])
        weblk = sb("weblk", [P, 2 * DH])
        wo = sb("wo", [P, 2, D])
        bo_b = sb("bo_b", [P, D])
        b2_b = sb("b2_b", [P, D])
        ab = sb("ab", [P, 2])
        w1 = sb("w1", [P, 2, FF])
        w2 = sb("w2", [P, GC, D])
        wr = sb("wr", [P, 2, NE])
        br_b = sb("br_b", [P, NE])
        mb2_sb = sb("mb2_sb", [NE, D])
        bias_raw = sb("bias_raw", [GC + NE * HC, P])
        bias_T = sb("bias_T", [P, GC + NE * HC])
        half = sb("half", [P, GT])
        ebase = sb("ebase", [P, GT])
        i8 = sb("i8", [P, NE])

        st = sb("st", [P, GT, 6])
        mv = sb("mv", [P, GT, 2])
        ve = sb("ve", [P, GT])
        rs = sb("rs", [P, GT])

        src_all = sb("src_all", [P, SLABS * SR], i32)
        src_i = src_all[:, 0:RUN]
        assert SLABS * SR >= RUN
        gat_i = sb("gat_i", [P, 2, 2 * CH], i32)
        edges = sb("edges", [P, 4 * RUN + 1])
        dst_i = edges[:, 0:RUN].bitcast(i32)
        dstf = edges[:, RUN:2 * RUN]
        ews = edges[:, 2 * RUN:3 * RUN]
        cut = edges[:, 3 * RUN:4 * RUN + 1]
        attn = edges[:, 0:GT * D].rearrange("p (t d) -> p t d", t=GT)
        wT = edges[0:NE, GT * D:GT * D + GT * P]
        got_carry = edges[:, GT * (D + P):GT * (D + P) + GT * ACC].rearrange("p (t n) -> p t n", t=GT)
        ex_slab = edges[:, GT * (D + P + ACC):GT * (D + P + ACC) + SR * H]
        assert GT * (D + P + ACC) + SR * H <= 4 * RUN + 1
        keep = sb("keep", [P, SLABS, SR])
        keep_c = sb("keep_c", [P, VC])
        keep_all = keep[:, :, :].rearrange("p s j -> p (s j)")
        bounds = sb("bounds", [P, SLABS, 3])
        bounds_all = bounds[:, :, :].rearrange("p s j -> p (s j)")
        bound_c = sb("bound_c", [P, 3])
        same = sb("same", [P, 1])
        last_part = sb("last_part", [P, 1])
        late = sb("late", [P, TILES])
        hist_T = sb("hist_T", [P, TILES])
        late_max = sb("late_max", [P, 1])
        late_i = sb("late_i", [1, 1], i32)
        totals = sb("totals", [P, ACC])
        span_i = sb("span_i", [CHUNKS, 2], i32)
        span = sb("span", [CHUNKS, 2])
        slow_i = sb("slow_i", [1, 1], i32)
        iota_col = sb("iota_col", [P, 1])
        win_id = sb("win_id", [P, 2])
        hist = sb("hist", [TILES, P])
        tots = sb("tots", [TILES, P])
        end_i = sb("end_i", [P, TILES + GT], i32)
        ring_i = sb("ring_i", [P, TILES + GT], i32)
        end_c = sb("end_c", [P, 2 * GT], i32)
        carry_i = sb("carry_i", [P, TILES + GT], i32)
        has = sb("has", [P, TILES + GT])
        has_c = sb("has_c", [P, GT])
        small = sb("small", [P, 2 + 2 * H])
        gmax = sb("gmax", [P, 2, H])
        sums = sb("sums", [P, 2, VC, ACC])
        v_ring = sb("v_ring", [P, 2, VC * D])

        SC = RUN * H
        arena = sb("arena", [P, 3 * SC + 4 * CH * D])
        S = arena[:, 0:SC]
        Fm = arena[:, SC:2 * SC]
        Mm = arena[:, 2 * SC:3 * SC]
        o = 3 * SC
        q_ring = [arena[:, o + r * CH * D:o + (r + 1) * CH * D] for r in range(2)]
        k_ring = [arena[:, o + (2 + r) * CH * D:o + (3 + r) * CH * D] for r in range(2)]
        m1_sb = arena[:, SC:SC + NE * 2 * EH].rearrange("p (e k n) -> p e k n", e=NE, k=2)
        m2_sb = arena[:, SC + NE * 2 * EH:SC + NE * (2 * EH + HC * D)].rearrange("p (e c n) -> p e c n", e=NE, c=HC)
        assert NE * (2 * EH + HC * D) <= 2 * SC + 2 * CH * D
        hid = [arena[:, r * HC * 512:(r + 1) * HC * 512].rearrange("p (c n) -> p c n", c=HC) for r in range(2)]
        x3T = arena[:, 2 * HC * 512:2 * HC * 512 + 2 * GT * P].rearrange("p (k n) -> p k n", k=2)
        got = arena[:, 2 * HC * 512 + 2 * GT * P:2 * HC * 512 + 2 * GT * P + GT * ACC].rearrange("p (t n) -> p t n", t=GT)
        assert 2 * HC * 512 + 2 * GT * P + GT * ACC <= SC
        hidg = arena[:, o + 2 * CH * D:o + 4 * CH * D].rearrange("p (c n) -> p c n", c=GC)

        win_hot = [Fm[:, r * EC:(r + 1) * EC] for r in range(2)]
        dst_row = [Fm[:, (2 + r) * EC:(3 + r) * EC].bitcast(i32) for r in range(2)]
        q_win = [Fm[:, 4 * EC + r * D:4 * EC + (r + 1) * D] for r in range(2)]
        assert 4 * EC + 2 * D <= SC
        dst_slab = Fm[:, 2 * RUN:2 * RUN + SLABS * SR].bitcast(i32)
        src_c = Mm[:, 0:RUN].bitcast(i32)
        zrow = Mm[:, RUN:RUN + D]
        zeros = Mm[:, RUN + D:RUN + D + 512]
        sc_out = [Mm[:, RUN + r * CH * H:RUN + (r + 1) * CH * H] for r in range(2)]

        xb = sb("xb", [P, GT, D])
        h0 = sb("h0", [P, GT, D])
        xn = sb("xn", [P, GT, D])
        xT = sb("xT", [P, 2, GT * P])
        efb = h0[:, :, :].rearrange("p t d -> p (t d)").rearrange("p (r n) -> p r n", r=2)
        efT = xT
        xn16 = xn[:, :, :].rearrange("p t d -> p (t d)").bitcast(bf16)
        hits_hi = xn16[:, 0:CH * TILES].rearrange("p (t n) -> p t n", t=CH)
        hits_lo = xn16[:, CH * TILES:CH * (TILES + P)].rearrange("p (t n) -> p t n", t=CH)
        xb16 = xb[:, :, :].rearrange("p t d -> p (t d)").bitcast(bf16)
        dhi = xb16[:, 0:RUN]
        dlo = xb16[:, RUN:2 * RUN]
        rec = sb("rec", [P, GT, H])
        lg = sb("lg", [P, 6, GT, NE])
        tv = sb("tv", [P, 6, GT])
        wmix = sb("wmix", [P, GT, NE])
        iota49 = iota[:, 0:TILES]

        ps = ctx.enter_context(nc.psum_tensor("ps", [P, 8 * 512], f32))

        def bank(b, n=1):
            return ps[:, b * 512:(b + n) * 512]

        const_ld = sem("const_ld")
        edge_ld = sem("edge_ld")
        pool_const = sem("pool_const")
        dve_steps = sem("dve_steps")
        pool_steps = sem("pool_steps")
        bias_ps = sem("bias_ps")
        bias_done = sem("bias_done")
        x_ld = sem("x_ld")
        h0_ready = sem("h0_ready")
        h0_stored = sem("h0_stored")
        var_ready = sem("var_ready")
        rstd_ready = sem("rstd_ready")
        xn_ready = sem("xn_ready")
        xT_ps = sem("xT_ps")
        xT_ready = sem("xT_ready")
        qkv_ps = sem("qkv_ps")
        qkv_ready = sem("qkv_ready")
        qkv_stored = [sem("qkv_stored0"), sem("qkv_stored1")]
        edges_ready = sem("edges_ready")
        idx_ready = sem("idx_ready")
        rows_in = [sem("rows_in0"), sem("rows_in1")]
        scores_done = sem("scores_done")
        ef_ld = [sem("ef_ld0"), sem("ef_ld1")]
        efT_ps = sem("efT_ps")
        efT_ready = sem("efT_ready")
        ep_ready = sem("ep_ready")
        hits_ready = sem("hits_ready")
        hits_used = sem("hits_used")
        diag_ready = sem("diag_ready")
        wide_ready = sem("wide_ready")
        wide_ps = sem("wide_ps")
        path_known = sem("path_known")
        srcc_ld = sem("srcc_ld")
        dstrow_ld = [sem("dstrow_ld0"), sem("dstrow_ld1")]
        qwin_ld = [sem("qwin_ld0"), sem("qwin_ld1")]
        hot_ready = sem("hot_ready")
        q_ps = sem("q_ps")
        q_used = sem("q_used")
        score_out = [sem("score_out0"), sem("score_out1")]
        score_in = sem("score_in")
        pad_stored = sem("pad_stored")
        small_ps = sem("small_ps")
        end_ready = sem("end_ready")
        exp_in = sem("exp_in")
        late_ready = sem("late_ready")
        late_ps = sem("late_ps")
        late_known = sem("late_known")
        exp_stored = sem("exp_stored")
        zero_stored = sem("zero_stored")
        src_ld = sem("src_ld")
        ex_ld = sem("ex_ld")
        row_ready = sem("row_ready")
        row_ps = sem("row_ps")
        masks_ready = sem("masks_ready")
        carry_ps = sem("carry_ps")
        carry_ready = sem("carry_ready")
        carry_stored = sem("carry_stored")
        end_idx = sem("end_idx")
        exp_done = sem("exp_done")
        v_in = [sem("v_in0"), sem("v_in1")]
        v_used = sem("v_used")
        run_ready = sem("run_ready")
        run_stored = [sem("run_stored0"), sem("run_stored1")]
        w_ld = sem("w_ld")
        got_in = sem("got_in")
        h0_ld = sem("h0_ld")
        xr_ld = sem("xr_ld")
        attn_ready = sem("attn_ready")
        t_ps = sem("t_ps")
        t_ready = sem("t_ready")
        o_ps = sem("o_ps")
        x1_ready = sem("x1_ready")
        h_ps = sem("h_ps")
        h_ready = sem("h_ready")
        f_ps = sem("f_ps")
        x3_ready = sem("x3_ready")
        r_ps = sem("r_ps")
        w_ready = sem("w_ready")
        wT_ps = sem("wT_ps")
        wT_ready = sem("wT_ready")
        b_ps = sem("b_ps")
        b_used = sem("b_used")
        y_ps = sem("y_ps")
        y_done = sem("y_done")
        out_stored = sem("out_stored")

        block = ctx.enter_context(nc.Block())

        def flat(v, p):
            return v.rearrange("(p n) -> p n", p=p)

        N_CONST = 25
        STEP_STEPS = 2 + VC - 1
        SLAB_STEPS = 2 + VS * STEP_STEPS + 2
        FAST_MORE = 0
        N_EDGE = 17

        @block.sync
        def _(sp):
            def x_tiles(dst_t, g, nt, s):
                if nt == GT:
                    sp.dma_start(dst_t[:, :, :], x[bass.ds(g * (GT * P), GT * P), :].rearrange("(t p) d -> p t d", p=P)).then_inc(s, 16)
                else:
                    sp.dma_start(dst_t[0:LAST, 0, :], x[(TILES - 1) * P:N, :]).then_inc(s, 16)

            x_tiles(xb, 0, GT, x_ld)
            sp.sem_inc(out_stored, 16)
            for j, w in enumerate((Wq, Wk, Wv)):
                sp.dma_start(wqkv[:, :, j * D:(j + 1) * D], w.rearrange("(c p) n -> p c n", p=P)).then_inc(const_ld, 16)
            for j, b in enumerate((bq, bk, bv)):
                sp.dma_start(bqkv[:, j * D:(j + 1) * D], b.partition_broadcast(P)).then_inc(const_ld, 16)
            sp.dma_start(beb[:, :], be.partition_broadcast(P)).then_inc(const_ld, 16)
            for t, (g, b) in ((ln1, (g1, b1n)), (ln2, (g2, b2n)), (lnm, (gm, bm))):
                sp.dma_start(t[:, 0, :], g.partition_broadcast(P)).then_inc(const_ld, 16)
                sp.dma_start(t[:, 1, :], b.partition_broadcast(P)).then_inc(const_ld, 16)
            sp.dma_start(wo[:, :, :], Wo.rearrange("(c p) n -> p c n", p=P)).then_inc(const_ld, 16)
            sp.dma_start(bo_b[:, :], bo.partition_broadcast(P)).then_inc(const_ld, 16)
            sp.dma_start(b2_b[:, :], b2.partition_broadcast(P)).then_inc(const_ld, 16)
            sp.dma_start(ab[:, 0:1], alpha.partition_broadcast(P)).then_inc(const_ld, 16)
            sp.dma_start(ab[:, 1:2], beta.partition_broadcast(P)).then_inc(const_ld, 16)
            sp.dma_start(wr[:, :, :], Wr.rearrange("(c p) n -> p c n", p=P)).then_inc(const_ld, 16)
            sp.dma_start(br_b[:, :], br.partition_broadcast(P)).then_inc(const_ld, 16)
            sp.dma_start(mb2_sb[:, :], mb2).then_inc(const_ld, 16)
            sp.dma_start(w1[:, :, :], W1.rearrange("(c p) n -> p c n", p=P)).then_inc(const_ld, 16)
            sp.dma_start(w2[:, :, :], W2.rearrange("(c p) n -> p c n", p=P)).then_inc(const_ld, 16)
            sp.dma_start(bias_raw[0:GC, :], b1.rearrange("(c p) -> c p", p=P)).then_inc(const_ld, 16)
            sp.dma_start(bias_raw[GC:GC + NE * HC, :], mb1.rearrange("e (c p) -> (e c) p", p=P)).then_inc(const_ld, 16)

            def h0_out(g, nt):
                sp.wait_ge(h0_ready, g + 1)
                sp.dma_start(h0_rows[bass.ds(g * (GT * P), nt * P), :].rearrange("(t p) d -> p t d", p=P), h0[:, 0:nt, :]).then_inc(h0_stored, 16)

            with sp.Fori(0, TURNS1) as g:
                h0_out(g, GT)
                x_tiles(xb, g + 1, GT, x_ld)
            h0_out(TURNS1, GT)
            x_tiles(xb, GROUPS, 1, x_ld)
            h0_out(GROUPS, 1)

            def ef_in(c, par):
                v = ef[0:(P - 1) * RUN, :].rearrange("(p r) d -> p (r d)", p=P - 1)
                w = CH * ED
                sp.dma_start(efb[0:A_SPLIT, par, :], v[0:A_SPLIT, bass.ds(c * w, w)]).then_inc(ef_ld[par], 16)
                sp.dma_start(efb[A_SPLIT:P - 1, par, :], v[A_SPLIT:P - 1, bass.ds(c * w, w)]).then_inc(ef_ld[par], 16)

            def ef_tail(c, par):
                w = CH * ED
                t = ef[(P - 1) * RUN:E, :].rearrange("(p r) d -> p (r d)", p=1)
                sp.dma_start(efb[P - 1:P, par, :], t[:, bass.ds(c * w, w)]).then_inc(ef_ld[par], 16)

            def ef_tail_again(par):
                w = CH * ED
                t = ef[(P - 1) * RUN:E, :].rearrange("(p r) d -> p (r d)", p=1)
                sp.dma_start(efb[P - 1:P, par, :], t[:, TAIL // CH * w - w:TAIL // CH * w]).then_inc(ef_ld[par], 16)

            sp.wait_ge(h0_stored, 16 * (GROUPS + 1))
            sp.wait_ge(xn_ready, GROUPS + 1)
            sp.wait_ge(path_known, 1)
            slow = sp.value_load(slow_i[0:1, 0:1], min_val=0, max_val=CHUNKS)
            with sp.If(slow > 0):
                for par in range(2):
                    ef_in(par, par)
                    ef_tail(par, par)
                half_tail = TAIL // CH // 2
                with sp.Fori(0, half_tail - 1) as i:
                    for par in range(2):
                        sp.wait_ge(efT_ps, 2 * i + par + 1)
                        ef_in(2 * i + par + 2, par)
                        ef_tail(2 * i + par + 2, par)
                with sp.Fori(half_tail - 1, CHUNKS // 2 - 1) as i:
                    for par in range(2):
                        sp.wait_ge(efT_ps, 2 * i + par + 1)
                        ef_in(2 * i + par + 2, par)
                        ef_tail_again(par)

            with sp.Else():
                def chunk_in(c, par, np_):
                    w = CH * ED
                    sp.dma_start(efb[0:np_, par, :], ef[bass.ds(c * EC, np_ * CH), :].rearrange("(p r) d -> p (r d)", p=np_)).then_inc(ef_ld[par], 16)

                def dst_in(c, par, n):
                    sp.dma_start(dst_row[par][:, 0:n], dst[bass.ds(c * EC, n)].partition_broadcast(P)).then_inc(dstrow_ld[par], 16)

                def win_in(c, par):
                    first = sp.value_load(dst[bass.ds(c * EC, 1)].rearrange("(o n) -> o n", o=1), min_val=0, max_val=N - 1)
                    sp.dma_start(q_win[par], q_rows[bass.ds(first, P), :]).then_inc(qwin_ld[par], 16)

                sp.wait_ge(edges_ready, 1)
                sp.wait_ge(pad_stored, 16)
                sp.wait_ge(qkv_stored[0], 3 * 16 * (TILES // 2 + 1))
                sp.wait_ge(qkv_stored[1], 3 * 16 * (TILES // 2))
                sp.dma_start(src_c[:, 0:(CHUNKS - 1) * CH].rearrange("p (c j) -> p c j", j=CH),
                             src[0:(CHUNKS - 1) * EC].rearrange("(c p j) -> p c j", p=P, j=CH)).then_inc(srcc_ld, 16)
                sp.dma_start(src_c[0:LASTP, (CHUNKS - 1) * CH:RUN], src[(CHUNKS - 1) * EC:E].rearrange("(p j) -> p j", j=CH)).then_inc(srcc_ld, 16)
                for par in range(2):
                    chunk_in(par, par, P)
                    dst_in(par, par, EC)
                    win_in(par, par)

                def turn(c, par, np_):
                    sp.wait_ge(efT_ps, c + 1)
                    chunk_in(c + 2, par, np_)
                    sp.wait_ge(hot_ready, c + 1)
                    sp.nop(nofuse=True)
                    dst_in(c + 2, par, np_ * CH)
                    sp.wait_ge(q_ps, 2 * c + 2)
                    sp.nop(nofuse=True)
                    win_in(c + 2, par)
                    scores_go(c, par)

                def scores_go(c, par):
                    sp.wait_ge(scores_done, c + 3)
                    sp.dma_start(score_rows[bass.ds(c * EC, EC), :].rearrange("(p j) h -> p (j h)", p=P), sc_out[par]).then_inc(score_out[par], 16)

                with sp.Fori(0, CHUNKS // 2 - 2) as i:
                    for par in range(2):
                        turn(2 * i + par, par, P)
                turn(CHUNKS - 4, 0, P)
                turn(CHUNKS - 3, 1, LASTP)
                scores_go(CHUNKS - 2, 0)
                scores_go(CHUNKS - 1, 1)
                for par in range(2):
                    sp.wait_ge(score_out[par], 16 * (CHUNKS // 2 + 1))
                sp.dma_start(S, score_rows[:, :].rearrange("(p r) h -> p (r h)", p=P)).then_inc(score_in, 16)

            sp.wait_ge(scores_done, CHUNKS + 2)
            for j in range(SLABS - 1):
                sp.dma_start(src_all[:, j * SR:(j + 1) * SR], src[j * SE:(j + 1) * SE].rearrange("(p j) -> p j", p=P)).then_inc(src_ld, 16)
            full, part = SLAB_TAIL // SR, SLAB_TAIL % SR
            last_slab = src[(SLABS - 1) * SE:E]
            sp.dma_start(src_all[0:full, (SLABS - 1) * SR:SLABS * SR], last_slab[0:full * SR].rearrange("(p j) -> p j", j=SR)).then_inc(src_ld, 16)
            sp.dma_start(src_all[full:full + 1, (SLABS - 1) * SR:(SLABS - 1) * SR + part], last_slab[full * SR:SLAB_TAIL].rearrange("(p j) -> p j", p=1)).then_inc(src_ld, 16)

            def exp_slab(n):
                if not (isinstance(n, int) and n == 0):
                    sp.wait_ge(run_ready, n * VS)
                sp.dma_start(ex_slab, exp_rows[bass.ds(n * SE, SE), :].rearrange("(p r) h -> p (r h)", p=P)).then_inc(ex_ld, 16)

            def sums_out(n, k, rows):
                sp.wait_ge(run_ready, n * VS + k + 1)
                rows = rows.rearrange("(p r) a -> p (r a)", p=P)
                sp.dma_start(rows[:, k * (VC * ACC):(k + 1) * (VC * ACC)],
                             sums[:, k % 2, :, :].rearrange("p t a -> p (t a)")).then_inc(run_stored[k % 2], 16)

            def carry_out(n):
                sp.wait_ge(carry_ready, n + 1)
                sp.dma_start(carry_rows[bass.ds(n * P, P), :], carry).then_inc(carry_stored, 16)

            def slab(n, rows):
                exp_slab(n)
                for k in range(VS):
                    sums_out(n, k, rows)
                carry_out(n)

            sp.wait_ge(exp_stored, 16)
            sp.wait_ge(zero_stored, 48)
            sp.wait_ge(late_known, 1)
            late_slabs = sp.value_load(late_i[0:1, 0:1], min_val=0, max_val=P)
            with sp.If(late_slabs > 0):
                slab(0, sum_rows[0:SE, :])
                with sp.Fori(1, SLABS) as n:
                    slab(n, sum_rows[bass.ds(n * SE, SE), :])
            with sp.Else():
                for n in range(AHEAD):
                    slab(n, ring_rows[n * SE:(n + 1) * SE, :])

            def node_in(g, nt):
                sp.dma_start(h0[:, 0:nt, :], h0_rows[bass.ds(g * (GT * P), nt * P), :].rearrange("(t p) d -> p t d", p=P)).then_inc(h0_ld, 16)
                x_tiles(xb, g, nt, xr_ld)

            def rows_out(g, nt):
                sp.wait_ge(y_done, (g + 1) * NE + 1)
                if nt == GT:
                    sp.dma_start(out[bass.ds(g * (GT * P), GT * P), :].rearrange("(t p) d -> p t d", p=P), yo[:, :, :]).then_inc(out_stored, 16)
                else:
                    sp.dma_start(out[(TILES - 1) * P:N, :], yo[0:LAST, 0, :]).then_inc(out_stored, 16)

            def beside(g, r, steps_out, first=False, last=False):
                with sp.If(late_slabs > 0):
                    pass
                with sp.Else():
                    if first:
                        exp_slab(g + AHEAD)
                    for k in steps_out:
                        sums_out(g + AHEAD, k, ring_rows[r * SE:(r + 1) * SE, :])
                    if last:
                        carry_out(g + AHEAD)

            node_in(0, GT)
            sp.wait_ge(x1_ready, 1)
            node_in(1, GT)
            def turn_beside(g, r):
                beside(g, r, range(0, 4), first=True)
                sp.wait_ge(x1_ready, g + 2)
                node_in(g + 2, GT)
                beside(g, r, range(4, VS))
                rows_out(g, GT)
                beside(g, r, (), last=True)

            assert (SLABS - AHEAD) % AHEAD == 1
            with sp.Fori(0, (SLABS - AHEAD) // AHEAD) as i:
                for r in range(AHEAD):
                    turn_beside(AHEAD * i + r, r)
            turn_beside(SLABS - AHEAD - 1, 0)
            for g in range(SLABS - AHEAD, TURNS1):
                sp.wait_ge(x1_ready, g + 2)
                node_in(g + 2, GT if g + 2 < GROUPS else 1)
                rows_out(g, GT)
            rows_out(TURNS1, GT)
            rows_out(GROUPS, 1)
            sp.wait_ge(out_stored, 16 * (GROUPS + 2))

        @block.gpsimd
        def _(pool):
            pool.memset(ident[:, :], 0.0).then_inc(pool_steps, 1)
            pool.memset(ones[:, :], 1.0).then_inc(pool_steps, 1)
            pool.memset(half[:, :], -0.5).then_inc(pool_steps, 1)
            pool.memset(ebase[:, :], 2.718281828459045).then_inc(pool_steps, 1)
            pool.memset(src_all[:, :], 0).then_inc(pool_const, 1)
            pool.memset(dst_slab, PADNODE).then_inc(pool_const, 1)
            pool.memset(dst_i[:, :], PADNODE).then_inc(pool_const, 1)
            pool.memset(ews[:, :], 0.0).then_inc(pool_const, 1)
            pool.memset(weblk[:, :], 0.0).then_inc(pool_const, 1)
            pool.memset(zrow, 0.0).then_inc(pool_const, 1)
            pool.memset(zeros, 0.0).then_inc(pool_const, 1)
            pool.iota(iota_col[:, :], pattern=[[0, 1]], base=0, channel_multiplier=1, allow_small_or_imprecise_dtypes=True).then_inc(pool_steps, 1)
            pool.iota(iota[:, :], pattern=[[1, P]], base=0, channel_multiplier=0, allow_small_or_imprecise_dtypes=True).then_inc(pool_steps, 1)
            pool.iota(i8[:, :], pattern=[[1, NE]], base=0, channel_multiplier=0, allow_small_or_imprecise_dtypes=True).then_inc(pool_steps, 1)
            pool.wait_ge(pool_steps, 7)
            pool.affine_select(out=ident[:, :], in_=ident[:, :], compare_op=ALU.not_equal, fill=1.0, base=0,
                               pattern=[[-1, P]], channel_multiplier=1).then_inc(pool_steps, 1)
            pool.affine_select(out=tri[:, :], in_=ones[:, :], compare_op=ALU.is_gt, fill=0.0, base=0,
                               pattern=[[1, P]], channel_multiplier=-1).then_inc(pool_steps, 1)

            def rstd(n, nt):
                pool.wait_ge(var_ready, n + 1)
                nc.gpsimd.tensor_tensor(rs[:, 0:nt], ve[:, 0:nt], half[:, 0:nt], ALU.pow).then_inc(rstd_ready, 1)

            with pool.Fori(0, GROUPS) as g:
                rstd(2 * g, GT)
                rstd(2 * g + 1, GT)
            rstd(2 * GROUPS, 1)
            rstd(2 * GROUPS + 1, 1)

            pool.wait_ge(edges_ready, 1)
            pool.wait_ge(qkv_stored[0], 3 * 16 * (TILES // 2 + 1))
            pool.wait_ge(qkv_stored[1], 3 * 16 * (TILES // 2))

            def gather(dst_t, table, par, j, s):
                pool.indirect_dma_start(dst_t, None, table[:, :], bass.IndirectOffsetOnAxis(ap=gat_i[:, par, j:j + 1], axis=0)).then_inc(s, 16)

            pool.wait_ge(path_known, 1)
            slow = pool.value_load(slow_i[0:1, 0:1], min_val=0, max_val=CHUNKS)
            with pool.If(slow > 0):
                with pool.Fori(0, CHUNKS // 2) as i:
                    for par in range(2):
                        c = 2 * i + par
                        pool.wait_ge(scores_done, c + 1)
                        pool.nop(nofuse=True)
                        pool.tensor_copy(gat_i[:, par, 0:CH], src_i[:, bass.ds(c * CH, CH)]).then_inc(idx_ready, 1)
                        pool.tensor_copy(gat_i[:, par, CH:2 * CH], dst_i[:, bass.ds(c * CH, CH)]).then_inc(idx_ready, 1)
                        pool.wait_ge(idx_ready, 2 * c + 2)
                        pool.nop(nofuse=True)
                        for j in range(CH):
                            gather(k_ring[par][:, j * D:(j + 1) * D], k_rows, par, j, rows_in[par])
                            gather(q_ring[par][:, j * D:(j + 1) * D], q_rows, par, CH + j, rows_in[par])

            with pool.Else():
                pool.memset(gat_i[:, :, :], 0).then_inc(idx_ready, 1)
                pool.wait_ge(srcc_ld, 32)
                pool.nop(nofuse=True)
                pool.wait_ge(idx_ready, 1)
                pool.nop(nofuse=True)

                def k_chunk(i, par, np_):
                    c = 2 * i + par
                    pool.wait_ge(scores_done, c + 1)
                    pool.nop(nofuse=True)
                    pool.tensor_copy(gat_i[0:np_, par, 0:CH], src_c[0:np_, bass.ds(c * CH, CH)]).then_inc(idx_ready, 1)
                    pool.wait_ge(idx_ready, c + 2)
                    pool.nop(nofuse=True)
                    for j in range(CH):
                        gather(k_ring[par][:, j * D:(j + 1) * D], k_rows, par, j, rows_in[par])

                with pool.Fori(0, CHUNKS // 2 - 1) as i:
                    for par in range(2):
                        k_chunk(i, par, P)
                k_chunk(CHUNKS // 2 - 1, 0, P)
                k_chunk(CHUNKS // 2 - 1, 1, LASTP)
                pool.sem_inc(idx_ready, CHUNKS - 1)

            pool.wait_ge(src_ld, 16 * (SLABS + 1))
            pool.nop(nofuse=True)

            def v_rows_in(n, k):
                c, par = n * VS + k, k % 2
                pool.wait_ge(v_used, c + 1)
                pool.nop(nofuse=True)
                pool.tensor_copy(gat_i[:, par, 0:VC], src_all[:, bass.ds(n * SR + k * VC, VC)]).then_inc(idx_ready, 1)
                pool.wait_ge(idx_ready, 2 * CHUNKS + c + 1)
                pool.nop(nofuse=True)
                for j in range(VC):
                    gather(v_ring[:, par, j * D:(j + 1) * D], v_rows, par, j, v_in[par])

            with pool.Fori(0, AHEAD) as n:
                for k in range(VS):
                    v_rows_in(n, k)
            pool.wait_ge(late_known, 1)
            late_slabs = pool.value_load(late_i[0:1, 0:1], min_val=0, max_val=P)
            with pool.If(late_slabs > 0):
                with pool.Fori(AHEAD, SLABS) as n:
                    for k in range(VS):
                        v_rows_in(n, k)
                for par in range(2):
                    pool.wait_ge(run_stored[par], 16 * (SLABS * VS // 2 + 1))
                pool.wait_ge(carry_stored, 16 * SLABS)

            pool.wait_ge(end_ready, 2)
            pool.wait_ge(zero_stored, 48)

            def ends(g, nt):
                done = min(max(g + 2, AHEAD), SLABS) if isinstance(g, int) else g + 2
                for par in range(2):
                    pool.wait_ge(run_stored[par], 16 * (done * (VS // 2) + 1))
                pool.wait_ge(carry_stored, 16 * done)
                pool.nop(nofuse=True)
                def rows_of(ends_i, table):
                    pool.tensor_copy(end_c[:, 0:nt], ends_i[:, bass.ds(g * GT, nt)]).then_inc(end_idx, 1)
                    pool.tensor_copy(end_c[:, GT:GT + nt], carry_i[:, bass.ds(g * GT, nt)]).then_inc(end_idx, 1)
                    pool.wait_ge(end_idx, 2 * g + 2)
                    pool.nop(nofuse=True)
                    for t in range(nt):
                        pool.indirect_dma_start(got[:, t, :], None, table[:, :],
                                                bass.IndirectOffsetOnAxis(ap=end_c[:, t:t + 1], axis=0)).then_inc(got_in, 16)
                        pool.indirect_dma_start(got_carry[:, t, :], None, carry_rows[:, :],
                                                bass.IndirectOffsetOnAxis(ap=end_c[:, GT + t:GT + t + 1], axis=0)).then_inc(got_in, 16)

                with pool.If(late_slabs > 0):
                    rows_of(end_i, sum_rows)
                with pool.Else():
                    rows_of(ring_i, ring_rows)

            n0 = 2 * (GROUPS + 1)

            def norm_power(g, j, nt):
                rstd(n0 + g * 4 + j, nt)

            def weight_power(g, nt):
                pool.wait_ge(var_ready, n0 + g * 4 + 4)
                nc.gpsimd.tensor_tensor(tv[:, 3, 0:nt], ebase[:, 0:nt], tv[:, 2, 0:nt], ALU.pow).then_inc(rstd_ready, 1)

            def powers(g, nt):
                for j in range(3):
                    norm_power(g, j, nt)
                weight_power(g, nt)

            def sums_used(g):
                pool.wait_ge(attn_ready, g + 1)
                pool.nop(nofuse=True)

            def beside(g, ks):
                with pool.If(late_slabs > 0):
                    pass
                with pool.Else():
                    for k in ks:
                        v_rows_in(g + AHEAD, k)

            ends(0, GT)
            sums_used(0)
            ends(1, GT)
            powers(0, GT)
            with pool.Fori(0, SLABS - AHEAD) as g:
                beside(g, range(0, 6))
                norm_power(g + 1, 0, GT)
                beside(g, range(6, 14))
                norm_power(g + 1, 1, GT)
                norm_power(g + 1, 2, GT)
                beside(g, range(14, VS))
                weight_power(g + 1, GT)
                sums_used(g + 1)
                ends(g + 2, GT)
            for g in range(SLABS - AHEAD, TURNS1):
                powers(g + 1, GT)
                sums_used(g + 1)
                ends(g + 2, GT if g + 2 < GROUPS else 1)
            powers(GROUPS, 1)

        @block.scalar
        def _(act):
            act.wait_ge(pool_const, 7)
            for d_t, s_t in ((src_i, src), (dst_i, dst), (ews, ew)):
                v = flat(s_t[0:(P - 1) * RUN], P - 1)
                act.dma_start(d_t[0:A_SPLIT, :], v[0:A_SPLIT, :]).then_inc(edge_ld, 16)
                act.dma_start(d_t[A_SPLIT:P - 1, :], v[A_SPLIT:P - 1, :]).then_inc(edge_ld, 16)
                act.dma_start(d_t[P - 1:P, 0:TAIL], flat(s_t[(P - 1) * RUN:E], 1)).then_inc(edge_ld, 16)
            full, part = SLAB_TAIL // SR, SLAB_TAIL % SR
            act.dma_start(dst_slab[:, 0:(SLABS - 1) * SR].rearrange("p (s j) -> p s j", j=SR),
                          dst[0:(SLABS - 1) * SE].rearrange("(s p j) -> p s j", p=P, j=SR)).then_inc(edge_ld, 16)
            last_slab = dst[(SLABS - 1) * SE:E]
            act.dma_start(dst_slab[0:full, (SLABS - 1) * SR:SLABS * SR], last_slab[0:full * SR].rearrange("(p j) -> p j", j=SR)).then_inc(edge_ld, 16)
            act.dma_start(dst_slab[full:full + 1, (SLABS - 1) * SR:(SLABS - 1) * SR + part], last_slab[full * SR:SLAB_TAIL].rearrange("(p j) -> p j", p=1)).then_inc(edge_ld, 16)
            with nc.allow_non_contiguous_dma(reason="the first and last destination of each chunk, once"):
                act.dma_start(span_i[0:CHUNKS, 0:1], dst[0:(CHUNKS - 1) * EC + 1:EC].rearrange("(p o) -> p o", o=1)).then_inc(edge_ld, 16)
                act.dma_start(span_i[0:CHUNKS - 1, 1:2], dst[EC - 1:(CHUNKS - 1) * EC:EC].rearrange("(p o) -> p o", o=1)).then_inc(edge_ld, 16)
            act.dma_start(span_i[CHUNKS - 1:CHUNKS, 1:2], dst[E - 1:E].rearrange("(p o) -> p o", o=1)).then_inc(edge_ld, 16)
            act.dma_start(q_rows[ROWS:ROWS + P, :], zrow[:, :]).then_inc(pad_stored, 16)
            zw = (SLABS * SE - CE) * H // P
            assert zw <= 512
            act.dma_start(exp_rows[CE:SLABS * SE, :].rearrange("(p r) h -> p (r h)", p=P), zeros[:, 0:zw]).then_inc(zero_stored, 16)
            act.dma_start(carry_rows[SLABS * P:SLABS * P + 1, :], zeros[0:1, 0:ACC]).then_inc(zero_stored, 16)
            act.dma_start(carry_rows[0:SLABS * P, :].rearrange("(s p) a -> p s a", p=P),
                          zeros[:, 0:ACC].unsqueeze(1).to_broadcast([P, SLABS, ACC])).then_inc(zero_stored, 16)
            act.dma_start(weblk[0:ED, 0:DH], We).then_inc(edge_ld, 16)
            act.dma_start(weblk[ED:2 * ED, DH:2 * DH], We).then_inc(edge_ld, 16)

            act.wait_ge(bias_ps, 1)
            nc.scalar.copy(bias_T[:, :], bank(7)[:, 0:GC + NE * HC]).then_inc(bias_done, 1)

            def qkv_group(g, nt):
                act.wait_ge(xT_ps, g + 1)
                nc.scalar.copy(xT[:, :, 0:nt * P].rearrange("p k (t n) -> p t k n", n=P),
                               bank(0, 2)[:, 0:nt * 2 * P].rearrange("p (t k n) -> p t k n", k=2, n=P)).then_inc(xT_ready, 1)
                for t in range(nt):
                    n = g * GT + t
                    act.wait_ge(qkv_ready, n + 1)
                    for j, rows_t in enumerate((q_rows, k_rows, v_rows)):
                        act.dma_start(rows_t[bass.ds(n * P, P), :], qkv[:, t % 2, j * D:(j + 1) * D]).then_inc(qkv_stored[t % 2], 16)

            with act.Fori(0, GROUPS) as g:
                qkv_group(g, GT)
            qkv_group(GROUPS, 1)

            act.wait_ge(path_known, 1)
            slow = act.value_load(slow_i[0:1, 0:1], min_val=0, max_val=CHUNKS)
            with act.If(slow > 0):
                with act.Fori(0, CHUNKS // 2) as i:
                    for par in range(2):
                        c = 2 * i + par
                        act.wait_ge(efT_ps, c + 1)
                        nc.scalar.copy(efT[:, par, :], bank(par)).then_inc(efT_ready, 1)

            with act.Else():
                with act.Fori(0, CHUNKS // 2) as i:
                    for par in range(2):
                        c = 2 * i + par
                        act.wait_ge(efT_ps, c + 1)
                        nc.scalar.copy(efT[:, par, :], bank(7)).then_inc(efT_ready, 1)

            act.wait_ge(exp_in, 1)
            nc.scalar.activation(S, S, ACT.Exp).then_inc(exp_done, 1)
            act.wait_ge(exp_done, 1)
            act.dma_start(exp_rows[0:CE, :].rearrange("(p r) h -> p (r h)", p=P), S).then_inc(exp_stored, 16)
            act.wait_ge(exp_stored, 16)
            for e in range(NE):
                act.dma_start(m1_sb[:, e, :, :], M1[e, :, :].rearrange("(k p) n -> p k n", p=P)).then_inc(w_ld, 16)
                act.dma_start(m2_sb[:, e, :, :], M2[e, :, :].rearrange("(c p) n -> p c n", p=P)).then_inc(w_ld, 16)

            count = Chain(act, h_ready)

            def gelus(chunks, nt, first_bias, dest):
                for j in range(chunks):
                    act.wait_ge(h_ps, count.base + count.n + 1)
                    b = count.n % 2
                    count.step(nc.scalar.activation(dest[:, j, 0:nt * P], bank(b)[:, 0:nt * P], ACT.Gelu,
                                                    bias=bias_T[:, first_bias + j:first_bias + j + 1]))

            def copy_T(k, g, nt, dest):
                act.wait_ge(t_ps, 3 * g + k + 1)
                nc.scalar.copy(dest[:, :, 0:nt * P].rearrange("p k (t n) -> p t k n", n=P),
                               bank(4, 2)[:, 0:nt * 2 * P].rearrange("p (t k n) -> p t k n", k=2, n=P)).then_inc(t_ready, 1)

            def copy_wT(g, nt):
                act.wait_ge(wT_ps, g + 1)
                nc.scalar.copy(wT[:, 0:nt * P], bank(7)[0:NE, 0:nt * P]).then_inc(wT_ready, 1)

            def prepare(g, nt):
                copy_T(0, g, nt, xT)
                copy_T(1, g, nt, xT)
                gelus(GC, nt, 0, hidg)
                copy_T(2, g, nt, x3T)

            def group(g, nt, ahead):
                def moe(e):
                    gelus(HC, nt, GC + e * HC, hid[e % 2])

                moe(0)
                copy_wT(g, nt)
                moe(1)
                moe(2)
                if ahead:
                    copy_T(0, g + 1, ahead, xT)
                moe(3)
                moe(4)
                if ahead:
                    copy_T(1, g + 1, ahead, xT)
                moe(5)
                if ahead:
                    gelus(GC, ahead, 0, hidg)
                moe(6)
                moe(7)
                if ahead:
                    copy_T(2, g + 1, ahead, x3T)

            prepare(0, GT)
            with act.Fori(0, TURNS1) as g:
                count.enter(g, NE * HC + GC)
                group(g, GT, GT)
            count.leave(TURNS1)
            group(TURNS1, GT, 1)
            group(GROUPS, 1, 0)

        @block.tensor
        def _(pe):
            def transposes(src_t, nt, first_bank):
                for t in range(nt):
                    for k in range(2):
                        last = nc.tensor.transpose(ps[:, first_bank * 512 + (2 * t + k) * P:first_bank * 512 + (2 * t + k + 1) * P],
                                                   src_t[:, t, k * P:(k + 1) * P], ident[:, :])
                return last

            pe.wait_ge(pool_steps, 9)
            pe.wait_ge(const_ld, 16 * N_CONST)
            nb = GC + NE * HC
            nc.tensor.transpose(bank(7)[:, 0:nb], bias_raw[:, :], ident[0:nb, 0:nb]).then_inc(bias_ps, 1)

            def qkv_group(g, nt):
                pe.wait_ge(xn_ready, g + 1)
                transposes(xn, nt, 0).then_inc(xT_ps, 1)
                pe.wait_ge(xT_ready, g + 1)
                for t in range(nt):
                    n = g * GT + t
                    if not (isinstance(g, int) and g == 0 and t < 2):
                        pe.wait_ge(qkv_ready, n - 1)
                    o_ = (2 + 2 * (t % 2)) * 512
                    for c0, c1 in ((0, 512), (512, 3 * D)):
                        for k in range(2):
                            last = nc.tensor.matmul(ps[:, o_ + c0:o_ + c1], xT[:, k, t * P:(t + 1) * P], wqkv[:, k, c0:c1],
                                                    start=k == 0, stop=k == 1)
                    last.then_inc(qkv_ps, 1)

            qkv_group(0, GT)
            with pe.Fori(1, GROUPS) as g:
                qkv_group(g, GT)
            qkv_group(GROUPS, 1)

            pe.wait_ge(wide_ready, 1)
            nc.tensor.matmul(bank(7)[0:1, 0:1], span[:, 0:1], ones[0:CHUNKS, 0:1], start=True, stop=True).then_inc(wide_ps, 1)

            pe.wait_ge(path_known, 1)
            pe.wait_ge(edges_ready, 1)
            pe.wait_ge(qkv_ready, TILES)
            nc.tensor.matmul(bank(4)[0:TILES, 0:P], hits_hi[:, 0, :], hits_lo[:, 0, :], start=True, stop=False,
                             skip_group_check=True).then_inc(hits_used, 1)

            slow = pe.value_load(slow_i[0:1, 0:1], min_val=0, max_val=CHUNKS)
            with pe.If(slow > 0):
                def ef_transposes(c, i, par):
                    pe.wait_ge(ef_ld[par], 48 * (i + 1))
                    for j in range(CH // 2):
                        last = nc.tensor.transpose(bank(par)[:, j * P:(j + 1) * P], efb[:, par, j * P:(j + 1) * P], ident[:, :])
                    last.then_inc(efT_ps, 1)

                def chunk(i, par, ahead, first=False):
                    c = 2 * i + par
                    if ahead:
                        ef_transposes(c + 1, i + par, 1 - par)
                    pe.wait_ge(efT_ready, c + 1)
                    pe.wait_ge(scores_done, c + 1)
                    for j in range(CH // 2):
                        last = nc.tensor.matmul(bank(2 + par)[:, 2 * j * DH:2 * (j + 1) * DH], efT[:, par, j * P:(j + 1) * P], weblk[:, :],
                                                start=True, stop=True)
                    last.then_inc(ep_ready, 1)
                    pe.wait_ge(hits_ready, c + 1)
                    for j in range(CH):
                        last = nc.tensor.matmul(bank(4)[0:TILES, 0:P], hits_hi[:, j, :], hits_lo[:, j, :], start=False,
                                                stop=False, skip_group_check=True)
                    last.then_inc(hits_used, 1)

                ef_transposes(0, 0, 0)
                with pe.Fori(0, CHUNKS // 2 - 1) as i:
                    chunk(i, 0, True)
                    chunk(i, 1, True)
                chunk(CHUNKS // 2 - 1, 0, True)
                chunk(CHUNKS // 2 - 1, 1, False)

            with pe.Else():
                def features_across(c, i, par):
                    pe.wait_ge(ef_ld[par], 16 * (i + 1))
                    for j in range(CH // 2):
                        last = nc.tensor.transpose(bank(7)[:, j * P:(j + 1) * P], efb[:, par, j * P:(j + 1) * P], ident[:, :])
                    last.then_inc(efT_ps, 1)

                def window_chunk(i, par, ahead):
                    c = 2 * i + par
                    pe.wait_ge(efT_ready, c + 1)
                    if ahead:
                        features_across(c + 1, i + par, 1 - par)
                    pe.wait_ge(scores_done, c + 1)
                    for j in range(CH // 2):
                        last = nc.tensor.matmul(bank(5 + par)[:, 2 * j * DH:2 * (j + 1) * DH], efT[:, par, j * P:(j + 1) * P], weblk[:, :], start=True, stop=True)
                    last.then_inc(ep_ready, 1)
                    pe.wait_ge(hot_ready, c + 1)
                    pe.wait_ge(qwin_ld[par], 16 * (i + 1))
                    for half_ in range(2):
                        pe.wait_ge(q_used, 2 * c + half_ + 1)
                        for j in range(CH // 2):
                            t = half_ * (CH // 2) + j
                            last = nc.tensor.matmul(bank(2 * half_, 2)[:, j * D:(j + 1) * D], win_hot[par].rearrange("n (p j) -> n j p", j=CH)[:, t, :],
                                                    q_win[par], start=True, stop=True)
                        last.then_inc(q_ps, 1)
                    pe.wait_ge(hits_ready, c + 1)
                    for j in range(CH):
                        last = nc.tensor.matmul(bank(4)[0:TILES, 0:P], hits_hi[:, j, :], hits_lo[:, j, :], start=False,
                                                stop=False, skip_group_check=True)
                    last.then_inc(hits_used, 1)

                features_across(0, 0, 0)
                with pe.Fori(0, CHUNKS // 2 - 1) as i:
                    window_chunk(i, 0, True)
                    window_chunk(i, 1, True)
                window_chunk(CHUNKS // 2 - 1, 0, True)
                window_chunk(CHUNKS // 2 - 1, 1, False)

            pe.wait_ge(diag_ready, 1)
            for r in range(2 + 2 * H):
                last = nc.tensor.matmul(ps[:, r * P:(r + 1) * P], ones[:, :], arena[:, 3 * SC + r * P:3 * SC + (r + 1) * P],
                                        start=True, stop=True)
            last.then_inc(small_ps, 1)
            nc.tensor.matmul(bank(5)[0:TILES, 0:1], tri[0:TILES, 0:TILES], tots[:, P - 1:P], start=True, stop=True).then_inc(small_ps, 1)
            pe.wait_ge(diag_ready, 2)
            nc.tensor.transpose(bank(6)[:, 0:TILES], tots[:, :], ident[0:TILES, 0:TILES])
            nc.tensor.transpose(bank(6)[:, P:P + TILES], hist[:, :], ident[0:TILES, 0:TILES]).then_inc(small_ps, 1)

            count = Chain(pe, h_ps)

            def hidden(chunks, nt, weights, xt):
                for j in range(chunks):
                    if not (isinstance(count.base, int) and count.base + count.n < 2):
                        pe.wait_ge(h_ready, count.base + count.n - 1)
                    b = count.n % 2
                    for k in range(2):
                        last = nc.tensor.matmul(bank(b)[:, 0:nt * P], weights(k, j), xt[:, k, 0:nt * P], start=k == 0, stop=k == 1)
                    count.step(last)

            def first_nodes(n):
                pe.wait_ge(row_ready, n + 1)
                nc.tensor.matmul(bank(7)[:, 0:P], ones[:, :], row_diag, start=True, stop=True).then_inc(row_ps, 1)

            def carries(n):
                pe.wait_ge(masks_ready, n + 1)
                nc.tensor.matmul(bank(7)[:, P:P + ACC], mask_in, sums[:, 1, VC - 1, :], start=True, stop=False)
                nc.tensor.matmul(bank(7)[:, P:P + ACC], mask_over, totals[:, :], start=False, stop=True).then_inc(carry_ps, 1)

            def beside(g, product):
                with pe.If(late_slabs > 0):
                    pass
                with pe.Else():
                    product(g + AHEAD)

            def T(k, g, nt, ready, src_t):
                pe.wait_ge(ready, g + 1)
                transposes(src_t, nt, 4).then_inc(t_ps, 1)

            def project(g, nt):
                pe.wait_ge(t_ready, 3 * g + 1)
                for t in range(nt):
                    for k in range(2):
                        last = nc.tensor.matmul(bank(4, 2)[:, t * D:(t + 1) * D], xT[:, k, t * P:(t + 1) * P], wo[:, k, :],
                                                start=k == 0, stop=k == 1)
                last.then_inc(o_ps, 1)

            def feed(g, nt):
                pe.wait_ge(t_ready, 3 * g + 2)
                hidden(GC, nt, lambda k, j: w1[:, k, j * P:(j + 1) * P], xT)

            def feed2(g, nt):
                pe.wait_ge(h_ready, count.base + feed_end[0])
                for t in range(nt):
                    for j in range(GC):
                        last = nc.tensor.matmul(bank(4, 2)[:, t * D:(t + 1) * D], hidg[:, j, t * P:(t + 1) * P], w2[:, j, :],
                                                start=j == 0, stop=j == GC - 1)
                last.then_inc(f_ps, 1)

            feed_end = [0]

            def route(g, nt):
                T(2, g, nt, x3_ready, xn)
                pe.wait_ge(t_ready, 3 * g + 3)
                for t in range(nt):
                    for k in range(2):
                        last = nc.tensor.matmul(bank(6)[:, t * NE:(t + 1) * NE], x3T[:, k, t * P:(t + 1) * P], wr[:, k, :],
                                                start=k == 0, stop=k == 1)
                last.then_inc(r_ps, 1)

            def group(g, nt, ahead, with_slab=False):
                ends_at = {}

                def m1(e):
                    hidden(HC, nt, lambda k, j: m1_sb[:, e, k, j * P:(j + 1) * P], x3T)
                    ends_at[e] = count.n

                def m2(e):
                    pe.wait_ge(h_ready, count.base + ends_at[e])
                    pe.wait_ge(y_done, g * NE + e + 1)
                    for t in range(nt):
                        for j in range(HC):
                            last = nc.tensor.matmul(bank(2, 2)[:, t * D:(t + 1) * D], hid[e % 2][:, j, t * P:(t + 1) * P],
                                                    m2_sb[:, e, j, :], start=j == 0, stop=j == HC - 1)
                    last.then_inc(y_ps, 1)

                m1(0)
                pe.wait_ge(w_ready, g + 1)
                for t in range(nt):
                    last = nc.tensor.transpose(bank(7)[0:NE, t * P:(t + 1) * P], wmix[:, t, :], ident[:, :])
                last.then_inc(wT_ps, 1)
                m1(1)
                pe.wait_ge(wT_ready, g + 1)
                for t in range(nt):
                    last = nc.tensor.matmul(bank(4, 2)[:, t * D:(t + 1) * D], wT[:, t * P:(t + 1) * P], mb2_sb[:, :], start=True, stop=True)
                last.then_inc(b_ps, 1)
                m2(0)
                m1(2)
                m2(1)
                if ahead:
                    T(0, g + 1, ahead, attn_ready, attn)
                m1(3)
                m2(2)
                if ahead:
                    project(g + 1, ahead)
                m1(4)
                m2(3)
                if ahead:
                    T(1, g + 1, ahead, x1_ready, xn)
                m1(5)
                m2(4)
                if with_slab:
                    beside(g, first_nodes)
                if ahead:
                    feed(g + 1, ahead)
                    feed_end[0] = count.n
                m1(6)
                m2(5)
                if ahead:
                    feed2(g + 1, ahead)
                m1(7)
                m2(6)
                m2(7)
                if with_slab:
                    beside(g, carries)
                if ahead:
                    route(g + 1, ahead)

            pe.wait_ge(late_ready, 1)
            nc.tensor.matmul(bank(7)[0:1, 0:1], late_max[:, :], ones[:, 0:1], start=True, stop=True).then_inc(late_ps, 1)
            with pe.Fori(0, AHEAD) as n:
                first_nodes(n)
                carries(n)
            pe.wait_ge(late_known, 1)
            late_slabs = pe.value_load(late_i[0:1, 0:1], min_val=0, max_val=P)
            with pe.If(late_slabs > 0):
                with pe.Fori(AHEAD, SLABS) as n:
                    first_nodes(n)
                    carries(n)
            T(0, 0, GT, attn_ready, attn)
            project(0, GT)
            T(1, 0, GT, x1_ready, xn)
            feed(0, GT)
            feed_end[0] = count.n
            feed2(0, GT)
            route(0, GT)
            pe.wait_ge(w_ld, 16 * 2 * NE)
            with pe.Fori(0, SLABS - AHEAD) as g:
                count.enter(g, NE * HC + GC)
                group(g, GT, GT, True)
            count.leave(SLABS - AHEAD)
            for g in range(SLABS - AHEAD, TURNS1):
                group(g, GT, GT)
            group(TURNS1, GT, 1)
            group(GROUPS, 1, 0)

        @block.vector
        def _(dve):
            steps = Chain(dve, dve_steps)
            link, step = steps.link, steps.step
            norms = Chain(dve, var_ready)

            dve.wait_ge(const_ld, 16 * N_CONST)
            dve.wait_ge(pool_steps, 9)
            link(nc.vector.tensor_tensor(bqkv[:, D:2 * D].rearrange("p (h d) -> p h d", h=H), bqkv[:, D:2 * D].rearrange("p (h d) -> p h d", h=H),
                                         beb[:, :].unsqueeze(1).to_broadcast([P, H, DH]), ALU.add))
            dve.sem_inc(scores_done, 2)
            dve.sem_inc(v_used, 2)
            dve.sem_inc(y_done, 1)

            def norm(src_t, nt):
                for t in range(nt):
                    step(nc.vector.bn_stats(st[:, t, :], src_t[:, t, :]))
                steps.wait(hold=True)
                for t in range(nt):
                    step(nc.vector.bn_aggr(mv[:, t, :], st[:, t, :]))
                steps.wait()
                norms.step(nc.vector.tensor_scalar(ve[:, 0:nt], mv[:, 0:nt, 1], EPS, None, ALU.add))
                dve.wait_ge(rstd_ready, norms.base + norms.n)

            def scale_rows(dst_t, src_t, nt, signal=None):
                for t in range(nt):
                    ins = nc.vector.tensor_scalar(dst_t[:, t, :], src_t[:, t, :], mv[:, t, 0:1], rs[:, t:t + 1], ALU.subtract, ALU.mult)
                    if signal and t == nt - 1:
                        ins.then_inc(signal, 1)
                    else:
                        step(ins)
                steps.wait()

            def affine(t_, nt, ln, signal=None):
                link(nc.vector.tensor_tensor(t_[:, 0:nt, :], t_[:, 0:nt, :], ln[:, 0:1, :].to_broadcast([P, nt, D]), ALU.mult))
                ins = nc.vector.tensor_tensor(t_[:, 0:nt, :], t_[:, 0:nt, :], ln[:, 1:2, :].to_broadcast([P, nt, D]), ALU.add)
                if signal:
                    ins.then_inc(signal, 1)
                else:
                    link(ins)

            def group_norms(g, nt):
                dve.wait_ge(x_ld, 16 * (g + 1))
                norm(xb, nt)
                if not (isinstance(g, int) and g == 0):
                    dve.wait_ge(h0_stored, 16 * g)
                scale_rows(h0, xb, nt, h0_ready)
                dve.wait_ge(h0_ready, g + 1)
                norm(h0, nt)
                if not (isinstance(g, int) and g == 0):
                    dve.wait_ge(xT_ps, g)
                scale_rows(xn, h0, nt)
                affine(xn, nt, ln1, xn_ready)

            def group_qkv(g, nt):
                for t in range(nt):
                    n = g * GT + t
                    dve.wait_ge(qkv_ps, n + 1)
                    if not (isinstance(g, int) and g == 0 and t < 2):
                        dve.wait_ge(qkv_stored[t % 2], 3 * 16 * (g * (GT // 2) + t // 2))
                    o_ = (2 + 2 * (t % 2)) * 512
                    nc.vector.tensor_tensor(qkv[:, t % 2, :], ps[:, o_:o_ + 3 * D], bqkv[:, :], ALU.add).then_inc(qkv_ready, 1)

            group_norms(0, GT)
            group_norms(1, GT)
            group_qkv(0, GT)
            with dve.Fori(1, GROUPS - 1) as g:
                steps.enter(g - 1, 24)
                norms.enter(g - 1, 2)
                group_norms(g + 1, GT)
                group_qkv(g, GT)
            steps.leave(GROUPS - 2)
            norms.leave(GROUPS - 2)
            group_norms(GROUPS, 1)
            group_qkv(GROUPS - 1, GT)
            group_qkv(GROUPS, 1)

            dve.wait_ge(edge_ld, 16 * N_EDGE)
            step(nc.vector.tensor_copy(dstf[:, :], dst_i[:, :]))
            step(nc.vector.tensor_scalar(Fm[:, 0:RUN].bitcast(i32), dst_i[:, :], 7, None, ALU.arith_shift_right))
            step(nc.vector.tensor_scalar(Fm[:, RUN:2 * RUN].bitcast(i32), dst_i[:, :], P - 1, None, ALU.bitwise_and))
            step(nc.vector.tensor_scalar(ews[:, :], ews[:, :], DH ** -0.5, None, ALU.mult))
            steps.wait()
            step(nc.vector.tensor_copy(dhi[:, :], Fm[:, 0:RUN].bitcast(i32)))
            step(nc.vector.tensor_copy(dlo[:, :], Fm[:, RUN:2 * RUN].bitcast(i32)))
            step(nc.vector.memset(cut[:, 0:1], 1.0))
            step(nc.vector.memset(cut[:, RUN:RUN + 1], 1.0))
            step(nc.vector.tensor_tensor(cut[:, 1:RUN], dstf[:, 1:RUN], dstf[:, 0:RUN - 1], ALU.not_equal))
            ds3 = dst_slab.rearrange("p (s j) -> p s j", j=SR)
            step(nc.vector.memset(keep[:, :, 0:1], 0.0))
            step(nc.vector.tensor_tensor(keep[:, :, 1:SR], ds3[:, :, 1:SR], ds3[:, :, 0:SR - 1], ALU.is_equal))
            step(nc.vector.tensor_copy(bounds[:, :, 0], ds3[:, :, 0]))
            step(nc.vector.tensor_copy(bounds[:, :, 1], ds3[:, :, SR - 1]))
            step(nc.vector.tensor_scalar(last_part[:, :], iota_col[:, :], float(P - 1), None, ALU.is_equal))
            step(nc.vector.memset(bounds[:, 0:1, 2], -1.0))
            step(nc.vector.memset(totals[:, :], 0.0))
            step(nc.vector.memset(hits_hi[:, 0, :], 0.0))
            step(nc.vector.memset(hits_lo[:, 0, :], 0.0))
            steps.wait()
            link(nc.vector.tensor_scalar(bounds[:, 1:SLABS, 2], bounds[:, 0:SLABS - 1, 1], 1.0, last_part[:, 0:1], ALU.add, ALU.mult))
            link(nc.vector.tensor_scalar(bounds[:, 1:SLABS, 2], bounds[:, 1:SLABS, 2], -1.0, None, ALU.add))
            step(nc.vector.tensor_scalar(cut[:, :], cut[:, :], -BIG, None, ALU.mult))
            nc.vector.tensor_scalar(dst_i[:, :], dst_i[:, :], float(N - 1), None, ALU.min).then_inc(edges_ready, 1)

            step(nc.vector.tensor_copy(span[:, :], span_i[:, :]))
            steps.wait()
            link(nc.vector.tensor_tensor(span[:, 0:1], span[:, 1:2], span[:, 0:1], ALU.subtract))
            nc.vector.tensor_scalar(span[:, 0:1], span[:, 0:1], float(P), None, ALU.is_ge).then_inc(wide_ready, 1)
            dve.wait_ge(wide_ps, 1)
            nc.vector.tensor_copy(slow_i[:, :], bank(7)[0:1, 0:1]).then_inc(path_known, 1)
            dve.wait_ge(path_known, 1)
            slow = dve.value_load(slow_i[0:1, 0:1], min_val=0, max_val=CHUNKS)

            before_paths = (steps.base, steps.n)
            with dve.If(slow > 0):
                with dve.Fori(0, CHUNKS // 2) as i:
                    steps.enter(i, 6)
                    for par in range(2):
                        c = 2 * i + par
                        dve.wait_ge(hits_used, c + 1)
                        step(nc.vector.tensor_tensor(hits_hi[:, :, :], iota49.unsqueeze(1).to_broadcast([P, CH, TILES]),
                                                     dhi[:, bass.ds(c * CH, CH)].unsqueeze(2).to_broadcast([P, CH, TILES]), ALU.is_equal))
                        nc.vector.tensor_tensor(hits_lo[:, :, :], iota[:, :].unsqueeze(1).to_broadcast([P, CH, P]),
                                                dlo[:, bass.ds(c * CH, CH)].unsqueeze(2).to_broadcast([P, CH, P]), ALU.is_equal).then_inc(hits_ready, 1)
                        k4 = k_ring[par].rearrange("p (t h d) -> p t h d", t=CH, h=H)
                        dve.wait_ge(rows_in[par], 16 * 2 * CH * (i + 1))
                        dve.wait_ge(ep_ready, c + 1)
                        link(nc.vector.tensor_tensor(k4, k4, bank(2 + par)[:, 0:CH * DH].rearrange("p (t d) -> p t d", t=CH).unsqueeze(2)
                                                     .to_broadcast([P, CH, H, DH]), ALU.add))
                        link(nc.vector.tensor_tensor(k_ring[par], k_ring[par], q_ring[par], ALU.mult))
                        nc.vector.tensor_reduce(S[:, bass.ds(c * (CH * H), CH * H)], k_ring[par].rearrange("p (a d) -> p a d", d=DH),
                                                AX.X, ALU.add).then_inc(scores_done, 1)
                steps.leave(CHUNKS // 2)

                after_slow = steps.base + steps.n
                if FAST_MORE > 0:
                    dve.sem_inc(dve_steps, FAST_MORE)
            steps.base, steps.n = before_paths
            with dve.Else():
                def hot(c, i, par):
                    dve.wait_ge(dstrow_ld[par], 16 * (i + 1))
                    link(nc.vector.tensor_tensor(win_id[:, par:par + 1], dst_row[par][:, 0:1], iota_col[:, :], ALU.add))
                    nc.vector.tensor_scalar(win_hot[par], dst_row[par], win_id[:, par:par + 1], None, ALU.is_equal).then_inc(hot_ready, 1)
                    dve.wait_ge(hits_used, c + 1)
                    step(nc.vector.tensor_tensor(hits_hi[:, :, :], iota49.unsqueeze(1).to_broadcast([P, CH, TILES]),
                                                 dhi[:, bass.ds(c * CH, CH)].unsqueeze(2).to_broadcast([P, CH, TILES]), ALU.is_equal))
                    nc.vector.tensor_tensor(hits_lo[:, :, :], iota[:, :].unsqueeze(1).to_broadcast([P, CH, P]),
                                            dlo[:, bass.ds(c * CH, CH)].unsqueeze(2).to_broadcast([P, CH, P]), ALU.is_equal).then_inc(hits_ready, 1)

                def multiply(i, par):
                    c = 2 * i + par
                    k4 = k_ring[par].rearrange("p (t h d) -> p t h d", t=CH, h=H)
                    hw = CH * D // 2
                    dve.wait_ge(rows_in[par], 16 * CH * (i + 1))
                    dve.wait_ge(ep_ready, c + 1)
                    link(nc.vector.tensor_tensor(k4, k4, bank(5 + par)[:, 0:CH * DH].rearrange("p (t d) -> p t d", t=CH).unsqueeze(2)
                                                 .to_broadcast([P, CH, H, DH]), ALU.add))
                    for half_ in range(2):
                        dve.wait_ge(q_ps, 2 * c + half_ + 1)
                        kh = k_ring[par][:, half_ * hw:(half_ + 1) * hw]
                        nc.vector.tensor_tensor(kh, kh, bank(2 * half_, 2), ALU.mult).then_inc(q_used, 1)
                    dve.wait_ge(q_used, 2 * c + 4)
                    dve.wait_ge(score_out[par], 16 * (i + 1))
                    nc.vector.tensor_reduce(sc_out[par], k_ring[par].rearrange("p (a d) -> p a d", d=DH), AX.X, ALU.add).then_inc(scores_done, 1)

                dve.sem_inc(q_used, 2)
                for par in range(2):
                    dve.sem_inc(score_out[par], 16)
                hot(0, 0, 0)
                with dve.Fori(0, CHUNKS // 2 - 1) as i:
                    steps.enter(i, 6)
                    hot(2 * i + 1, i, 1)
                    multiply(i, 0)
                    hot(2 * i + 2, i + 1, 0)
                    multiply(i, 1)
                steps.leave(CHUNKS // 2 - 1)
                i_last = CHUNKS // 2 - 1
                hot(CHUNKS - 1, i_last, 1)
                multiply(i_last, 0)
                multiply(i_last, 1)
                dve.wait_ge(score_in, 16)
            assert steps.base + steps.n == after_slow + FAST_MORE, (steps.base + steps.n - after_slow)

            dve.wait_ge(hits_used, CHUNKS + 1)
            link(nc.vector.tensor_copy(hist[:, :], bank(4)[0:TILES, 0:P]))
            link(nc.vector.tensor_tensor_scan(tots[:, :], ones[0:TILES, :], hist[:, :], 0.0, ALU.mult, ALU.add))

            S3 = S.rearrange("p (t h) -> p t h", h=H)
            F3 = Fm.rearrange("p (t h) -> p t h", h=H)
            M3 = Mm.rearrange("p (t h) -> p t h", h=H)
            dve.wait_ge(scores_done, CHUNKS + 2)
            link(nc.vector.tensor_tensor(S3, S3, ews[:, :].unsqueeze(2).to_broadcast([P, RUN, H]), ALU.mult))
            for h in range(H):
                step(nc.vector.tensor_tensor_scan(F3[:, :, h], cut[:, 0:RUN], S3[:, :, h], -BIG, ALU.add, ALU.max))
            steps.wait()
            for h in range(H):
                step(nc.vector.tensor_tensor_scan(M3[:, ::-1, h], cut[:, RUN:0:-1], F3[:, ::-1, h], -BIG, ALU.add, ALU.max))
            steps.wait()
            step(nc.vector.tensor_copy(small[:, 0:1], dstf[:, 0:1]))
            step(nc.vector.tensor_copy(small[:, 1:2], dstf[:, RUN - 1:RUN]))
            step(nc.vector.tensor_copy(small[:, 2:2 + H], M3[:, 0, :]))
            step(nc.vector.tensor_copy(small[:, 2 + H:2 + 2 * H], M3[:, RUN - 1, :]))
            steps.wait()
            nr = 2 + 2 * H
            diag = arena[:, 3 * SC:3 * SC + nr * P]
            nc.vector.tensor_tensor(diag.rearrange("p (r n) -> p r n", r=nr), ident[:, :].unsqueeze(1).to_broadcast([P, nr, P]),
                                    small[:, :].unsqueeze(2).to_broadcast([P, nr, P]), ALU.mult).then_inc(diag_ready, 1)
            dve.wait_ge(small_ps, 1)
            pen = sums[:, 0, 0:2, 0:P]
            for f in range(2):
                link(nc.vector.tensor_scalar(pen, ps[:, 0:2 * P].rearrange("p (s n) -> p s n", s=2), small[:, f:f + 1], BIG, ALU.is_equal, ALU.mult))
                link(nc.vector.tensor_scalar(pen, pen, -BIG, None, ALU.add))
                cand = Fm[:, 0:2 * H * P].rearrange("p (s h n) -> p s h n", s=2, h=H)
                link(nc.vector.tensor_tensor(cand, ps[:, 2 * P:nr * P].rearrange("p (s h n) -> p s h n", s=2, h=H),
                                             pen.unsqueeze(2).to_broadcast([P, 2, H, P]), ALU.add))
                link(nc.vector.tensor_reduce(gmax[:, f, :], cand.rearrange("p s h n -> p h s n"), AX.XY, ALU.max))
            for f in range(2):
                mask = Fm[:, f * RUN:(f + 1) * RUN]
                link(nc.vector.tensor_scalar(mask, dstf[:, :], small[:, f:f + 1], BIG, ALU.is_equal, ALU.mult))
                link(nc.vector.tensor_scalar(mask, mask, -BIG, None, ALU.add))
                for h in range(H):
                    step(nc.vector.scalar_tensor_tensor(M3[:, :, h], mask, gmax[:, f, h:h + 1], M3[:, :, h], ALU.add, ALU.max))
                steps.wait()
            nc.vector.tensor_tensor(S, S, Mm, ALU.subtract).then_inc(exp_in, 1)

            dve.wait_ge(small_ps, 2)
            step(nc.vector.tensor_copy(small[0:TILES, 0:1], bank(5)[0:TILES, 0:1]))
            steps.wait()
            nc.vector.tensor_scalar(tots[:, :], tots[:, :], small[0:TILES, 0:1], -1.0, ALU.add, ALU.add).then_inc(diag_ready, 1)
            dve.wait_ge(small_ps, 3)
            step(nc.vector.tensor_scalar(end_i[:, 0:TILES], bank(6)[:, 0:TILES], 0.0, None, ALU.max))
            step(nc.vector.tensor_scalar(has[:, 0:TILES], bank(6)[:, P:P + TILES], 0.0, None, ALU.is_gt))
            step(nc.vector.memset(late[:, :], 0.0))
            steps.wait()
            for g in range(SLABS - 2):
                step(nc.vector.tensor_scalar(late[:, g * GT:(g + 1) * GT], bank(6)[:, g * GT:(g + 1) * GT], float((g + 2) * SE), None, ALU.is_ge))
            steps.wait()
            for g in range(2, GROUPS + 1):
                t0, t1 = g * GT, min((g + 1) * GT, TILES)
                step(nc.vector.scalar_tensor_tensor(late[:, t0:t1], bank(6)[:, t0:t1], float((g - 1) * SE), late[:, t0:t1], ALU.is_lt, ALU.add))
            number = [sums[:, 0, 0, j * TILES:(j + 1) * TILES] for j in range(3)]
            step(nc.vector.tensor_scalar(number[2].bitcast(i32), end_i[:, 0:TILES], 6, None, ALU.arith_shift_right))
            assert SR == 1 << 6
            ringf = sums[:, 0, 1, 0:TILES]
            link(nc.vector.tensor_copy(ringf, end_i[:, 0:TILES]))
            turn_ = sums[:, 0, 2, 0:TILES]
            step(nc.vector.tensor_scalar(turn_, ringf, float(AHEAD * SE), None, ALU.is_ge))
            for m in range(2, -(-E // (AHEAD * SE))):
                steps.wait()
                step(nc.vector.scalar_tensor_tensor(turn_, ringf, float(m * AHEAD * SE), turn_, ALU.is_ge, ALU.add))
            steps.wait()
            nc.vector.scalar_tensor_tensor(ring_i[:, 0:TILES], turn_, -float(AHEAD * SE), ringf, ALU.mult, ALU.add).then_inc(end_ready, 1)
            steps.wait()
            nc.vector.tensor_reduce(late_max[:, :], late[:, :], AX.X, ALU.max).then_inc(late_ready, 1)
            link(nc.vector.tensor_copy(number[0], number[2].bitcast(i32)))
            step(nc.vector.tensor_copy(hist_T[:, :], bank(6)[:, P:P + TILES]))
            steps.wait()
            link(nc.vector.tensor_tensor(number[1], bank(6)[:, 0:TILES], hist_T[:, :], ALU.subtract))
            link(nc.vector.scalar_tensor_tensor(number[1], number[0], -float(SR), number[1], ALU.mult, ALU.add))
            link(nc.vector.tensor_scalar(number[1], number[1], -1.0, None, ALU.is_lt))
            link(nc.vector.scalar_tensor_tensor(number[0], number[0], -float(SLABS * P), number[1], ALU.add, ALU.mult))
            nc.vector.tensor_scalar(carry_i[:, 0:TILES], number[0], float(SLABS * P), None, ALU.add).then_inc(end_ready, 1)
            link(nc.vector.memset(sums[:, 1, VC - 1, :], 0.0))
            for par in range(2):
                dve.sem_inc(run_stored[par], 16)
            dve.wait_ge(late_ps, 1)
            nc.vector.tensor_copy(late_i[:, :], bank(7)[0:1, 0:1]).then_inc(late_known, 1)
            dve.wait_ge(late_known, 1)

            def run_step(n, k):
                c, par = n * VS + k, k % 2
                new = sums[:, par, :, :]
                step(nc.vector.tensor_copy(keep_c[:, :], keep_all[:, bass.ds(n * SR + k * VC, VC)]))
                dve.wait_ge(run_stored[par], 16 * (n * (VS // 2) + k // 2 + 1))
                if k == 0:
                    dve.wait_ge(ex_ld, 16 * (n + 1))
                ex = ex_slab[:, k * (VC * H):(k + 1) * (VC * H)].rearrange("p (t h) -> p t h", h=H)
                step(nc.vector.tensor_copy(new[:, :, D:ACC], ex))
                dve.wait_ge(v_in[par], 16 * VC * (n * (VS // 2) + k // 2 + 1))
                nc.vector.tensor_tensor(new[:, :, 0:D].rearrange("p t (h d) -> p t h d", h=H),
                                        v_ring[:, par, :].rearrange("p (t h d) -> p t h d", t=VC, h=H),
                                        ex.unsqueeze(3).to_broadcast([P, VC, H, DH]), ALU.mult).then_inc(v_used, 1)
                dve.wait_ge(v_used, c + 3)
                steps.wait()
                for j in range(VC):
                    before = new[:, j - 1, :] if j else sums[:, 1 - par, VC - 1, :]
                    ins = nc.vector.scalar_tensor_tensor(new[:, j, :], before, keep_c[:, j:j + 1], new[:, j, :], ALU.mult, ALU.add)
                    if j < VC - 1:
                        link(ins)
                    else:
                        ins.then_inc(run_ready, 1)
                        dve.wait_ge(run_ready, c + 1)

            def carry_rows_ask(n):
                step(nc.vector.tensor_copy(bound_c[:, :], bounds_all[:, bass.ds(n * 3, 3)]))
                steps.wait()
                step(nc.vector.tensor_tensor(same[:, :], bound_c[:, 0:1], bound_c[:, 1:2], ALU.is_equal))
                nc.vector.tensor_scalar(row_diag, ident[:, :], bound_c[:, 0:1], None, ALU.mult).then_inc(row_ready, 1)

            def carry_masks(n):
                dve.wait_ge(row_ps, n + 1)
                link(nc.vector.tensor_scalar(mask_over, bank(7)[:, 0:P], bound_c[:, 2:3], None, ALU.is_equal))
                nc.vector.scalar_tensor_tensor(mask_in, bank(7)[:, 0:P], bound_c[:, 1:2], tri[:, :], ALU.is_equal, ALU.mult).then_inc(masks_ready, 1)

            def carry_take(n):
                dve.wait_ge(carry_ps, n + 1)
                if not (isinstance(n, int) and n == 0):
                    dve.wait_ge(carry_stored, 16 * n)
                nc.vector.tensor_copy(carry, bank(7)[:, P:P + ACC]).then_inc(carry_ready, 1)
                dve.wait_ge(carry_ready, n + 1)
                link(nc.vector.scalar_tensor_tensor(totals[:, :], carry, same[:, 0:1], sums[:, 1, VC - 1, :], ALU.mult, ALU.add))

            def slab(n):
                carry_rows_ask(n)
                for k in range(VS):
                    run_step(n, k)
                carry_masks(n)
                carry_take(n)

            slab(0)
            with dve.Fori(1, AHEAD) as n:
                steps.enter(n - 1, SLAB_STEPS)
                slab(n)
            steps.leave(AHEAD - 1)
            late_slabs = dve.value_load(late_i[0:1, 0:1], min_val=0, max_val=P)
            before_paths = (steps.base, steps.n)
            with dve.If(late_slabs > 0):
                with dve.Fori(AHEAD, SLABS) as n:
                    steps.enter(n - AHEAD, SLAB_STEPS)
                    slab(n)
                steps.leave(SLABS - AHEAD)
            with dve.Else():
                dve.sem_inc(dve_steps, (SLABS - AHEAD) * SLAB_STEPS)

            def bc(t_, nt):
                return t_.unsqueeze(1).to_broadcast([P, nt, D])

            def D1(g, nt):
                step(nc.vector.tensor_copy(has_c[:, 0:nt], has[:, bass.ds(g * GT, nt)]))
                steps.wait()
                dve.wait_ge(got_in, (g * GT + nt) * 32)
                link(nc.vector.tensor_tensor(got[:, 0:nt, :], got[:, 0:nt, :], got_carry[:, 0:nt, :], ALU.add))
                link(nc.vector.reciprocal(rec[:, 0:nt, :], got[:, 0:nt, D:ACC]))
                link(nc.vector.tensor_tensor(rec[:, 0:nt, :], rec[:, 0:nt, :], has_c[:, 0:nt].unsqueeze(2).to_broadcast([P, nt, H]), ALU.mult))
                for t in range(nt):
                    ins = nc.vector.tensor_tensor(attn[:, t, :].rearrange("p (h d) -> p h d", h=H), got[:, t, 0:D].rearrange("p (h d) -> p h d", h=H),
                                                  rec[:, t, :].unsqueeze(2).to_broadcast([P, H, DH]), ALU.mult)
                    if t < nt - 1:
                        step(ins)
                    else:
                        ins.then_inc(attn_ready, 1)

            def D2(g, nt):
                dve.wait_ge(o_ps, g + 1)
                dve.wait_ge(h0_ld, 16 * (g + 1))
                dve.wait_ge(xr_ld, 16 * (g + 1))
                op = bank(4, 2)[:, 0:nt * D].rearrange("p (t d) -> p t d", t=nt)
                link(nc.vector.tensor_tensor(attn[:, 0:nt, :], op, bc(bo_b[:, :], nt), ALU.add))
                link(nc.vector.scalar_tensor_tensor(h0[:, 0:nt, :], attn[:, 0:nt, :], ab[:, 0:1], h0[:, 0:nt, :], ALU.mult, ALU.add))
                link(nc.vector.tensor_tensor(attn[:, 0:nt, :], h0[:, 0:nt, :], xb[:, 0:nt, :], ALU.add))
                norm(h0, nt)
                scale_rows(xn, h0, nt)
                affine(xn, nt, ln2, x1_ready)

            def D3(g, nt):
                dve.wait_ge(f_ps, g + 1)
                fp = bank(4, 2)[:, 0:nt * D].rearrange("p (t d) -> p t d", t=nt)
                link(nc.vector.tensor_tensor(x2[:, 0:nt, :], fp, bc(b2_b[:, :], nt), ALU.add))
                link(nc.vector.scalar_tensor_tensor(x2[:, 0:nt, :], x2[:, 0:nt, :], ab[:, 1:2], attn[:, 0:nt, :], ALU.mult, ALU.add))
                norm(x2, nt)
                scale_rows(xn, x2, nt)
                norm(xn, nt)
                scale_rows(xn, xn, nt)
                affine(xn, nt, lnm, x3_ready)

            def D4(g, nt):
                dve.wait_ge(r_ps, g + 1)
                L, A, B, O1, O2, L2 = (lg[:, j, 0:nt, :] for j in range(6))
                m1_, m2_, df, z, t4, t5 = (tv[:, j, 0:nt] for j in range(6))

                def col(v):
                    return v.unsqueeze(2).to_broadcast([P, nt, NE])

                ib = i8[:, :].unsqueeze(1).to_broadcast([P, nt, NE])
                link(nc.vector.tensor_tensor(L, bank(6)[:, 0:nt * NE].rearrange("p (t e) -> p t e", t=nt), br_b[:, :].unsqueeze(1).to_broadcast([P, nt, NE]), ALU.add))

                def first_of_max(logits, m, one):
                    link(nc.vector.tensor_reduce(m, logits, AX.X, ALU.max))
                    link(nc.vector.tensor_tensor(A, logits, col(m), ALU.is_lt))
                    link(nc.vector.scalar_tensor_tensor(A, A, float(NE), ib, ALU.mult, ALU.add))
                    link(nc.vector.tensor_reduce(t4, A, AX.X, ALU.min))
                    link(nc.vector.tensor_tensor(one, ib, col(t4), ALU.is_equal))

                first_of_max(L, m1_, O1)
                link(nc.vector.scalar_tensor_tensor(L2, O1, -BIG, L, ALU.mult, ALU.add))
                first_of_max(L2, m2_, O2)
                norms.step(nc.vector.tensor_tensor(df, m2_, m1_, ALU.subtract))
                dve.wait_ge(rstd_ready, norms.base + norms.n)
                link(nc.vector.tensor_scalar(t4, z, 1.0, None, ALU.add))
                link(nc.vector.reciprocal(t5, t4))
                link(nc.vector.tensor_tensor(t4, z, t5, ALU.mult))
                link(nc.vector.tensor_tensor(A, O1, col(t5), ALU.mult))
                link(nc.vector.tensor_tensor(B, O2, col(t4), ALU.mult))
                nc.vector.tensor_tensor(wmix[:, 0:nt, :], A, B, ALU.add).then_inc(w_ready, 1)
                dve.wait_ge(w_ready, g + 1)

            def beside(g, ks, ask=False, masks=False, take=False):
                before = steps.n
                dve.nop(nofuse=True)
                with dve.If(late_slabs > 0):
                    dve.sem_inc(dve_steps, len(ks) * STEP_STEPS + 2 * ask + masks + take)
                with dve.Else():
                    if ask:
                        carry_rows_ask(g + AHEAD)
                    for k in ks:
                        run_step(g + AHEAD, k)
                    if masks:
                        carry_masks(g + AHEAD)
                    if take:
                        carry_take(g + AHEAD)
                    dve.nop(nofuse=True)
                assert steps.n - before == len(ks) * STEP_STEPS + 2 * ask + masks + take

            def prepare_first(nt):
                D1(0, nt)
                D2(0, nt)
                D3(0, nt)
                D4(0, nt)

            def group(g, nt, ahead, with_slab=False):
                def add(e):
                    dve.wait_ge(y_ps, g * NE + e + 1)
                    dest = yo if e == NE - 1 else y
                    base = x2 if e == 0 else y
                    if e == NE - 1:
                        dve.wait_ge(out_stored, 16 * g + 16)
                    for t in range(nt):
                        ins = nc.vector.scalar_tensor_tensor(dest[:, t, :], bank(2, 2)[:, t * D:(t + 1) * D], wmix[:, t, e:e + 1],
                                                             base[:, t, :], ALU.mult, ALU.add)
                        if t < nt - 1:
                            step(ins)
                        else:
                            ins.then_inc(y_done, 1)
                    steps.wait()
                    dve.wait_ge(y_done, g * NE + e + 2)

                dve.wait_ge(b_ps, g + 1)
                link(nc.vector.tensor_tensor(x2[:, 0:nt, :], x2[:, 0:nt, :], bank(4, 2)[:, 0:nt * D].rearrange("p (t d) -> p t d", t=nt), ALU.add))
                add(0)
                if ahead:
                    D1(g + 1, ahead)
                if with_slab:
                    beside(g, (0, 1))
                add(1)
                if with_slab:
                    beside(g, (2, 3))
                add(2)
                if ahead:
                    D2(g + 1, ahead)
                if with_slab:
                    beside(g, (4, 5), ask=True)
                add(3)
                if with_slab:
                    beside(g, (6, 7))
                add(4)
                if with_slab:
                    beside(g, (8, 9))
                add(5)
                if with_slab:
                    beside(g, (10, 11))
                if ahead:
                    D3(g + 1, ahead)
                if with_slab:
                    beside(g, (12, 13))
                add(6)
                if with_slab:
                    beside(g, (14, 15), masks=True)
                add(7)
                if with_slab:
                    beside(g, (), take=True)
                if ahead:
                    D4(g + 1, ahead)

            prepare_first(GT)
            with dve.Fori(0, SLABS - AHEAD) as g:
                steps.enter(g, 176)
                norms.enter(g, 4)
                group(g, GT, GT, True)
            steps.leave(SLABS - AHEAD)
            norms.leave(SLABS - AHEAD)
            for g in range(SLABS - AHEAD, TURNS1):
                group(g, GT, GT)
            group(TURNS1, GT, 1)
            group(GROUPS, 1, 0)


_INS = ["x", "src", "dst", "edge_attr_64", "edge_weight", "L0_gnn_Wq", "L0_gnn_bq", "L0_gnn_Wk", "L0_gnn_bk", "L0_gnn_Wv",
        "L0_gnn_bv", "L0_gnn_We", "L0_gnn_be", "L0_gnn_Wo", "L0_gnn_bo", "L0_gnn_ln1_g", "L0_gnn_ln1_b", "L0_gnn_ln2_g",
        "L0_gnn_ln2_b", "L0_gnn_W1", "L0_gnn_b1", "L0_gnn_W2", "L0_gnn_b2", "L0_gnn_alpha", "L0_gnn_beta", "L0_ffn_gamma",
        "L0_ffn_beta", "L0_ffn_Wr", "L0_ffn_br", "L0_ffn_W1", "L0_ffn_b1", "L0_ffn_W2", "L0_ffn_b2"]


def kernel(**inputs):
    import numpy as _np
    import concourse.bacc as _bacc
    from concourse import mybir as _mybir
    from concourse.bass_utils import run_bass_kernel_spmd as _run

    nc = _bacc.Bacc("TRN2", target_bir_lowering=False, num_devices=1)
    arrays, args = {}, []
    for name in _INS:
        a = _np.ascontiguousarray(inputs[name])
        arrays[f"in_{name}"] = a
        args.append(nc.dram_tensor(f"in_{name}", a.shape, _mybir.dt.from_np(a.dtype), kind="ExternalInput").ap())
    args.append(nc.dram_tensor("out_0", (N, D), _mybir.dt.float32, kind="ExternalOutput").ap())
    gnn_moe_program(nc, *args)
    return _run(nc, [arrays], core_ids=[0]).results[0]["out_0"]
```

```python
import concourse.bass as bass
from concourse import mybir
from contextlib import ExitStack

P = 128
N, D, H, ED, FF = 6250, 256, 8, 64, 1024
DH = D // H
E = 100000
NE, EH = 8, 512
EPS = 1e-5
TILES = -(-N // P)
LAST = N - (TILES - 1) * P
ROWS = TILES * P
RUN = 784
CH = 8
CHUNKS = RUN // CH
TAIL = E - (P - 1) * RUN
ACC = D + H
BIG = 1e38
PADNODE = 8191
GT = 4
GROUPS = TILES // GT
GC = FF // P
HC = EH // P
A_SPLIT = 112
EC = CH * P
CE = CHUNKS * EC
LASTP = (E - (CHUNKS - 1) * EC) // CH
VC = 4
SR = 64
SE = SR * P
SLABS = -(-E // SE)
VS = SR // VC
AHEAD = 3
FIRST = 2
EARLY_STEPS = 4 * CH // VC
SLAB_TAIL = E - (SLABS - 1) * SE
assert VS % 2 == 0 and SLABS - AHEAD < GROUPS
assert LASTP * CH == E - (CHUNKS - 1) * EC and CE == P * RUN


class Chain:

    def __init__(self, engine, sem):
        self.engine, self.sem, self.base, self.n = engine, sem, 0, 0

    def step(self, instruction):
        instruction.then_inc(self.sem, 1)
        self.n += 1

    def wait(self, hold=False):
        self.engine.wait_ge(self.sem, self.base + self.n)
        if hold:
            self.engine.nop(nofuse=True)

    def link(self, instruction):
        self.step(instruction)
        self.wait()

    def enter(self, i, per_turn):
        self.start = self.base + self.n
        self.base, self.n, self.per = self.start + i * per_turn, 0, per_turn

    def leave(self, turns):
        assert self.n == self.per, (self.n, self.per)
        self.base, self.n = self.start + turns * self.per, 0


def gnn_moe_program(nc, x, src, dst, ef, ew, Wq, bq, Wk, bk, Wv, bv, We, be, Wo, bo, g1, b1n, g2, b2n,
                    W1, b1, W2, b2, alpha, beta, gm, bm, Wr, br, M1, mb1, M2, mb2, out):
    f32, i32, bf16 = mybir.dt.float32, mybir.dt.int32, mybir.dt.bfloat16
    ALU, ACT, AX = mybir.AluOpType, mybir.ActivationFunctionType, mybir.AxisListType
    TURNS1 = GROUPS - 1

    q_rows = nc.dram_tensor("q_rows", [ROWS + P, D], f32)
    score_rows = nc.dram_tensor("score_rows", [CE, H], f32)
    k_rows = nc.dram_tensor("k_rows", [ROWS, D], f32)
    v_rows = nc.dram_tensor("v_rows", [ROWS, D], f32)
    h0_rows = nc.dram_tensor("h0_rows", [ROWS, D], f32)
    exp_rows = nc.dram_tensor("exp_rows", [SLABS * SE, H], f32)
    sum_rows = nc.dram_tensor("sum_rows", [SLABS * SE, ACC], f32)
    ring_rows = nc.dram_tensor("ring_rows", [AHEAD * SE, ACC], f32)
    carry_rows = nc.dram_tensor("carry_rows", [SLABS * P + 1, ACC], f32)

    with ExitStack() as ctx:
        def sb(name, shape, dt=f32):
            return ctx.enter_context(nc.sbuf_tensor(name, shape, dt))

        def sem(name):
            return ctx.enter_context(nc.semaphore(name))

        ident = sb("ident", [P, P])
        ones = sb("ones", [P, P])
        iota = sb("iota", [P, P])
        tri = sb("tri", [P, P])
        early = sb("early", [P, 5 * 3 * D])
        wqkv = early[:, 0:6 * D].rearrange("p (k n) -> p k n", k=2)
        qkv = early[:, 6 * D:12 * D].rearrange("p (r n) -> p r n", r=2)
        bqkv = early[:, 12 * D:15 * D]
        x2, y, yo = (early[:, j * GT * D:(j + 1) * GT * D].rearrange("p (t d) -> p t d", t=GT) for j in range(3))
        row_diag = early[:, 12 * D:12 * D + P]
        ex_second = early[:, 9 * D:9 * D + SR * H]
        assert (2 + 2 * H) * P <= 9 * D and SR * H <= 3 * D
        mask_in = early[:, 12 * D + P:12 * D + 2 * P]
        mask_over = early[:, 12 * D + 2 * P:12 * D + 3 * P]
        carry = early[:, 12 * D + 3 * P:12 * D + 3 * P + ACC]
        assert 3 * P + ACC <= 3 * D
        beb = sb("beb", [P, DH])
        ln1 = sb("ln1", [P, 2, 2])
        ln2 = sb("ln2", [P, 2, D])
        lnm = sb("lnm", [P, 2, D])
        weblk = sb("weblk", [P, 2 * DH])
        wo = sb("wo", [P, 2, D])
        bo_b = sb("bo_b", [P, D])
        b2_b = sb("b2_b", [P, D])
        ab = sb("ab", [P, 2])
        w1 = sb("w1", [P, 2, FF])
        w2 = sb("w2", [P, GC, D])
        wr = sb("wr", [P, 2, NE])
        br_b = sb("br_b", [P, NE])
        mb2_sb = sb("mb2_sb", [NE, D])
        bias_raw = sb("bias_raw", [GC + NE * HC, P])
        bias_T = sb("bias_T", [P, GC + NE * HC])
        half = sb("half", [P, GT])
        ebase = sb("ebase", [P, GT])
        i8 = sb("i8", [P, NE])

        st = sb("st", [P, GT, 6])
        mv = sb("mv", [P, GT, 2])
        ve = sb("ve", [P, GT])
        rs = sb("rs", [P, GT])

        src_all = sb("src_all", [P, SLABS * SR], i32)
        src_i = src_all[:, 0:RUN]
        assert SLABS * SR >= RUN
        gat_i = sb("gat_i", [P, 2, 2 * CH], i32)
        edges = sb("edges", [P, 4 * RUN + 1])
        dst_i = edges[:, 0:RUN].bitcast(i32)
        dstf = edges[:, RUN:2 * RUN]
        ews = edges[:, 2 * RUN:3 * RUN]
        cut = edges[:, 3 * RUN:4 * RUN + 1]
        attn = edges[:, 0:GT * D].rearrange("p (t d) -> p t d", t=GT)
        wT = edges[0:NE, GT * D:GT * D + GT * P]
        got_carry = edges[:, GT * (D + P):GT * (D + P) + GT * ACC].rearrange("p (t n) -> p t n", t=GT)
        ex_slab = edges[:, GT * (D + P + ACC):GT * (D + P + ACC) + SR * H]
        assert GT * (D + P + ACC) + SR * H <= 4 * RUN + 1
        keep = sb("keep", [P, SLABS, SR])
        keep_c = sb("keep_c", [P, VC])
        keep_all = keep[:, :, :].rearrange("p s j -> p (s j)")
        bounds = sb("bounds", [P, SLABS, 3])
        bounds_all = bounds[:, :, :].rearrange("p s j -> p (s j)")
        bound_c = sb("bound_c", [P, 3])
        same = sb("same", [P, 1])
        last_part = sb("last_part", [P, 1])
        late = sb("late", [P, TILES])
        hist_T = sb("hist_T", [P, TILES])
        late_max = sb("late_max", [P, 1])
        late_i = sb("late_i", [1, 1], i32)
        totals = sb("totals", [P, ACC])
        span_i = sb("span_i", [CHUNKS, 2], i32)
        span = sb("span", [CHUNKS, 2])
        slow_i = sb("slow_i", [1, 1], i32)
        iota_col = sb("iota_col", [P, 1])
        win_c = sb("win_c", [P, 2, 3])
        node_count = sb("node_count", [P, 2])
        hist = sb("hist", [TILES, P])
        tots = sb("tots", [TILES, P])
        end_i = sb("end_i", [P, TILES + GT], i32)
        ring_i = sb("ring_i", [P, TILES + GT], i32)
        end_c = sb("end_c", [P, 2 * GT], i32)
        carry_i = sb("carry_i", [P, TILES + GT], i32)
        has = sb("has", [P, TILES + GT])
        has_c = sb("has_c", [P, GT])
        small = sb("small", [P, 2 + 2 * H])
        gmax = sb("gmax", [P, 2, H])
        sums = sb("sums", [P, 2, VC, ACC])
        v_ring = sb("v_ring", [P, 2, VC * D])

        SC = RUN * H
        arena = sb("arena", [P, 3 * SC + 4 * CH * D])
        S = arena[:, 0:SC]
        Fm = arena[:, SC:2 * SC]
        Mm = arena[:, 2 * SC:3 * SC]
        o = 3 * SC
        q_ring = [arena[:, o + r * CH * D:o + (r + 1) * CH * D] for r in range(2)]
        k_ring = [arena[:, o + (2 + r) * CH * D:o + (3 + r) * CH * D] for r in range(2)]
        m1_sb = arena[:, SC:SC + NE * 2 * EH].rearrange("p (e k n) -> p e k n", e=NE, k=2)
        m2_sb = arena[:, SC + NE * 2 * EH:SC + NE * (2 * EH + HC * D)].rearrange("p (e c n) -> p e c n", e=NE, c=HC)
        assert NE * (2 * EH + HC * D) <= 2 * SC + 2 * CH * D
        hid = [arena[:, r * HC * 512:(r + 1) * HC * 512].rearrange("p (c n) -> p c n", c=HC) for r in range(2)]
        x3T = arena[:, 2 * HC * 512:2 * HC * 512 + 2 * GT * P].rearrange("p (k n) -> p k n", k=2)
        got = arena[:, 2 * HC * 512 + 2 * GT * P:2 * HC * 512 + 2 * GT * P + GT * ACC].rearrange("p (t n) -> p t n", t=GT)
        assert 2 * HC * 512 + 2 * GT * P + GT * ACC <= SC
        hidg = arena[:, o + 2 * CH * D:o + 4 * CH * D].rearrange("p (c n) -> p c n", c=GC)

        win_hot = [Fm[:, r * EC:(r + 1) * EC] for r in range(2)]
        dst_row = [Fm[:, (2 + r) * EC:(3 + r) * EC].bitcast(i32) for r in range(2)]
        count_junk = qkv[:, 0:2, :].rearrange("p r n -> p (r n)")[:, 0:EC]
        k4_ring = [arena[:, o + r * CH * D:o + (r + 1) * CH * D] for r in range(4)]
        v_early = [arena[:, o + k * VC * D:o + (k + 1) * VC * D] for k in range(EARLY_STEPS)]
        assert EARLY_STEPS * VC == 4 * CH and EARLY_STEPS % 2 == 0
        q_win = [Fm[:, 4 * EC + r * D:4 * EC + (r + 1) * D] for r in range(2)]
        assert 4 * EC + 2 * D <= SC
        dst_slab = Fm[:, 2 * RUN:2 * RUN + SLABS * SR].bitcast(i32)
        first_diag = Fm[0:CHUNKS, 2 * RUN + SLABS * SR:2 * RUN + SLABS * SR + CHUNKS]
        src_c = Mm[:, 0:RUN].bitcast(i32)
        zrow = Mm[:, RUN:RUN + D]
        win_all = Mm[:, RUN + D + 512:RUN + D + 512 + 3 * CHUNKS]
        win_node = win_all.rearrange("p (c j) -> p c j", j=3)
        node_split = Mm[:, RUN + D + 512 + 3 * CHUNKS:RUN + D + 512 + 6 * CHUNKS]
        zeros = Mm[:, RUN + D:RUN + D + 512]
        sc_out = [Mm[:, RUN + r * CH * H:RUN + (r + 1) * CH * H] for r in range(2)]

        xb = sb("xb", [P, GT, D])
        h0 = sb("h0", [P, GT, D])
        xn = sb("xn", [P, GT, D])
        xT = sb("xT", [P, 2, GT * P])
        efb = h0[:, :, :].rearrange("p t d -> p (t d)").rearrange("p (r n) -> p r n", r=2)
        efT = xT
        shift_cols = xT[:, :, 0:P]
        xn16 = xn[:, :, :].rearrange("p t d -> p (t d)").bitcast(bf16)
        hits_hi = xn16[:, 0:CH * TILES].rearrange("p (t n) -> p t n", t=CH)
        hits_lo = xn16[:, CH * TILES:CH * (TILES + P)].rearrange("p (t n) -> p t n", t=CH)
        tile_hot = [xn[:, r, 0:TILES] for r in range(2)]
        place_hot = [xn[:, r, P:2 * P] for r in range(2)]
        xb16 = xb[:, :, :].rearrange("p t d -> p (t d)").bitcast(bf16)
        dhi = xb16[:, 0:RUN]
        dlo = xb16[:, RUN:2 * RUN]
        rec = sb("rec", [P, GT, H])
        lg = sb("lg", [P, 6, GT, NE])
        tv = sb("tv", [P, 6, GT])
        wmix = sb("wmix", [P, GT, NE])
        iota49 = iota[:, 0:TILES]

        ps = ctx.enter_context(nc.psum_tensor("ps", [P, 8 * 512], f32))

        def bank(b, n=1):
            return ps[:, b * 512:(b + n) * 512]

        const_ld = sem("const_ld")
        edge_ld = sem("edge_ld")
        proj_ld = sem("proj_ld")
        shift_ready = sem("shift_ready")
        shift_ps = sem("shift_ps")
        pool_const = sem("pool_const")
        dve_steps = sem("dve_steps")
        pool_steps = sem("pool_steps")
        bias_ps = sem("bias_ps")
        bias_done = sem("bias_done")
        x_ld = sem("x_ld")
        h0_ready = sem("h0_ready")
        h0_stored = sem("h0_stored")
        var_ready = sem("var_ready")
        rstd_ready = sem("rstd_ready")
        xn_ready = sem("xn_ready")
        xT_ps = sem("xT_ps")
        xT_ready = sem("xT_ready")
        qkv_ps = sem("qkv_ps")
        qkv_ready = sem("qkv_ready")
        qkv_stored = [sem("qkv_stored0"), sem("qkv_stored1")]
        edges_ready = sem("edges_ready")
        idx_ready = sem("idx_ready")
        rows_in = [sem("rows_in0"), sem("rows_in1"), sem("rows_in2"), sem("rows_in3")]
        scores_done = sem("scores_done")
        ef_ld = [sem("ef_ld0"), sem("ef_ld1")]
        efT_ps = sem("efT_ps")
        efT_ready = sem("efT_ready")
        ep_ready = sem("ep_ready")
        hits_ready = sem("hits_ready")
        hits_used = sem("hits_used")
        diag_ready = sem("diag_ready")
        wide_ready = sem("wide_ready")
        wide_ps = sem("wide_ps")
        path_known = sem("path_known")
        srcc_ld = sem("srcc_ld")
        dstrow_ld = [sem("dstrow_ld0"), sem("dstrow_ld1")]
        qwin_ld = [sem("qwin_ld0"), sem("qwin_ld1")]
        hot_ready = sem("hot_ready")
        counted = sem("counted")
        first_ready = sem("first_ready")
        first_ps = sem("first_ps")
        q_ps = sem("q_ps")
        q_used = sem("q_used")
        score_out = [sem("score_out0"), sem("score_out1")]
        score_in = sem("score_in")
        pad_stored = sem("pad_stored")
        small_ps = sem("small_ps")
        end_ready = sem("end_ready")
        exp_in = sem("exp_in")
        late_ready = sem("late_ready")
        late_ps = sem("late_ps")
        late_known = sem("late_known")
        exp_stored = sem("exp_stored")
        exp_rest = sem("exp_rest")
        zero_stored = sem("zero_stored")
        src_ld = sem("src_ld")
        ex_ld = sem("ex_ld")
        ex_second_ld = sem("ex_second_ld")
        row_ready = sem("row_ready")
        row_ps = sem("row_ps")
        masks_ready = sem("masks_ready")
        carry_ps = sem("carry_ps")
        carry_ready = sem("carry_ready")
        carry_stored = sem("carry_stored")
        end_idx = sem("end_idx")
        exp_done = sem("exp_done")
        v_in = [sem("v_in0"), sem("v_in1")]
        v_early_in = sem("v_early_in")
        v_used = sem("v_used")
        run_ready = sem("run_ready")
        run_stored = [sem("run_stored0"), sem("run_stored1")]
        w_ld = sem("w_ld")
        got_in = sem("got_in")
        h0_ld = sem("h0_ld")
        xr_ld = sem("xr_ld")
        attn_ready = sem("attn_ready")
        t_ps = sem("t_ps")
        t_ready = sem("t_ready")
        o_ps = sem("o_ps")
        x1_ready = sem("x1_ready")
        h_ps = sem("h_ps")
        h_ready = sem("h_ready")
        f_ps = sem("f_ps")
        x3_ready = sem("x3_ready")
        r_ps = sem("r_ps")
        w_ready = sem("w_ready")
        wT_ps = sem("wT_ps")
        wT_ready = sem("wT_ready")
        b_ps = sem("b_ps")
        b_used = sem("b_used")
        y_ps = sem("y_ps")
        y_done = sem("y_done")
        out_stored = sem("out_stored")

        block = ctx.enter_context(nc.Block())

        def flat(v, p):
            return v.rearrange("(p n) -> p n", p=p)

        N_PROJ = 9
        N_CONST = 16
        STEP_STEPS = 2 + VC - 1
        SLAB_STEPS = 2 + VS * STEP_STEPS + 2
        FAST_STEPS, SLOW_STEPS = 1 + 12 * (CHUNKS // 4) + 1 + 4, 6 * (CHUNKS // 2)
        fast_more = max(FAST_STEPS - SLOW_STEPS, 0)
        fast_less = max(SLOW_STEPS - FAST_STEPS, 0)
        N_EDGE = 17

        @block.sync
        def _(sp):
            def x_tiles(dst_t, g, nt, s):
                if nt == GT:
                    sp.dma_start(dst_t[:, :, :], x[bass.ds(g * (GT * P), GT * P), :].rearrange("(t p) d -> p t d", p=P)).then_inc(s, 16)
                else:
                    sp.dma_start(dst_t[0:LAST, 0, :], x[(TILES - 1) * P:N, :]).then_inc(s, 16)

            x_tiles(xb, 0, GT, x_ld)
            sp.sem_inc(out_stored, 16)
            with nc.allow_non_contiguous_dma(reason="two columns, once"):
                sp.dma_start(ln1[:, 0, :], g1.rearrange("(k p) -> p k", p=P)).then_inc(proj_ld, 16)
                sp.dma_start(ln1[:, 1, :], b1n.rearrange("(k p) -> p k", p=P)).then_inc(proj_ld, 16)
            for j, w in enumerate((Wq, Wk, Wv)):
                sp.dma_start(wqkv[:, :, j * D:(j + 1) * D], w.rearrange("(c p) n -> p c n", p=P)).then_inc(proj_ld, 16)
            for j, b in enumerate((bq, bk, bv)):
                sp.dma_start(bqkv[:, j * D:(j + 1) * D], b.partition_broadcast(P)).then_inc(proj_ld, 16)
            sp.dma_start(beb[:, :], be.partition_broadcast(P)).then_inc(proj_ld, 16)
            for t, (g, b) in ((ln2, (g2, b2n)), (lnm, (gm, bm))):
                sp.dma_start(t[:, 0, :], g.partition_broadcast(P)).then_inc(const_ld, 16)
                sp.dma_start(t[:, 1, :], b.partition_broadcast(P)).then_inc(const_ld, 16)
            sp.dma_start(wo[:, :, :], Wo.rearrange("(c p) n -> p c n", p=P)).then_inc(const_ld, 16)
            sp.dma_start(bo_b[:, :], bo.partition_broadcast(P)).then_inc(const_ld, 16)
            sp.dma_start(b2_b[:, :], b2.partition_broadcast(P)).then_inc(const_ld, 16)
            sp.dma_start(ab[:, 0:1], alpha.partition_broadcast(P)).then_inc(const_ld, 16)
            sp.dma_start(ab[:, 1:2], beta.partition_broadcast(P)).then_inc(const_ld, 16)
            sp.dma_start(wr[:, :, :], Wr.rearrange("(c p) n -> p c n", p=P)).then_inc(const_ld, 16)
            sp.dma_start(br_b[:, :], br.partition_broadcast(P)).then_inc(const_ld, 16)
            sp.dma_start(mb2_sb[:, :], mb2).then_inc(const_ld, 16)
            sp.dma_start(w1[:, :, :], W1.rearrange("(c p) n -> p c n", p=P)).then_inc(const_ld, 16)
            sp.dma_start(w2[:, :, :], W2.rearrange("(c p) n -> p c n", p=P)).then_inc(const_ld, 16)
            sp.dma_start(bias_raw[0:GC, :], b1.rearrange("(c p) -> c p", p=P)).then_inc(const_ld, 16)
            sp.dma_start(bias_raw[GC:GC + NE * HC, :], mb1.rearrange("e (c p) -> (e c) p", p=P)).then_inc(const_ld, 16)

            def h0_out(g, nt):
                sp.wait_ge(h0_ready, g + 1)
                sp.dma_start(h0_rows[bass.ds(g * (GT * P), nt * P), :].rearrange("(t p) d -> p t d", p=P), h0[:, 0:nt, :]).then_inc(h0_stored, 16)

            def qkv_out(g, nt):
                for t in range(nt):
                    n = g * GT + t
                    sp.wait_ge(qkv_ready, n + 1)
                    for j, rows_t in enumerate((q_rows, k_rows, v_rows)):
                        sp.dma_start(rows_t[bass.ds(n * P, P), :], qkv[:, t % 2, j * D:(j + 1) * D]).then_inc(qkv_stored[t % 2], 16)

            h0_out(0, GT)
            x_tiles(xb, 1, GT, x_ld)
            h0_out(1, GT)
            x_tiles(xb, 2, GT, x_ld)
            qkv_out(0, GT)
            with sp.Fori(1, GROUPS - 2) as g:
                h0_out(g + 1, GT)
                x_tiles(xb, g + 2, GT, x_ld)
                qkv_out(g, GT)
            h0_out(GROUPS - 1, GT)
            x_tiles(xb, GROUPS, 1, x_ld)
            qkv_out(GROUPS - 2, GT)
            h0_out(GROUPS, 1)
            qkv_out(GROUPS - 1, GT)
            qkv_out(GROUPS, 1)

            def ef_in(c, par):
                v = ef[0:(P - 1) * RUN, :].rearrange("(p r) d -> p (r d)", p=P - 1)
                w = CH * ED
                sp.dma_start(efb[0:A_SPLIT, par, :], v[0:A_SPLIT, bass.ds(c * w, w)]).then_inc(ef_ld[par], 16)
                sp.dma_start(efb[A_SPLIT:P - 1, par, :], v[A_SPLIT:P - 1, bass.ds(c * w, w)]).then_inc(ef_ld[par], 16)

            def ef_tail(c, par):
                w = CH * ED
                t = ef[(P - 1) * RUN:E, :].rearrange("(p r) d -> p (r d)", p=1)
                sp.dma_start(efb[P - 1:P, par, :], t[:, bass.ds(c * w, w)]).then_inc(ef_ld[par], 16)

            def ef_tail_again(par):
                w = CH * ED
                t = ef[(P - 1) * RUN:E, :].rearrange("(p r) d -> p (r d)", p=1)
                sp.dma_start(efb[P - 1:P, par, :], t[:, TAIL // CH * w - w:TAIL // CH * w]).then_inc(ef_ld[par], 16)

            sp.wait_ge(h0_stored, 16 * (GROUPS + 1))
            sp.wait_ge(xn_ready, GROUPS + 1)
            sp.wait_ge(path_known, 1)
            slow = sp.value_load(slow_i[0:1, 0:1], min_val=0, max_val=CHUNKS)
            with sp.If(slow > 0):
                for par in range(2):
                    ef_in(par, par)
                    ef_tail(par, par)
                half_tail = TAIL // CH // 2
                with sp.Fori(0, half_tail - 1) as i:
                    for par in range(2):
                        sp.wait_ge(efT_ps, 2 * i + par + 1)
                        ef_in(2 * i + par + 2, par)
                        ef_tail(2 * i + par + 2, par)
                with sp.Fori(half_tail - 1, CHUNKS // 2 - 1) as i:
                    for par in range(2):
                        sp.wait_ge(efT_ps, 2 * i + par + 1)
                        ef_in(2 * i + par + 2, par)
                        ef_tail_again(par)

            with sp.Else():
                def chunk_in(c, par, np_):
                    w = CH * ED
                    sp.dma_start(efb[0:np_, par, :], ef[bass.ds(c * EC, np_ * CH), :].rearrange("(p r) d -> p (r d)", p=np_)).then_inc(ef_ld[par], 16)

                def dst_in(c, par, n):
                    sp.dma_start(dst_row[par][:, 0:n], dst[bass.ds(c * EC, n)].partition_broadcast(P)).then_inc(dstrow_ld[par], 16)

                def win_in(c, par):
                    first = sp.value_load(dst[bass.ds(c * EC, 1)].rearrange("(o n) -> o n", o=1), min_val=0, max_val=N - 1)
                    sp.dma_start(q_win[par], q_rows[bass.ds(first, P), :]).then_inc(qwin_ld[par], 16)

                sp.wait_ge(edges_ready, 1)
                sp.wait_ge(pad_stored, 16)
                sp.wait_ge(qkv_stored[0], 3 * 16 * (TILES // 2 + 1))
                sp.wait_ge(qkv_stored[1], 3 * 16 * (TILES // 2))
                for par in range(2):
                    chunk_in(par, par, P)
                    dst_in(par, par, EC)
                    win_in(par, par)

                def turn(c, par, np_):
                    sp.wait_ge(efT_ps, c + 1)
                    chunk_in(c + 2, par, np_)
                    sp.wait_ge(hot_ready, c + 1)
                    sp.nop(nofuse=True)
                    dst_in(c + 2, par, np_ * CH)
                    sp.wait_ge(q_ps, 2 * c + 2)
                    sp.nop(nofuse=True)
                    win_in(c + 2, par)
                    scores_go(c, par)

                def scores_go(c, par):
                    sp.wait_ge(scores_done, c + 3)
                    sp.dma_start(score_rows[bass.ds(c * EC, EC), :].rearrange("(p j) h -> p (j h)", p=P), sc_out[par]).then_inc(score_out[par], 16)

                EARLY = CHUNKS // 2 - 8
                p1 = 2 * EARLY * EC // RUN
                runs = score_rows[:, :].rearrange("(p r) h -> p (r h)", p=P)
                with sp.Fori(0, EARLY) as i:
                    for par in range(2):
                        turn(2 * i + par, par, P)
                for par in range(2):
                    sp.wait_ge(score_out[par], 16 * (EARLY + 1))
                sp.dma_start(S[0:p1, :], runs[0:p1, :]).then_inc(score_in, 16)
                with sp.Fori(EARLY, CHUNKS // 2 - 2) as i:
                    for par in range(2):
                        turn(2 * i + par, par, P)
                turn(CHUNKS - 4, 0, P)
                turn(CHUNKS - 3, 1, LASTP)
                scores_go(CHUNKS - 2, 0)
                scores_go(CHUNKS - 1, 1)
                for par in range(2):
                    sp.wait_ge(score_out[par], 16 * (CHUNKS // 2 + 1))
                sp.dma_start(S[p1:P, :], runs[p1:P, :]).then_inc(score_in, 16)

            sp.wait_ge(scores_done, CHUNKS + 2)
            for j in range(SLABS - 1):
                sp.dma_start(src_all[:, j * SR:(j + 1) * SR], src[j * SE:(j + 1) * SE].rearrange("(p j) -> p j", p=P)).then_inc(src_ld, 16)
            full, part = SLAB_TAIL // SR, SLAB_TAIL % SR
            last_slab = src[(SLABS - 1) * SE:E]
            sp.dma_start(src_all[0:full, (SLABS - 1) * SR:SLABS * SR], last_slab[0:full * SR].rearrange("(p j) -> p j", j=SR)).then_inc(src_ld, 16)
            sp.dma_start(src_all[full:full + 1, (SLABS - 1) * SR:(SLABS - 1) * SR + part], last_slab[full * SR:SLAB_TAIL].rearrange("(p j) -> p j", p=1)).then_inc(src_ld, 16)

            def exp_slab(n, to=ex_slab, after=None, s=ex_ld):
                if after is None:
                    sp.wait_ge(run_ready, n * VS)
                elif after > 0:
                    sp.wait_ge(run_ready, after * VS)
                sp.dma_start(to, exp_rows[bass.ds(n * SE, SE), :].rearrange("(p r) h -> p (r h)", p=P)).then_inc(s, 16)

            def sums_out(n, k, rows):
                sp.wait_ge(run_ready, n * VS + k + 1)
                rows = rows.rearrange("(p r) a -> p (r a)", p=P)
                sp.dma_start(rows[:, k * (VC * ACC):(k + 1) * (VC * ACC)],
                             sums[:, k % 2, :, :].rearrange("p t a -> p (t a)")).then_inc(run_stored[k % 2], 16)

            def carry_out(n):
                sp.wait_ge(carry_ready, n + 1)
                sp.dma_start(carry_rows[bass.ds(n * P, P), :], carry).then_inc(carry_stored, 16)

            def slab(n, rows):
                for k in range(VS):
                    sums_out(n, k, rows)
                carry_out(n)

            sp.wait_ge(exp_stored, 16)
            sp.wait_ge(zero_stored, 48)
            exp_slab(0, after=0)
            exp_slab(1, to=ex_second, after=0, s=ex_second_ld)
            sp.wait_ge(late_known, 1)
            late_slabs = sp.value_load(late_i[0:1, 0:1], min_val=0, max_val=P)
            with sp.If(late_slabs > 0):
                slab(0, sum_rows[0:SE, :])
                sp.wait_ge(exp_rest, 16)
                exp_slab(2, after=1)
                slab(1, sum_rows[SE:2 * SE, :])
                slab(2, sum_rows[2 * SE:3 * SE, :])
                with sp.Fori(3, SLABS) as n:
                    exp_slab(n)
                    slab(n, sum_rows[bass.ds(n * SE, SE), :])
            with sp.Else():
                slab(0, ring_rows[0:SE, :])
                sp.wait_ge(exp_rest, 16)
                exp_slab(2, after=1)
                slab(1, ring_rows[SE:2 * SE, :])
            assert FIRST == 2 and AHEAD == 3

            def node_in(g, nt):
                sp.dma_start(h0[:, 0:nt, :], h0_rows[bass.ds(g * (GT * P), nt * P), :].rearrange("(t p) d -> p t d", p=P)).then_inc(h0_ld, 16)
                x_tiles(xb, g, nt, xr_ld)

            def rows_out(g, nt):
                sp.wait_ge(y_done, (g + 1) * NE + 1)
                if nt == GT:
                    sp.dma_start(out[bass.ds(g * (GT * P), GT * P), :].rearrange("(t p) d -> p t d", p=P), yo[:, :, :]).then_inc(out_stored, 16)
                else:
                    sp.dma_start(out[(TILES - 1) * P:N, :], yo[0:LAST, 0, :]).then_inc(out_stored, 16)

            def beside(g, r, steps_out, first=False, last=False):
                with sp.If(late_slabs > 0):
                    pass
                with sp.Else():
                    if first:
                        exp_slab(g + AHEAD)
                    for k in steps_out:
                        sums_out(g + AHEAD, k, ring_rows[r * SE:(r + 1) * SE, :])
                    if last:
                        carry_out(g + AHEAD)

            sp.wait_ge(exp_rest, 16)
            node_in(0, GT)
            beside(-1, AHEAD - 1, range(0, 4))
            sp.wait_ge(x1_ready, 1)
            node_in(1, GT)
            beside(-1, AHEAD - 1, range(4, VS), last=True)
            def turn_beside(g, r):
                beside(g, r, range(0, 6), first=True)
                sp.wait_ge(x1_ready, g + 2)
                node_in(g + 2, GT)
                beside(g, r, range(6, VS))
                rows_out(g, GT)
                beside(g, r, (), last=True)

            assert (SLABS - AHEAD) % AHEAD == 1
            with sp.Fori(0, (SLABS - AHEAD) // AHEAD) as i:
                for r in range(AHEAD):
                    turn_beside(AHEAD * i + r, r)
            turn_beside(SLABS - AHEAD - 1, 0)
            for g in range(SLABS - AHEAD, TURNS1):
                sp.wait_ge(x1_ready, g + 2)
                node_in(g + 2, GT if g + 2 < GROUPS else 1)
                rows_out(g, GT)
            rows_out(TURNS1, GT)
            rows_out(GROUPS, 1)
            sp.wait_ge(out_stored, 16 * (GROUPS + 2))

        @block.gpsimd
        def _(pool):
            pool.memset(ident[:, :], 0.0).then_inc(pool_steps, 1)
            pool.memset(ones[:, :], 1.0).then_inc(pool_steps, 1)
            pool.memset(half[:, :], -0.5).then_inc(pool_steps, 1)
            pool.memset(ebase[:, :], 2.718281828459045).then_inc(pool_steps, 1)
            pool.memset(src_all[:, :], 0).then_inc(pool_const, 1)
            pool.memset(dst_slab, PADNODE).then_inc(pool_const, 1)
            pool.memset(dst_i[:, :], PADNODE).then_inc(pool_const, 1)
            pool.memset(ews[:, :], 0.0).then_inc(pool_const, 1)
            pool.memset(weblk[:, :], 0.0).then_inc(pool_const, 1)
            pool.memset(zrow, 0.0).then_inc(pool_const, 1)
            pool.memset(zeros, 0.0).then_inc(pool_const, 1)
            pool.iota(iota_col[:, :], pattern=[[0, 1]], base=0, channel_multiplier=1, allow_small_or_imprecise_dtypes=True).then_inc(pool_steps, 1)
            pool.iota(iota[:, :], pattern=[[1, P]], base=0, channel_multiplier=0, allow_small_or_imprecise_dtypes=True).then_inc(pool_steps, 1)
            pool.iota(i8[:, :], pattern=[[1, NE]], base=0, channel_multiplier=0, allow_small_or_imprecise_dtypes=True).then_inc(pool_steps, 1)
            pool.wait_ge(pool_steps, 7)
            pool.affine_select(out=ident[:, :], in_=ident[:, :], compare_op=ALU.not_equal, fill=1.0, base=0,
                               pattern=[[-1, P]], channel_multiplier=1).then_inc(pool_steps, 1)
            pool.affine_select(out=tri[:, :], in_=ones[:, :], compare_op=ALU.is_gt, fill=0.0, base=0,
                               pattern=[[1, P]], channel_multiplier=-1).then_inc(pool_steps, 1)

            def rstd(n, nt):
                pool.wait_ge(var_ready, n + 1)
                nc.gpsimd.tensor_tensor(rs[:, 0:nt], ve[:, 0:nt], half[:, 0:nt], ALU.pow).then_inc(rstd_ready, 1)

            with pool.Fori(0, GROUPS) as g:
                rstd(2 * g, GT)
                rstd(2 * g + 1, GT)
            rstd(2 * GROUPS, 1)
            rstd(2 * GROUPS + 1, 1)

            pool.wait_ge(qkv_stored[0], 3 * 16 * (TILES // 2 + 1))
            pool.wait_ge(qkv_stored[1], 3 * 16 * (TILES // 2))

            def gather(dst_t, table, par, j, s):
                pool.indirect_dma_start(dst_t, None, table[:, :], bass.IndirectOffsetOnAxis(ap=gat_i[:, par, j:j + 1], axis=0)).then_inc(s, 16)

            pool.wait_ge(srcc_ld, 32)
            pool.wait_ge(path_known, 1)
            slow = pool.value_load(slow_i[0:1, 0:1], min_val=0, max_val=CHUNKS)
            with pool.If(slow > 0):
                pool.wait_ge(edges_ready, 1)
                with pool.Fori(0, CHUNKS // 2) as i:
                    for par in range(2):
                        c = 2 * i + par
                        pool.wait_ge(scores_done, c + 1)
                        pool.nop(nofuse=True)
                        pool.tensor_copy(gat_i[:, par, 0:CH], src_i[:, bass.ds(c * CH, CH)]).then_inc(idx_ready, 1)
                        pool.tensor_copy(gat_i[:, par, CH:2 * CH], dst_i[:, bass.ds(c * CH, CH)]).then_inc(idx_ready, 1)
                        pool.wait_ge(idx_ready, 2 * c + 2)
                        pool.nop(nofuse=True)
                        for j in range(CH):
                            gather(k_ring[par][:, j * D:(j + 1) * D], k_rows, par, j, rows_in[par])
                            gather(q_ring[par][:, j * D:(j + 1) * D], q_rows, par, CH + j, rows_in[par])

            with pool.Else():
                pool.memset(gat_i[:, :, :], 0).then_inc(idx_ready, 1)
                pool.wait_ge(idx_ready, 1)
                pool.nop(nofuse=True)

                def k_chunk(c, slot, np_, wait=True):
                    if wait:
                        pool.wait_ge(scores_done, c - 1)
                    pool.nop(nofuse=True)
                    b, j0 = slot // 2, slot % 2 * CH
                    pool.tensor_copy(gat_i[0:np_, b, j0:j0 + CH], src_c[0:np_, bass.ds(c * CH, CH)]).then_inc(idx_ready, 1)
                    pool.wait_ge(idx_ready, c + 2)
                    pool.nop(nofuse=True)
                    for j in range(CH):
                        gather(k4_ring[slot][:, j * D:(j + 1) * D], k_rows, b, j0 + j, rows_in[slot])

                for c in range(4):
                    k_chunk(c, c, P, wait=False)
                with pool.Fori(1, CHUNKS // 4) as i:
                    for slot in range(4):
                        k_chunk(4 * i + slot, slot, P)
                k_chunk(CHUNKS - 2, 0, P)
                k_chunk(CHUNKS - 1, 1, LASTP)
                pool.sem_inc(idx_ready, CHUNKS - 1)

            pool.wait_ge(src_ld, 16 * (SLABS + 1))
            pool.nop(nofuse=True)

            def v_rows_in(n, k, wait=True):
                c, par = n * VS + k, k % 2
                if wait:
                    pool.wait_ge(v_used, c + 1)
                pool.nop(nofuse=True)
                pool.tensor_copy(gat_i[:, par, 0:VC], src_all[:, bass.ds(n * SR + k * VC, VC)]).then_inc(idx_ready, 1)
                pool.wait_ge(idx_ready, 2 * CHUNKS + c + 1)
                pool.nop(nofuse=True)
                for j in range(VC):
                    gather(v_ring[:, par, j * D:(j + 1) * D], v_rows, par, j, v_in[par])

            pool.tensor_copy(gat_i[:, :, :].rearrange("p r j -> p (r j)"), src_all[:, 0:4 * CH]).then_inc(idx_ready, EARLY_STEPS)
            pool.wait_ge(idx_ready, 2 * CHUNKS + EARLY_STEPS)
            pool.nop(nofuse=True)
            for k in range(EARLY_STEPS):
                for j in range(VC):
                    col = k * VC + j
                    gather(v_early[k][:, j * D:(j + 1) * D], v_rows, col // (2 * CH), col % (2 * CH), v_early_in)
            pool.wait_ge(v_early_in, 16 * VC * EARLY_STEPS)
            pool.nop(nofuse=True)
            for k in range(EARLY_STEPS, VS):
                v_rows_in(0, k, wait=k >= EARLY_STEPS + 2)
            with pool.Fori(1, FIRST) as n:
                for k in range(VS):
                    v_rows_in(n, k)
            pool.wait_ge(late_known, 1)
            late_slabs = pool.value_load(late_i[0:1, 0:1], min_val=0, max_val=P)
            with pool.If(late_slabs > 0):
                with pool.Fori(FIRST, SLABS) as n:
                    for k in range(VS):
                        v_rows_in(n, k)
                for par in range(2):
                    pool.wait_ge(run_stored[par], 16 * (SLABS * VS // 2 + 1))
                pool.wait_ge(carry_stored, 16 * SLABS)

            pool.wait_ge(end_ready, 2)
            pool.wait_ge(exp_rest, 16)
            pool.wait_ge(zero_stored, 48)

            def ends(g, nt):
                done = min(g + 2, SLABS) if isinstance(g, int) else g + 2
                for par in range(2):
                    pool.wait_ge(run_stored[par], 16 * (done * (VS // 2) + 1))
                pool.wait_ge(carry_stored, 16 * done)
                pool.nop(nofuse=True)
                def rows_of(ends_i, table, rows):
                    pool.tensor_copy(end_c[:, 0:nt], ends_i[:, bass.ds(g * GT, nt)]).then_inc(end_idx, 1)
                    pool.tensor_copy(end_c[:, GT:GT + nt], carry_i[:, bass.ds(g * GT, nt)]).then_inc(end_idx, 1)
                    pool.wait_ge(end_idx, 2 * g + 2)
                    pool.nop(nofuse=True)
                    for t in range(nt):
                        pool.indirect_dma_start(got[:, t, :], None, table[0:rows, :],
                                                bass.IndirectOffsetOnAxis(ap=end_c[:, t:t + 1], axis=0)).then_inc(got_in, 16)
                        pool.indirect_dma_start(got_carry[:, t, :], None, carry_rows[:, :],
                                                bass.IndirectOffsetOnAxis(ap=end_c[:, GT + t:GT + t + 1], axis=0)).then_inc(got_in, 16)

                with pool.If(late_slabs > 0):
                    rows_of(end_i, sum_rows, SLABS * SE)
                with pool.Else():
                    rows_of(ring_i, ring_rows, (FIRST if isinstance(g, int) and g == 0 else AHEAD) * SE)

            n0 = 2 * (GROUPS + 1)

            def norm_power(g, j, nt):
                rstd(n0 + g * 4 + j, nt)

            def weight_power(g, nt):
                pool.wait_ge(var_ready, n0 + g * 4 + 4)
                nc.gpsimd.tensor_tensor(tv[:, 3, 0:nt], ebase[:, 0:nt], tv[:, 2, 0:nt], ALU.pow).then_inc(rstd_ready, 1)

            def powers(g, nt):
                for j in range(3):
                    norm_power(g, j, nt)
                weight_power(g, nt)

            def sums_used(g):
                pool.wait_ge(attn_ready, g + 1)
                pool.nop(nofuse=True)

            def beside(g, ks):
                with pool.If(late_slabs > 0):
                    pass
                with pool.Else():
                    for k in ks:
                        v_rows_in(g + AHEAD, k)

            beside(-1, (0, 1))
            ends(0, GT)
            beside(-1, (2, 3))
            norm_power(0, 0, GT)
            beside(-1, range(4, 12))
            norm_power(0, 1, GT)
            norm_power(0, 2, GT)
            beside(-1, range(12, VS))
            weight_power(0, GT)
            sums_used(0)
            ends(1, GT)
            with pool.Fori(0, SLABS - AHEAD) as g:
                beside(g, range(0, 8))
                norm_power(g + 1, 0, GT)
                beside(g, range(8, 14))
                norm_power(g + 1, 1, GT)
                norm_power(g + 1, 2, GT)
                beside(g, range(14, VS))
                weight_power(g + 1, GT)
                sums_used(g + 1)
                ends(g + 2, GT)
            for g in range(SLABS - AHEAD, TURNS1):
                powers(g + 1, GT)
                sums_used(g + 1)
                ends(g + 2, GT if g + 2 < GROUPS else 1)
            powers(GROUPS, 1)

        @block.scalar
        def _(act):
            act.wait_ge(pool_const, 7)
            for d_t, s_t in ((src_i, src), (dst_i, dst), (ews, ew)):
                v = flat(s_t[0:(P - 1) * RUN], P - 1)
                act.dma_start(d_t[0:A_SPLIT, :], v[0:A_SPLIT, :]).then_inc(edge_ld, 16)
                act.dma_start(d_t[A_SPLIT:P - 1, :], v[A_SPLIT:P - 1, :]).then_inc(edge_ld, 16)
                act.dma_start(d_t[P - 1:P, 0:TAIL], flat(s_t[(P - 1) * RUN:E], 1)).then_inc(edge_ld, 16)
            full, part = SLAB_TAIL // SR, SLAB_TAIL % SR
            act.dma_start(dst_slab[:, 0:(SLABS - 1) * SR].rearrange("p (s j) -> p s j", j=SR),
                          dst[0:(SLABS - 1) * SE].rearrange("(s p j) -> p s j", p=P, j=SR)).then_inc(edge_ld, 16)
            last_slab = dst[(SLABS - 1) * SE:E]
            act.dma_start(dst_slab[0:full, (SLABS - 1) * SR:SLABS * SR], last_slab[0:full * SR].rearrange("(p j) -> p j", j=SR)).then_inc(edge_ld, 16)
            act.dma_start(dst_slab[full:full + 1, (SLABS - 1) * SR:(SLABS - 1) * SR + part], last_slab[full * SR:SLAB_TAIL].rearrange("(p j) -> p j", p=1)).then_inc(edge_ld, 16)
            with nc.allow_non_contiguous_dma(reason="the first and last destination of each chunk, once"):
                act.dma_start(span_i[0:CHUNKS, 0:1], dst[0:(CHUNKS - 1) * EC + 1:EC].rearrange("(p o) -> p o", o=1)).then_inc(edge_ld, 16)
                act.dma_start(span_i[0:CHUNKS - 1, 1:2], dst[EC - 1:(CHUNKS - 1) * EC:EC].rearrange("(p o) -> p o", o=1)).then_inc(edge_ld, 16)
            act.dma_start(span_i[CHUNKS - 1:CHUNKS, 1:2], dst[E - 1:E].rearrange("(p o) -> p o", o=1)).then_inc(edge_ld, 16)
            act.dma_start(q_rows[ROWS:ROWS + P, :], zrow[:, :]).then_inc(pad_stored, 16)
            zw = (SLABS * SE - CE) * H // P
            assert zw <= 512
            act.dma_start(exp_rows[CE:SLABS * SE, :].rearrange("(p r) h -> p (r h)", p=P), zeros[:, 0:zw]).then_inc(zero_stored, 16)
            act.dma_start(carry_rows[SLABS * P:SLABS * P + 1, :], zeros[0:1, 0:ACC]).then_inc(zero_stored, 16)
            act.dma_start(carry_rows[0:SLABS * P, :].rearrange("(s p) a -> p s a", p=P),
                          zeros[:, 0:ACC].unsqueeze(1).to_broadcast([P, SLABS, ACC])).then_inc(zero_stored, 16)
            act.dma_start(src_c[:, 0:(CHUNKS - 1) * CH].rearrange("p (c j) -> p c j", j=CH),
                          src[0:(CHUNKS - 1) * EC].rearrange("(c p j) -> p c j", p=P, j=CH)).then_inc(srcc_ld, 16)
            act.dma_start(src_c[0:LASTP, (CHUNKS - 1) * CH:RUN], src[(CHUNKS - 1) * EC:E].rearrange("(p j) -> p j", j=CH)).then_inc(srcc_ld, 16)
            act.dma_start(weblk[0:ED, 0:DH], We).then_inc(edge_ld, 16)
            act.dma_start(weblk[ED:2 * ED, DH:2 * DH], We).then_inc(edge_ld, 16)

            def qkv_group(g, nt):
                act.wait_ge(xT_ps, g + 1)
                nc.scalar.copy(xT[:, :, 0:nt * P].rearrange("p k (t n) -> p t k n", n=P),
                               bank(0, 2)[:, 0:nt * 2 * P].rearrange("p (t k n) -> p t k n", k=2, n=P)).then_inc(xT_ready, 1)

            qkv_group(0, GT)
            with act.Fori(1, GROUPS) as g:
                qkv_group(g, GT)
            qkv_group(GROUPS, 1)

            act.wait_ge(bias_ps, 1)
            nc.scalar.copy(bias_T[:, :], bank(7)[:, 0:GC + NE * HC]).then_inc(bias_done, 1)

            act.wait_ge(path_known, 1)
            slow = act.value_load(slow_i[0:1, 0:1], min_val=0, max_val=CHUNKS)
            with act.If(slow > 0):
                with act.Fori(0, CHUNKS // 2) as i:
                    for par in range(2):
                        c = 2 * i + par
                        act.wait_ge(efT_ps, c + 1)
                        nc.scalar.copy(efT[:, par, :], bank(par)).then_inc(efT_ready, 1)

            with act.Else():
                act.sem_inc(counted, 1)

                def chunk(c, par, n):
                    act.wait_ge(efT_ps, c + 1)
                    nc.scalar.copy(efT[:, par, :], bank(7)).then_inc(efT_ready, 1)
                    act.wait_ge(hot_ready, c + 1)
                    act.wait_ge(counted, c + 1)
                    nc.scalar.activation(count_junk[:, 0:n], win_hot[par][:, 0:n], ACT.Copy, accum_out=node_count[:, par:par + 1]).then_inc(counted, 1)

                with act.Fori(0, CHUNKS // 2 - 1) as i:
                    for par in range(2):
                        chunk(2 * i + par, par, EC)
                chunk(CHUNKS - 2, 0, EC)
                chunk(CHUNKS - 1, 1, LASTP * CH)

            for half_, (c0, c1) in enumerate(((0, SC // 2), (SC // 2, SC))):
                act.wait_ge(exp_in, half_ + 1)
                nc.scalar.activation(S[:, c0:c1], S[:, c0:c1], ACT.Exp).then_inc(exp_done, 1)
            act.wait_ge(exp_done, 2)
            p1 = -(-FIRST * SE // RUN)
            v = exp_rows[0:CE, :].rearrange("(p r) h -> p (r h)", p=P)
            act.dma_start(v[0:p1, :], S[0:p1, :]).then_inc(exp_stored, 16)
            act.wait_ge(ex_ld, 16)
            act.wait_ge(ex_second_ld, 16)
            act.dma_start(v[p1:P, :], S[p1:P, :]).then_inc(exp_rest, 16)
            act.wait_ge(exp_rest, 16)
            assert NE >= EARLY_STEPS // 2
            for e in range(NE):
                act.wait_ge(run_ready, 2 * e + 1)
                act.dma_start(m1_sb[:, e, :, :], M1[e, :, :].rearrange("(k p) n -> p k n", p=P)).then_inc(w_ld, 16)
            for e in range(NE):
                act.wait_ge(run_ready, 2 * (NE + e) + 1)
                act.dma_start(m2_sb[:, e, :, :], M2[e, :, :].rearrange("(c p) n -> p c n", p=P)).then_inc(w_ld, 16)

            count = Chain(act, h_ready)

            def gelus(chunks, nt, first_bias, dest):
                for j in range(chunks):
                    act.wait_ge(h_ps, count.base + count.n + 1)
                    b = count.n % 2
                    count.step(nc.scalar.activation(dest[:, j, 0:nt * P], bank(b)[:, 0:nt * P], ACT.Gelu,
                                                    bias=bias_T[:, first_bias + j:first_bias + j + 1]))

            def copy_T(k, g, nt, dest):
                act.wait_ge(t_ps, 3 * g + k + 1)
                nc.scalar.copy(dest[:, :, 0:nt * P].rearrange("p k (t n) -> p t k n", n=P),
                               bank(4, 2)[:, 0:nt * 2 * P].rearrange("p (t k n) -> p t k n", k=2, n=P)).then_inc(t_ready, 1)

            def copy_wT(g, nt):
                act.wait_ge(wT_ps, g + 1)
                nc.scalar.copy(wT[:, 0:nt * P], bank(7)[0:NE, 0:nt * P]).then_inc(wT_ready, 1)

            def prepare(g, nt):
                copy_T(0, g, nt, xT)
                copy_T(1, g, nt, xT)
                gelus(GC, nt, 0, hidg)
                copy_T(2, g, nt, x3T)

            def group(g, nt, ahead):
                def moe(e):
                    gelus(HC, nt, GC + e * HC, hid[e % 2])

                moe(0)
                copy_wT(g, nt)
                moe(1)
                moe(2)
                if ahead:
                    copy_T(0, g + 1, ahead, xT)
                moe(3)
                moe(4)
                if ahead:
                    copy_T(1, g + 1, ahead, xT)
                moe(5)
                if ahead:
                    gelus(GC, ahead, 0, hidg)
                moe(6)
                moe(7)
                if ahead:
                    copy_T(2, g + 1, ahead, x3T)

            prepare(0, GT)
            with act.Fori(0, TURNS1) as g:
                count.enter(g, NE * HC + GC)
                group(g, GT, GT)
            count.leave(TURNS1)
            group(TURNS1, GT, 1)
            group(GROUPS, 1, 0)

        @block.tensor
        def _(pe):
            def transposes(src_t, nt, first_bank):
                for t in range(nt):
                    for k in range(2):
                        last = nc.tensor.transpose(ps[:, first_bank * 512 + (2 * t + k) * P:first_bank * 512 + (2 * t + k + 1) * P],
                                                   src_t[:, t, k * P:(k + 1) * P], ident[:, :])
                return last

            pe.wait_ge(pool_steps, 9)
            pe.wait_ge(shift_ready, 1)
            for c0, c1 in ((0, 512), (512, 3 * D)):
                for k in range(2):
                    last = nc.tensor.matmul(ps[:, 2 * 512 + c0:2 * 512 + c1], shift_cols[:, k, :], wqkv[:, k, c0:c1], start=k == 0, stop=k == 1)
            last.then_inc(shift_ps, 1)

            def qkv_group(g, nt):
                pe.wait_ge(xn_ready, g + 1)
                transposes(xn, nt, 0).then_inc(xT_ps, 1)
                pe.wait_ge(xT_ready, g + 1)
                for t in range(nt):
                    n = g * GT + t
                    if not (isinstance(g, int) and g == 0 and t < 2):
                        pe.wait_ge(qkv_ready, n - 1)
                    o_ = (2 + 2 * (t % 2)) * 512
                    for c0, c1 in ((0, 512), (512, 3 * D)):
                        for k in range(2):
                            last = nc.tensor.matmul(ps[:, o_ + c0:o_ + c1], xT[:, k, t * P:(t + 1) * P], wqkv[:, k, c0:c1],
                                                    start=k == 0, stop=k == 1)
                    last.then_inc(qkv_ps, 1)

            qkv_group(0, GT)
            pe.wait_ge(first_ready, 1)
            nc.tensor.matmul(bank(6)[:, 0:CHUNKS], ones[0:CHUNKS, :], first_diag, start=True, stop=True).then_inc(first_ps, 1)

            pe.wait_ge(wide_ready, 1)
            nc.tensor.matmul(bank(7)[0:1, 0:1], span[:, 0:1], ones[0:CHUNKS, 0:1], start=True, stop=True).then_inc(wide_ps, 1)

            with pe.Fori(1, GROUPS) as g:
                qkv_group(g, GT)
            qkv_group(GROUPS, 1)

            pe.wait_ge(const_ld, 16 * N_CONST)
            pe.wait_ge(path_known, 1)
            nb = GC + NE * HC
            nc.tensor.transpose(bank(7)[:, 0:nb], bias_raw[:, :], ident[0:nb, 0:nb]).then_inc(bias_ps, 1)
            pe.wait_ge(bias_done, 1)

            pe.wait_ge(path_known, 1)
            pe.wait_ge(edges_ready, 1)
            pe.wait_ge(qkv_ready, TILES)
            nc.tensor.matmul(bank(4)[0:TILES, 0:P], hits_hi[:, 0, :], hits_lo[:, 0, :], start=True, stop=False,
                             skip_group_check=True).then_inc(hits_used, 1)

            slow = pe.value_load(slow_i[0:1, 0:1], min_val=0, max_val=CHUNKS)
            with pe.If(slow > 0):
                def ef_transposes(c, i, par):
                    pe.wait_ge(ef_ld[par], 48 * (i + 1))
                    for j in range(CH // 2):
                        last = nc.tensor.transpose(bank(par)[:, j * P:(j + 1) * P], efb[:, par, j * P:(j + 1) * P], ident[:, :])
                    last.then_inc(efT_ps, 1)

                def chunk(i, par, ahead, first=False):
                    c = 2 * i + par
                    if ahead:
                        ef_transposes(c + 1, i + par, 1 - par)
                    pe.wait_ge(efT_ready, c + 1)
                    pe.wait_ge(scores_done, c + 1)
                    for j in range(CH // 2):
                        last = nc.tensor.matmul(bank(2 + par)[:, 2 * j * DH:2 * (j + 1) * DH], efT[:, par, j * P:(j + 1) * P], weblk[:, :],
                                                start=True, stop=True)
                    last.then_inc(ep_ready, 1)
                    pe.wait_ge(hits_ready, c + 1)
                    for j in range(CH):
                        last = nc.tensor.matmul(bank(4)[0:TILES, 0:P], hits_hi[:, j, :], hits_lo[:, j, :], start=False,
                                                stop=False, skip_group_check=True)
                    last.then_inc(hits_used, 1)

                ef_transposes(0, 0, 0)
                with pe.Fori(0, CHUNKS // 2 - 1) as i:
                    chunk(i, 0, True)
                    chunk(i, 1, True)
                chunk(CHUNKS // 2 - 1, 0, True)
                chunk(CHUNKS // 2 - 1, 1, False)

            with pe.Else():
                def features_across(c, i, par):
                    pe.wait_ge(ef_ld[par], 16 * (i + 1))
                    for j in range(CH // 2):
                        last = nc.tensor.transpose(bank(7)[:, j * P:(j + 1) * P], efb[:, par, j * P:(j + 1) * P], ident[:, :])
                    last.then_inc(efT_ps, 1)

                def window_chunk(i, par, ahead):
                    c = 2 * i + par
                    pe.wait_ge(efT_ready, c + 1)
                    if ahead:
                        features_across(c + 1, i + par, 1 - par)
                    pe.wait_ge(scores_done, c + 1)
                    for j in range(CH // 2):
                        last = nc.tensor.matmul(bank(5 + par)[:, 2 * j * DH:2 * (j + 1) * DH], efT[:, par, j * P:(j + 1) * P], weblk[:, :], start=True, stop=True)
                    last.then_inc(ep_ready, 1)
                    pe.wait_ge(hot_ready, c + 1)
                    pe.wait_ge(qwin_ld[par], 16 * (i + 1))
                    for half_ in range(2):
                        pe.wait_ge(q_used, 2 * c + half_ + 1)
                        for j in range(CH // 2):
                            t = half_ * (CH // 2) + j
                            last = nc.tensor.matmul(bank(2 * half_, 2)[:, j * D:(j + 1) * D], win_hot[par].rearrange("n (p j) -> n j p", j=CH)[:, t, :],
                                                    q_win[par], start=True, stop=True)
                        last.then_inc(q_ps, 1)
                    pe.wait_ge(hits_ready, c + 1)
                    nc.tensor.matmul(bank(4)[0:TILES, 0:P], tile_hot[par], place_hot[par], start=False, stop=False,
                                     skip_group_check=True).then_inc(hits_used, 1)

                features_across(0, 0, 0)
                with pe.Fori(0, CHUNKS // 2 - 1) as i:
                    window_chunk(i, 0, True)
                    window_chunk(i, 1, True)
                window_chunk(CHUNKS // 2 - 1, 0, True)
                window_chunk(CHUNKS // 2 - 1, 1, False)

            pe.wait_ge(diag_ready, 1)
            for r in range(2 + 2 * H):
                last = nc.tensor.matmul(ps[:, r * P:(r + 1) * P], ones[:, :], early[:, r * P:(r + 1) * P],
                                        start=True, stop=True)
            last.then_inc(small_ps, 1)
            nc.tensor.matmul(bank(5)[0:TILES, 0:1], tri[0:TILES, 0:TILES], tots[:, P - 1:P], start=True, stop=True).then_inc(small_ps, 1)
            pe.wait_ge(diag_ready, 2)
            nc.tensor.transpose(bank(6)[:, 0:TILES], tots[:, :], ident[0:TILES, 0:TILES])
            nc.tensor.transpose(bank(6)[:, P:P + TILES], hist[:, :], ident[0:TILES, 0:TILES]).then_inc(small_ps, 1)

            count = Chain(pe, h_ps)

            def hidden(chunks, nt, weights, xt):
                for j in range(chunks):
                    if not (isinstance(count.base, int) and count.base + count.n < 2):
                        pe.wait_ge(h_ready, count.base + count.n - 1)
                    b = count.n % 2
                    for k in range(2):
                        last = nc.tensor.matmul(bank(b)[:, 0:nt * P], weights(k, j), xt[:, k, 0:nt * P], start=k == 0, stop=k == 1)
                    count.step(last)

            def first_nodes(n):
                pe.wait_ge(row_ready, n + 1)
                nc.tensor.matmul(bank(7)[:, 0:P], ones[:, :], row_diag, start=True, stop=True).then_inc(row_ps, 1)

            def carries(n):
                pe.wait_ge(masks_ready, n + 1)
                nc.tensor.matmul(bank(7)[:, P:P + ACC], mask_in, sums[:, 1, VC - 1, :], start=True, stop=False)
                nc.tensor.matmul(bank(7)[:, P:P + ACC], mask_over, totals[:, :], start=False, stop=True).then_inc(carry_ps, 1)

            def beside(g, product):
                with pe.If(late_slabs > 0):
                    pass
                with pe.Else():
                    product(g + AHEAD)

            def T(k, g, nt, ready, src_t):
                pe.wait_ge(ready, g + 1)
                transposes(src_t, nt, 4).then_inc(t_ps, 1)

            def project(g, nt):
                pe.wait_ge(t_ready, 3 * g + 1)
                for t in range(nt):
                    for k in range(2):
                        last = nc.tensor.matmul(bank(4, 2)[:, t * D:(t + 1) * D], xT[:, k, t * P:(t + 1) * P], wo[:, k, :],
                                                start=k == 0, stop=k == 1)
                last.then_inc(o_ps, 1)

            def feed(g, nt):
                pe.wait_ge(t_ready, 3 * g + 2)
                hidden(GC, nt, lambda k, j: w1[:, k, j * P:(j + 1) * P], xT)

            def feed2(g, nt):
                pe.wait_ge(h_ready, count.base + feed_end[0])
                for t in range(nt):
                    for j in range(GC):
                        last = nc.tensor.matmul(bank(4, 2)[:, t * D:(t + 1) * D], hidg[:, j, t * P:(t + 1) * P], w2[:, j, :],
                                                start=j == 0, stop=j == GC - 1)
                last.then_inc(f_ps, 1)

            feed_end = [0]

            def route(g, nt):
                pe.wait_ge(t_ready, 3 * g + 3)
                for t in range(nt):
                    for k in range(2):
                        last = nc.tensor.matmul(bank(6)[:, t * NE:(t + 1) * NE], x3T[:, k, t * P:(t + 1) * P], wr[:, k, :],
                                                start=k == 0, stop=k == 1)
                last.then_inc(r_ps, 1)

            def group(g, nt, ahead, with_slab=False):
                ends_at = {}

                def m1(e):
                    hidden(HC, nt, lambda k, j: m1_sb[:, e, k, j * P:(j + 1) * P], x3T)
                    ends_at[e] = count.n

                def m2(e):
                    pe.wait_ge(h_ready, count.base + ends_at[e])
                    pe.wait_ge(y_done, g * NE + e + 1)
                    for t in range(nt):
                        for j in range(HC):
                            last = nc.tensor.matmul(bank(2, 2)[:, t * D:(t + 1) * D], hid[e % 2][:, j, t * P:(t + 1) * P],
                                                    m2_sb[:, e, j, :], start=j == 0, stop=j == HC - 1)
                    last.then_inc(y_ps, 1)

                m1(0)
                pe.wait_ge(w_ready, g + 1)
                for t in range(nt):
                    last = nc.tensor.transpose(bank(7)[0:NE, t * P:(t + 1) * P], wmix[:, t, :], ident[:, :])
                last.then_inc(wT_ps, 1)
                m1(1)
                pe.wait_ge(wT_ready, g + 1)
                for t in range(nt):
                    last = nc.tensor.matmul(bank(4, 2)[:, t * D:(t + 1) * D], wT[:, t * P:(t + 1) * P], mb2_sb[:, :], start=True, stop=True)
                last.then_inc(b_ps, 1)
                m2(0)
                m1(2)
                m2(1)
                if ahead:
                    T(0, g + 1, ahead, attn_ready, attn)
                m1(3)
                m2(2)
                if ahead:
                    project(g + 1, ahead)
                m1(4)
                m2(3)
                if ahead:
                    T(1, g + 1, ahead, x1_ready, xn)
                m1(5)
                m2(4)
                if with_slab:
                    beside(g, first_nodes)
                if ahead:
                    feed(g + 1, ahead)
                    feed_end[0] = count.n
                m1(6)
                m2(5)
                if ahead:
                    feed2(g + 1, ahead)
                m1(7)
                m2(6)
                if ahead:
                    T(2, g + 1, ahead, x3_ready, xn)
                m2(7)
                if with_slab:
                    beside(g, carries)
                if ahead:
                    route(g + 1, ahead)

            pe.wait_ge(late_ready, 1)
            nc.tensor.matmul(bank(7)[0:1, 0:1], late_max[:, :], ones[:, 0:1], start=True, stop=True).then_inc(late_ps, 1)
            with pe.Fori(0, FIRST) as n:
                first_nodes(n)
                carries(n)
            pe.wait_ge(late_known, 1)
            late_slabs = pe.value_load(late_i[0:1, 0:1], min_val=0, max_val=P)
            with pe.If(late_slabs > 0):
                with pe.Fori(FIRST, SLABS) as n:
                    first_nodes(n)
                    carries(n)
            T(0, 0, GT, attn_ready, attn)
            project(0, GT)
            T(1, 0, GT, x1_ready, xn)
            beside(-1, first_nodes)
            feed(0, GT)
            feed_end[0] = count.n
            feed2(0, GT)
            T(2, 0, GT, x3_ready, xn)
            route(0, GT)
            beside(-1, carries)
            pe.wait_ge(w_ld, 16 * 2 * NE)
            with pe.Fori(0, SLABS - AHEAD) as g:
                count.enter(g, NE * HC + GC)
                group(g, GT, GT, True)
            count.leave(SLABS - AHEAD)
            for g in range(SLABS - AHEAD, TURNS1):
                group(g, GT, GT)
            group(TURNS1, GT, 1)
            group(GROUPS, 1, 0)

        @block.vector
        def _(dve):
            steps = Chain(dve, dve_steps)
            link, step = steps.link, steps.step
            norms = Chain(dve, var_ready)

            dve.wait_ge(pool_steps, 9)
            dve.sem_inc(scores_done, 2)
            dve.sem_inc(v_used, 2)
            dve.sem_inc(y_done, 1)

            def norm(src_t, nt):
                for t in range(nt):
                    step(nc.vector.bn_stats(st[:, t, :], src_t[:, t, :]))
                steps.wait(hold=True)
                for t in range(nt):
                    step(nc.vector.bn_aggr(mv[:, t, :], st[:, t, :]))
                steps.wait()
                norms.step(nc.vector.tensor_scalar(ve[:, 0:nt], mv[:, 0:nt, 1], EPS, None, ALU.add))
                dve.wait_ge(rstd_ready, norms.base + norms.n)

            def scale_rows(dst_t, src_t, nt, signal=None):
                for t in range(nt):
                    ins = nc.vector.tensor_scalar(dst_t[:, t, :], src_t[:, t, :], mv[:, t, 0:1], rs[:, t:t + 1], ALU.subtract, ALU.mult)
                    if signal and t == nt - 1:
                        ins.then_inc(signal, 1)
                    else:
                        step(ins)
                steps.wait()

            def affine(t_, nt, ln, signal=None):
                link(nc.vector.tensor_tensor(t_[:, 0:nt, :], t_[:, 0:nt, :], ln[:, 0:1, :].to_broadcast([P, nt, D]), ALU.mult))
                ins = nc.vector.tensor_tensor(t_[:, 0:nt, :], t_[:, 0:nt, :], ln[:, 1:2, :].to_broadcast([P, nt, D]), ALU.add)
                if signal:
                    ins.then_inc(signal, 1)
                else:
                    link(ins)

            def rows_normed(g, nt):
                dve.wait_ge(x_ld, 16 * (g + 1))
                norm(xb, nt)
                if not (isinstance(g, int) and g == 0):
                    dve.wait_ge(h0_stored, 16 * g)
                scale_rows(h0, xb, nt, h0_ready)

            def first_norm(g, nt):
                dve.wait_ge(h0_ready, g + 1)
                norm(h0, nt)
                if not (isinstance(g, int) and g == 0):
                    dve.wait_ge(xT_ps, g)
                scale_rows(xn, h0, nt, xn_ready)

            def add_bias(g, tiles):
                for t in tiles:
                    n = g * GT + t
                    dve.wait_ge(qkv_ps, n + 1)
                    if not (isinstance(g, int) and g == 0 and t < 2):
                        dve.wait_ge(qkv_stored[t % 2], 3 * 16 * (g * (GT // 2) + t // 2))
                    o_ = (2 + 2 * (t % 2)) * 512
                    nc.vector.tensor_tensor(qkv[:, t % 2, :], ps[:, o_:o_ + 3 * D], bqkv[:, :], ALU.add).then_inc(qkv_ready, 1)

            rows_normed(0, GT)
            dve.wait_ge(proj_ld, 16 * N_PROJ)
            step(nc.vector.tensor_scalar(shift_cols[:, 0, :], ones[:, :], ln1[:, 1, 0:1], None, ALU.mult))
            steps.wait()
            nc.vector.tensor_scalar(shift_cols[:, 1, :], ones[:, :], ln1[:, 1, 1:2], None, ALU.mult).then_inc(shift_ready, 1)
            link(nc.vector.tensor_tensor(bqkv[:, D:2 * D].rearrange("p (h d) -> p h d", h=H), bqkv[:, D:2 * D].rearrange("p (h d) -> p h d", h=H),
                                         beb[:, :].unsqueeze(1).to_broadcast([P, H, DH]), ALU.add))
            dve.wait_ge(shift_ps, 1)
            step(nc.vector.tensor_tensor(bqkv[:, :], ps[:, 2 * 512:2 * 512 + 3 * D], bqkv[:, :], ALU.add))
            for k in range(2):
                step(nc.vector.tensor_scalar(wqkv[:, k, :], wqkv[:, k, :], ln1[:, 0, k:k + 1], None, ALU.mult))
            steps.wait()
            first_norm(0, GT)
            rows_normed(1, GT)
            add_bias(0, (0, 1))
            first_norm(1, GT)
            add_bias(0, (2, 3))

            dve.wait_ge(edge_ld, 16 * N_EDGE)
            step(nc.vector.tensor_copy(span[:, :], span_i[:, :]))
            steps.wait()
            nc.vector.tensor_scalar(first_diag, ident[0:CHUNKS, 0:CHUNKS], span[:, 0:1], None, ALU.mult).then_inc(first_ready, 1)
            dve.wait_ge(first_ps, 1)
            node_i = [node_split[:, j * CHUNKS:(j + 1) * CHUNKS].bitcast(i32) for j in range(3)]
            step(nc.vector.tensor_scalar(win_node[:, :, 0], bank(6)[:, 0:CHUNKS], iota_col[:, 0:1], None, ALU.add))
            link(nc.vector.tensor_scalar(node_i[0], bank(6)[:, 0:CHUNKS], iota_col[:, 0:1], None, ALU.add))
            step(nc.vector.tensor_scalar(node_i[1], node_i[0], 7, None, ALU.arith_shift_right))
            link(nc.vector.tensor_scalar(node_i[2], node_i[0], P - 1, None, ALU.bitwise_and))
            step(nc.vector.tensor_copy(win_node[:, :, 1], node_i[1]))
            link(nc.vector.tensor_copy(win_node[:, :, 2], node_i[2]))
            link(nc.vector.tensor_tensor(span[:, 0:1], span[:, 1:2], span[:, 0:1], ALU.subtract))
            nc.vector.tensor_scalar(span[:, 0:1], span[:, 0:1], float(P), None, ALU.is_ge).then_inc(wide_ready, 1)
            dve.wait_ge(wide_ps, 1)
            nc.vector.tensor_copy(slow_i[:, :], bank(7)[0:1, 0:1]).then_inc(path_known, 1)
            dve.wait_ge(path_known, 1)

            with dve.Fori(1, GROUPS - 1) as g:
                steps.enter(g - 1, 22)
                norms.enter(g - 1, 2)
                rows_normed(g + 1, GT)
                add_bias(g, (0, 1))
                first_norm(g + 1, GT)
                add_bias(g, (2, 3))
            steps.leave(GROUPS - 2)
            norms.leave(GROUPS - 2)
            rows_normed(GROUPS, 1)
            first_norm(GROUPS, 1)
            add_bias(GROUPS - 1, range(GT))
            add_bias(GROUPS, (0,))

            dve.wait_ge(const_ld, 16 * N_CONST)
            dve.wait_ge(edge_ld, 16 * N_EDGE)
            step(nc.vector.tensor_copy(dstf[:, :], dst_i[:, :]))
            step(nc.vector.tensor_scalar(Fm[:, 0:RUN].bitcast(i32), dst_i[:, :], 7, None, ALU.arith_shift_right))
            step(nc.vector.tensor_scalar(Fm[:, RUN:2 * RUN].bitcast(i32), dst_i[:, :], P - 1, None, ALU.bitwise_and))
            step(nc.vector.tensor_scalar(ews[:, :], ews[:, :], DH ** -0.5, None, ALU.mult))
            steps.wait()
            step(nc.vector.tensor_copy(dhi[:, :], Fm[:, 0:RUN].bitcast(i32)))
            step(nc.vector.tensor_copy(dlo[:, :], Fm[:, RUN:2 * RUN].bitcast(i32)))
            step(nc.vector.memset(cut[:, 0:1], 1.0))
            step(nc.vector.memset(cut[:, RUN:RUN + 1], 1.0))
            step(nc.vector.tensor_tensor(cut[:, 1:RUN], dstf[:, 1:RUN], dstf[:, 0:RUN - 1], ALU.not_equal))
            ds3 = dst_slab.rearrange("p (s j) -> p s j", j=SR)
            step(nc.vector.memset(keep[:, :, 0:1], 0.0))
            step(nc.vector.tensor_tensor(keep[:, :, 1:SR], ds3[:, :, 1:SR], ds3[:, :, 0:SR - 1], ALU.is_equal))
            step(nc.vector.tensor_copy(bounds[:, :, 0], ds3[:, :, 0]))
            step(nc.vector.tensor_copy(bounds[:, :, 1], ds3[:, :, SR - 1]))
            step(nc.vector.tensor_scalar(last_part[:, :], iota_col[:, :], float(P - 1), None, ALU.is_equal))
            step(nc.vector.memset(bounds[:, 0:1, 2], -1.0))
            step(nc.vector.memset(totals[:, :], 0.0))
            step(nc.vector.memset(hits_hi[:, 0, :], 0.0))
            step(nc.vector.memset(hits_lo[:, 0, :], 0.0))
            steps.wait()
            link(nc.vector.tensor_scalar(bounds[:, 1:SLABS, 2], bounds[:, 0:SLABS - 1, 1], 1.0, last_part[:, 0:1], ALU.add, ALU.mult))
            link(nc.vector.tensor_scalar(bounds[:, 1:SLABS, 2], bounds[:, 1:SLABS, 2], -1.0, None, ALU.add))
            step(nc.vector.tensor_scalar(cut[:, :], cut[:, :], -BIG, None, ALU.mult))
            nc.vector.tensor_scalar(dst_i[:, :], dst_i[:, :], float(N - 1), None, ALU.min).then_inc(edges_ready, 1)

            slow = dve.value_load(slow_i[0:1, 0:1], min_val=0, max_val=CHUNKS)

            before_paths = (steps.base, steps.n)
            with dve.If(slow > 0):
                with dve.Fori(0, CHUNKS // 2) as i:
                    steps.enter(i, 6)
                    for par in range(2):
                        c = 2 * i + par
                        dve.wait_ge(hits_used, c + 1)
                        step(nc.vector.tensor_tensor(hits_hi[:, :, :], iota49.unsqueeze(1).to_broadcast([P, CH, TILES]),
                                                     dhi[:, bass.ds(c * CH, CH)].unsqueeze(2).to_broadcast([P, CH, TILES]), ALU.is_equal))
                        nc.vector.tensor_tensor(hits_lo[:, :, :], iota[:, :].unsqueeze(1).to_broadcast([P, CH, P]),
                                                dlo[:, bass.ds(c * CH, CH)].unsqueeze(2).to_broadcast([P, CH, P]), ALU.is_equal).then_inc(hits_ready, 1)
                        k4 = k_ring[par].rearrange("p (t h d) -> p t h d", t=CH, h=H)
                        dve.wait_ge(rows_in[par], 16 * 2 * CH * (i + 1))
                        dve.wait_ge(ep_ready, c + 1)
                        link(nc.vector.tensor_tensor(k4, k4, bank(2 + par)[:, 0:CH * DH].rearrange("p (t d) -> p t d", t=CH).unsqueeze(2)
                                                     .to_broadcast([P, CH, H, DH]), ALU.add))
                        link(nc.vector.tensor_tensor(k_ring[par], k_ring[par], q_ring[par], ALU.mult))
                        nc.vector.tensor_reduce(S[:, bass.ds(c * (CH * H), CH * H)], k_ring[par].rearrange("p (a d) -> p a d", d=DH),
                                                AX.X, ALU.add).then_inc(scores_done, 1)
                steps.leave(CHUNKS // 2)

                after_slow = steps.base + steps.n
                if fast_more > 0:
                    dve.sem_inc(dve_steps, fast_more)
            steps.base, steps.n = before_paths
            with dve.Else():
                def hot(c, turn, par):
                    link(nc.vector.tensor_copy(win_c[:, par, :], win_all[:, bass.ds(c * 3, 3)]))
                    dve.wait_ge(dstrow_ld[par], 16 * (turn + 1))
                    nc.vector.tensor_scalar(win_hot[par], dst_row[par], win_c[:, par, 0:1], None, ALU.is_equal).then_inc(hot_ready, 1)

                def spread(c, par):
                    dve.wait_ge(hits_used, c + 1)
                    dve.wait_ge(counted, c + 2)
                    step(nc.vector.tensor_scalar(tile_hot[par], iota49, win_c[:, par, 1:2], node_count[:, par:par + 1], ALU.is_equal, ALU.mult))
                    steps.wait()
                    nc.vector.tensor_scalar(place_hot[par], iota[:, :], win_c[:, par, 2:3], None, ALU.is_equal).then_inc(hits_ready, 1)

                def multiply(c, turn, slot, slot_turn):
                    par = slot % 2
                    ring = k4_ring[slot]
                    k4 = ring.rearrange("p (t h d) -> p t h d", t=CH, h=H)
                    hw = CH * D // 2
                    dve.wait_ge(rows_in[slot], 16 * CH * (slot_turn + 1))
                    dve.wait_ge(ep_ready, c + 1)
                    link(nc.vector.tensor_tensor(k4, k4, bank(5 + par)[:, 0:CH * DH].rearrange("p (t d) -> p t d", t=CH).unsqueeze(2)
                                                 .to_broadcast([P, CH, H, DH]), ALU.add))
                    for half_ in range(2):
                        dve.wait_ge(q_ps, 2 * c + half_ + 1)
                        kh = ring[:, half_ * hw:(half_ + 1) * hw]
                        nc.vector.tensor_tensor(kh, kh, bank(2 * half_, 2), ALU.mult).then_inc(q_used, 1)
                    dve.wait_ge(q_used, 2 * c + 4)
                    dve.wait_ge(score_out[par], 16 * (turn + 1))
                    nc.vector.tensor_reduce(sc_out[par], ring.rearrange("p (a d) -> p a d", d=DH), AX.X, ALU.add).then_inc(scores_done, 1)

                dve.sem_inc(q_used, 2)
                for par in range(2):
                    dve.sem_inc(score_out[par], 16)
                hot(0, 0, 0)
                with dve.Fori(0, CHUNKS // 4) as i:
                    steps.enter(i, 12)
                    for slot in range(4):
                        c = 4 * i + slot
                        hot(c + 1, 2 * i + (slot + 1) // 2, (slot + 1) % 2)
                        spread(c, slot % 2)
                        multiply(c, 2 * i + slot // 2, slot, i)
                steps.leave(CHUNKS // 4)
                i_last = CHUNKS // 2 - 1
                hot(CHUNKS - 1, i_last, 1)
                for par in range(2):
                    spread(CHUNKS - 2 + par, par)
                    multiply(CHUNKS - 2 + par, i_last, par, CHUNKS // 4)
                if fast_less > 0:
                    dve.sem_inc(dve_steps, fast_less)
                    steps.n += fast_less
                dve.wait_ge(score_in, 32)
            assert steps.base + steps.n == after_slow + fast_more, (steps.base + steps.n - after_slow)

            dve.wait_ge(hits_used, CHUNKS + 1)
            link(nc.vector.tensor_copy(hist[:, :], bank(4)[0:TILES, 0:P]))
            link(nc.vector.tensor_tensor_scan(tots[:, :], ones[0:TILES, :], hist[:, :], 0.0, ALU.mult, ALU.add))

            S3 = S.rearrange("p (t h) -> p t h", h=H)
            F3 = Fm.rearrange("p (t h) -> p t h", h=H)
            M3 = Mm.rearrange("p (t h) -> p t h", h=H)
            dve.wait_ge(scores_done, CHUNKS + 2)
            link(nc.vector.tensor_tensor(S3, S3, ews[:, :].unsqueeze(2).to_broadcast([P, RUN, H]), ALU.mult))
            for h in range(H):
                step(nc.vector.tensor_tensor_scan(F3[:, :, h], cut[:, 0:RUN], S3[:, :, h], -BIG, ALU.add, ALU.max))
            steps.wait()
            for h in range(H):
                step(nc.vector.tensor_tensor_scan(M3[:, ::-1, h], cut[:, RUN:0:-1], F3[:, ::-1, h], -BIG, ALU.add, ALU.max))
            steps.wait()
            step(nc.vector.tensor_copy(small[:, 0:1], dstf[:, 0:1]))
            step(nc.vector.tensor_copy(small[:, 1:2], dstf[:, RUN - 1:RUN]))
            step(nc.vector.tensor_copy(small[:, 2:2 + H], M3[:, 0, :]))
            step(nc.vector.tensor_copy(small[:, 2 + H:2 + 2 * H], M3[:, RUN - 1, :]))
            steps.wait()
            nr = 2 + 2 * H
            diag = early[:, 0:nr * P]
            nc.vector.tensor_tensor(diag.rearrange("p (r n) -> p r n", r=nr), ident[:, :].unsqueeze(1).to_broadcast([P, nr, P]),
                                    small[:, :].unsqueeze(2).to_broadcast([P, nr, P]), ALU.mult).then_inc(diag_ready, 1)
            dve.wait_ge(small_ps, 1)
            pen = sums[:, 0, 0:2, 0:P]
            for f in range(2):
                link(nc.vector.tensor_scalar(pen, ps[:, 0:2 * P].rearrange("p (s n) -> p s n", s=2), small[:, f:f + 1], BIG, ALU.is_equal, ALU.mult))
                link(nc.vector.tensor_scalar(pen, pen, -BIG, None, ALU.add))
                cand = Fm[:, 0:2 * H * P].rearrange("p (s h n) -> p s h n", s=2, h=H)
                link(nc.vector.tensor_tensor(cand, ps[:, 2 * P:nr * P].rearrange("p (s h n) -> p s h n", s=2, h=H),
                                             pen.unsqueeze(2).to_broadcast([P, 2, H, P]), ALU.add))
                link(nc.vector.tensor_reduce(gmax[:, f, :], cand.rearrange("p s h n -> p h s n"), AX.XY, ALU.max))
            for f in range(2):
                mask = Fm[:, f * RUN:(f + 1) * RUN]
                link(nc.vector.tensor_scalar(mask, dstf[:, :], small[:, f:f + 1], BIG, ALU.is_equal, ALU.mult))
                link(nc.vector.tensor_scalar(mask, mask, -BIG, None, ALU.add))
                for h in range(H):
                    step(nc.vector.scalar_tensor_tensor(M3[:, :, h], mask, gmax[:, f, h:h + 1], M3[:, :, h], ALU.add, ALU.max))
                steps.wait()
            for c0, c1 in ((0, SC // 2), (SC // 2, SC)):
                nc.vector.tensor_tensor(S[:, c0:c1], S[:, c0:c1], Mm[:, c0:c1], ALU.subtract).then_inc(exp_in, 1)

            dve.wait_ge(small_ps, 2)
            step(nc.vector.tensor_copy(small[0:TILES, 0:1], bank(5)[0:TILES, 0:1]))
            steps.wait()
            nc.vector.tensor_scalar(tots[:, :], tots[:, :], small[0:TILES, 0:1], -1.0, ALU.add, ALU.add).then_inc(diag_ready, 1)
            dve.wait_ge(small_ps, 3)
            step(nc.vector.tensor_scalar(end_i[:, 0:TILES], bank(6)[:, 0:TILES], 0.0, None, ALU.max))
            step(nc.vector.tensor_scalar(has[:, 0:TILES], bank(6)[:, P:P + TILES], 0.0, None, ALU.is_gt))
            step(nc.vector.memset(late[:, :], 0.0))
            steps.wait()
            for g in range(SLABS - 2):
                step(nc.vector.tensor_scalar(late[:, g * GT:(g + 1) * GT], bank(6)[:, g * GT:(g + 1) * GT], float((g + 2) * SE), None, ALU.is_ge))
            steps.wait()
            for g in range(2, GROUPS + 1):
                t0, t1 = g * GT, min((g + 1) * GT, TILES)
                step(nc.vector.scalar_tensor_tensor(late[:, t0:t1], bank(6)[:, t0:t1], float((g - 1) * SE), late[:, t0:t1], ALU.is_lt, ALU.add))
            number = [sums[:, 0, 0, j * TILES:(j + 1) * TILES] for j in range(3)]
            step(nc.vector.tensor_scalar(number[2].bitcast(i32), end_i[:, 0:TILES], 6, None, ALU.arith_shift_right))
            assert SR == 1 << 6
            ringf = sums[:, 0, 1, 0:TILES]
            link(nc.vector.tensor_copy(ringf, end_i[:, 0:TILES]))
            turn_ = sums[:, 0, 2, 0:TILES]
            step(nc.vector.tensor_scalar(turn_, ringf, float(AHEAD * SE), None, ALU.is_ge))
            for m in range(2, -(-E // (AHEAD * SE))):
                steps.wait()
                step(nc.vector.scalar_tensor_tensor(turn_, ringf, float(m * AHEAD * SE), turn_, ALU.is_ge, ALU.add))
            steps.wait()
            nc.vector.scalar_tensor_tensor(ring_i[:, 0:TILES], turn_, -float(AHEAD * SE), ringf, ALU.mult, ALU.add).then_inc(end_ready, 1)
            steps.wait()
            nc.vector.tensor_reduce(late_max[:, :], late[:, :], AX.X, ALU.max).then_inc(late_ready, 1)
            link(nc.vector.tensor_copy(number[0], number[2].bitcast(i32)))
            step(nc.vector.tensor_copy(hist_T[:, :], bank(6)[:, P:P + TILES]))
            steps.wait()
            link(nc.vector.tensor_tensor(number[1], bank(6)[:, 0:TILES], hist_T[:, :], ALU.subtract))
            link(nc.vector.scalar_tensor_tensor(number[1], number[0], -float(SR), number[1], ALU.mult, ALU.add))
            link(nc.vector.tensor_scalar(number[1], number[1], -1.0, None, ALU.is_lt))
            link(nc.vector.scalar_tensor_tensor(number[0], number[0], -float(SLABS * P), number[1], ALU.add, ALU.mult))
            nc.vector.tensor_scalar(carry_i[:, 0:TILES], number[0], float(SLABS * P), None, ALU.add).then_inc(end_ready, 1)
            link(nc.vector.memset(sums[:, 1, VC - 1, :], 0.0))
            for par in range(2):
                dve.sem_inc(run_stored[par], 16)
            dve.wait_ge(late_ps, 1)
            nc.vector.tensor_copy(late_i[:, :], bank(7)[0:1, 0:1]).then_inc(late_known, 1)
            dve.wait_ge(late_known, 1)

            def run_step(n, k):
                c, par = n * VS + k, k % 2
                new = sums[:, par, :, :]
                step(nc.vector.tensor_copy(keep_c[:, :], keep_all[:, bass.ds(n * SR + k * VC, VC)]))
                dve.wait_ge(run_stored[par], 16 * (n * (VS // 2) + k // 2 + 1))
                if k == 0 and isinstance(n, int) and n <= 1:
                    dve.wait_ge((ex_ld, ex_second_ld)[n], 16)
                elif k == 0:
                    dve.wait_ge(ex_ld, 16 * n)
                exps = ex_second if isinstance(n, int) and n == 1 else ex_slab
                ex = exps[:, k * (VC * H):(k + 1) * (VC * H)].rearrange("p (t h) -> p t h", h=H)
                step(nc.vector.tensor_copy(new[:, :, D:ACC], ex))
                if isinstance(n, int) and n == 0 and k < EARLY_STEPS:
                    dve.wait_ge(v_early_in, 16 * VC * EARLY_STEPS)
                    rows = v_early[k]
                else:
                    dve.wait_ge(v_in[par], 16 * VC * (n * (VS // 2) + k // 2 + 1 - EARLY_STEPS // 2))
                    rows = v_ring[:, par, :]
                nc.vector.tensor_tensor(new[:, :, 0:D].rearrange("p t (h d) -> p t h d", h=H),
                                        rows.rearrange("p (t h d) -> p t h d", t=VC, h=H),
                                        ex.unsqueeze(3).to_broadcast([P, VC, H, DH]), ALU.mult).then_inc(v_used, 1)
                dve.wait_ge(v_used, c + 3)
                steps.wait()
                for j in range(VC):
                    before = new[:, j - 1, :] if j else sums[:, 1 - par, VC - 1, :]
                    ins = nc.vector.scalar_tensor_tensor(new[:, j, :], before, keep_c[:, j:j + 1], new[:, j, :], ALU.mult, ALU.add)
                    if j < VC - 1:
                        link(ins)
                    else:
                        ins.then_inc(run_ready, 1)
                        dve.wait_ge(run_ready, c + 1)

            def carry_rows_ask(n):
                step(nc.vector.tensor_copy(bound_c[:, :], bounds_all[:, bass.ds(n * 3, 3)]))
                steps.wait()
                step(nc.vector.tensor_tensor(same[:, :], bound_c[:, 0:1], bound_c[:, 1:2], ALU.is_equal))
                nc.vector.tensor_scalar(row_diag, ident[:, :], bound_c[:, 0:1], None, ALU.mult).then_inc(row_ready, 1)

            def carry_masks(n):
                dve.wait_ge(row_ps, n + 1)
                link(nc.vector.tensor_scalar(mask_over, bank(7)[:, 0:P], bound_c[:, 2:3], None, ALU.is_equal))
                nc.vector.scalar_tensor_tensor(mask_in, bank(7)[:, 0:P], bound_c[:, 1:2], tri[:, :], ALU.is_equal, ALU.mult).then_inc(masks_ready, 1)

            def carry_take(n):
                dve.wait_ge(carry_ps, n + 1)
                if not (isinstance(n, int) and n == 0):
                    dve.wait_ge(carry_stored, 16 * n)
                nc.vector.tensor_copy(carry, bank(7)[:, P:P + ACC]).then_inc(carry_ready, 1)
                dve.wait_ge(carry_ready, n + 1)
                link(nc.vector.scalar_tensor_tensor(totals[:, :], carry, same[:, 0:1], sums[:, 1, VC - 1, :], ALU.mult, ALU.add))

            def slab(n):
                carry_rows_ask(n)
                for k in range(VS):
                    run_step(n, k)
                carry_masks(n)
                carry_take(n)

            for n in range(FIRST):
                slab(n)
            late_slabs = dve.value_load(late_i[0:1, 0:1], min_val=0, max_val=P)
            before_paths = (steps.base, steps.n)
            with dve.If(late_slabs > 0):
                with dve.Fori(FIRST, SLABS) as n:
                    steps.enter(n - FIRST, SLAB_STEPS)
                    slab(n)
                steps.leave(SLABS - FIRST)
            with dve.Else():
                dve.sem_inc(dve_steps, (SLABS - FIRST) * SLAB_STEPS)

            def bc(t_, nt):
                return t_.unsqueeze(1).to_broadcast([P, nt, D])

            def D1(g, nt):
                step(nc.vector.tensor_copy(has_c[:, 0:nt], has[:, bass.ds(g * GT, nt)]))
                steps.wait()
                dve.wait_ge(got_in, (g * GT + nt) * 32)
                link(nc.vector.tensor_tensor(got[:, 0:nt, :], got[:, 0:nt, :], got_carry[:, 0:nt, :], ALU.add))
                link(nc.vector.reciprocal(rec[:, 0:nt, :], got[:, 0:nt, D:ACC]))
                link(nc.vector.tensor_tensor(rec[:, 0:nt, :], rec[:, 0:nt, :], has_c[:, 0:nt].unsqueeze(2).to_broadcast([P, nt, H]), ALU.mult))
                for t in range(nt):
                    ins = nc.vector.tensor_tensor(attn[:, t, :].rearrange("p (h d) -> p h d", h=H), got[:, t, 0:D].rearrange("p (h d) -> p h d", h=H),
                                                  rec[:, t, :].unsqueeze(2).to_broadcast([P, H, DH]), ALU.mult)
                    if t < nt - 1:
                        step(ins)
                    else:
                        ins.then_inc(attn_ready, 1)

            def D2(g, nt):
                dve.wait_ge(o_ps, g + 1)
                dve.wait_ge(h0_ld, 16 * (g + 1))
                dve.wait_ge(xr_ld, 16 * (g + 1))
                op = bank(4, 2)[:, 0:nt * D].rearrange("p (t d) -> p t d", t=nt)
                link(nc.vector.tensor_tensor(attn[:, 0:nt, :], op, bc(bo_b[:, :], nt), ALU.add))
                link(nc.vector.scalar_tensor_tensor(h0[:, 0:nt, :], attn[:, 0:nt, :], ab[:, 0:1], h0[:, 0:nt, :], ALU.mult, ALU.add))
                link(nc.vector.tensor_tensor(attn[:, 0:nt, :], h0[:, 0:nt, :], xb[:, 0:nt, :], ALU.add))
                norm(h0, nt)
                scale_rows(xn, h0, nt)
                affine(xn, nt, ln2, x1_ready)

            def D3(g, nt):
                dve.wait_ge(f_ps, g + 1)
                fp = bank(4, 2)[:, 0:nt * D].rearrange("p (t d) -> p t d", t=nt)
                link(nc.vector.tensor_tensor(x2[:, 0:nt, :], fp, bc(b2_b[:, :], nt), ALU.add))
                link(nc.vector.scalar_tensor_tensor(x2[:, 0:nt, :], x2[:, 0:nt, :], ab[:, 1:2], attn[:, 0:nt, :], ALU.mult, ALU.add))
                norm(x2, nt)
                scale_rows(xn, x2, nt)
                norm(xn, nt)
                scale_rows(xn, xn, nt)
                affine(xn, nt, lnm, x3_ready)

            def D4(g, nt):
                dve.wait_ge(r_ps, g + 1)
                L, A, B, O1, O2, L2 = (lg[:, j, 0:nt, :] for j in range(6))
                m1_, m2_, df, z, t4, t5 = (tv[:, j, 0:nt] for j in range(6))

                def col(v):
                    return v.unsqueeze(2).to_broadcast([P, nt, NE])

                ib = i8[:, :].unsqueeze(1).to_broadcast([P, nt, NE])
                link(nc.vector.tensor_tensor(L, bank(6)[:, 0:nt * NE].rearrange("p (t e) -> p t e", t=nt), br_b[:, :].unsqueeze(1).to_broadcast([P, nt, NE]), ALU.add))

                def first_of_max(logits, m, one):
                    link(nc.vector.tensor_reduce(m, logits, AX.X, ALU.max))
                    link(nc.vector.tensor_tensor(A, logits, col(m), ALU.is_lt))
                    link(nc.vector.scalar_tensor_tensor(A, A, float(NE), ib, ALU.mult, ALU.add))
                    link(nc.vector.tensor_reduce(t4, A, AX.X, ALU.min))
                    link(nc.vector.tensor_tensor(one, ib, col(t4), ALU.is_equal))

                first_of_max(L, m1_, O1)
                link(nc.vector.scalar_tensor_tensor(L2, O1, -BIG, L, ALU.mult, ALU.add))
                first_of_max(L2, m2_, O2)
                norms.step(nc.vector.tensor_tensor(df, m2_, m1_, ALU.subtract))
                dve.wait_ge(rstd_ready, norms.base + norms.n)
                link(nc.vector.tensor_scalar(t4, z, 1.0, None, ALU.add))
                link(nc.vector.reciprocal(t5, t4))
                link(nc.vector.tensor_tensor(t4, z, t5, ALU.mult))
                link(nc.vector.tensor_tensor(A, O1, col(t5), ALU.mult))
                link(nc.vector.tensor_tensor(B, O2, col(t4), ALU.mult))
                nc.vector.tensor_tensor(wmix[:, 0:nt, :], A, B, ALU.add).then_inc(w_ready, 1)
                dve.wait_ge(w_ready, g + 1)

            def beside(g, ks, ask=False, masks=False, take=False):
                before = steps.n
                dve.nop(nofuse=True)
                with dve.If(late_slabs > 0):
                    dve.sem_inc(dve_steps, len(ks) * STEP_STEPS + 2 * ask + masks + take)
                with dve.Else():
                    if ask:
                        carry_rows_ask(g + AHEAD)
                    for k in ks:
                        run_step(g + AHEAD, k)
                    if masks:
                        carry_masks(g + AHEAD)
                    if take:
                        carry_take(g + AHEAD)
                    dve.nop(nofuse=True)
                assert steps.n - before == len(ks) * STEP_STEPS + 2 * ask + masks + take

            def prepare_first(nt):
                beside(-1, (0, 1))
                D1(0, nt)
                beside(-1, (2, 3), ask=True)
                D2(0, nt)
                beside(-1, range(4, 10))
                D3(0, nt)
                beside(-1, range(10, VS), masks=True)
                beside(-1, (), take=True)
                D4(0, nt)

            def group(g, nt, ahead, with_slab=False):
                def add(e):
                    dve.wait_ge(y_ps, g * NE + e + 1)
                    dest = yo if e == NE - 1 else y
                    base = x2 if e == 0 else y
                    if e == NE - 1:
                        dve.wait_ge(out_stored, 16 * g + 16)
                    for t in range(nt):
                        ins = nc.vector.scalar_tensor_tensor(dest[:, t, :], bank(2, 2)[:, t * D:(t + 1) * D], wmix[:, t, e:e + 1],
                                                             base[:, t, :], ALU.mult, ALU.add)
                        if t < nt - 1:
                            step(ins)
                        else:
                            ins.then_inc(y_done, 1)
                    steps.wait()
                    dve.wait_ge(y_done, g * NE + e + 2)

                dve.wait_ge(b_ps, g + 1)
                link(nc.vector.tensor_tensor(x2[:, 0:nt, :], x2[:, 0:nt, :], bank(4, 2)[:, 0:nt * D].rearrange("p (t d) -> p t d", t=nt), ALU.add))
                if with_slab:
                    beside(g, (0, 1))
                add(0)
                if ahead:
                    D1(g + 1, ahead)
                if with_slab:
                    beside(g, (2, 3))
                add(1)
                if with_slab:
                    beside(g, (4, 5))
                add(2)
                if ahead:
                    D2(g + 1, ahead)
                if with_slab:
                    beside(g, (6, 7), ask=True)
                add(3)
                if with_slab:
                    beside(g, (8, 9))
                add(4)
                if with_slab:
                    beside(g, (10, 11))
                add(5)
                if with_slab:
                    beside(g, (12, 13))
                if ahead:
                    D3(g + 1, ahead)
                add(6)
                if with_slab:
                    beside(g, (14, 15), masks=True)
                add(7)
                if with_slab:
                    beside(g, (), take=True)
                if ahead:
                    D4(g + 1, ahead)

            prepare_first(GT)
            with dve.Fori(0, SLABS - AHEAD) as g:
                steps.enter(g, 176)
                norms.enter(g, 4)
                group(g, GT, GT, True)
            steps.leave(SLABS - AHEAD)
            norms.leave(SLABS - AHEAD)
            for g in range(SLABS - AHEAD, TURNS1):
                group(g, GT, GT)
            group(TURNS1, GT, 1)
            group(GROUPS, 1, 0)


_INS = ["x", "src", "dst", "edge_attr_64", "edge_weight", "L0_gnn_Wq", "L0_gnn_bq", "L0_gnn_Wk", "L0_gnn_bk", "L0_gnn_Wv",
        "L0_gnn_bv", "L0_gnn_We", "L0_gnn_be", "L0_gnn_Wo", "L0_gnn_bo", "L0_gnn_ln1_g", "L0_gnn_ln1_b", "L0_gnn_ln2_g",
        "L0_gnn_ln2_b", "L0_gnn_W1", "L0_gnn_b1", "L0_gnn_W2", "L0_gnn_b2", "L0_gnn_alpha", "L0_gnn_beta", "L0_ffn_gamma",
        "L0_ffn_beta", "L0_ffn_Wr", "L0_ffn_br", "L0_ffn_W1", "L0_ffn_b1", "L0_ffn_W2", "L0_ffn_b2"]


def kernel(**inputs):
    import numpy as _np
    import concourse.bacc as _bacc
    from concourse import mybir as _mybir
    from concourse.bass_utils import run_bass_kernel_spmd as _run

    nc = _bacc.Bacc("TRN2", target_bir_lowering=False, num_devices=1)
    arrays, args = {}, []
    for name in _INS:
        a = _np.ascontiguousarray(inputs[name])
        arrays[f"in_{name}"] = a
        args.append(nc.dram_tensor(f"in_{name}", a.shape, _mybir.dt.from_np(a.dtype), kind="ExternalInput").ap())
    args.append(nc.dram_tensor("out_0", (N, D), _mybir.dt.float32, kind="ExternalOutput").ap())
    gnn_moe_program(nc, *args)
    return _run(nc, [arrays], core_ids=[0]).results[0]["out_0"]
```
